# Optimizing a Trainium2 kernel written in Bass

```python
import numpy as np
import jax
import jax.numpy as jnp

def _softmax(x, axis=-1):
    return jax.nn.softmax(x, axis=axis)

def _gelu(x):
    return jax.nn.gelu(x, approximate=True)

def _silu(x):
    return jax.nn.silu(x)

def _sigmoid(x):
    return jax.nn.sigmoid(x)

def _layernorm(x, axis=-1, eps=1e-05):
    m = jnp.mean(x, axis=axis, keepdims=True)
    v = jnp.var(x, axis=axis, keepdims=True)
    return (x - m) / jnp.sqrt(v + eps)

def _scatter_add(tgt, idx, src, axis=0):
    return tgt.at[idx].add(src)

def _segment_sum(src, seg, n):
    return jax.ops.segment_sum(src, seg, n)
kernel_name = 'mk_recurrent_d2_jaxref_r8_73516b'

def setup_inputs(seed: int=0):
    np.random.seed(seed)
    _w = jnp.asarray

    def _L0_attn_setup():
        import jax, jax.numpy as jnp
        import numpy as np
        D_MODEL = 128

        def _reference_tuple_inner(x, W_state, b_state, W_gate, b_gate):
            B, T, C = x.shape
            px = jnp.einsum('btc,dc->btd', x, W_state) + b_state
            g = jax.nn.sigmoid(jnp.einsum('btc,dc->btd', x, W_gate) + b_gate)

            def step(state, inp):
                p_t, g_t = inp
                state = jnp.tanh(p_t + state)
                return (state, g_t * state)
            s0 = jnp.zeros((B, C), dtype=x.dtype)
            final_state, outs = jax.lax.scan(step, s0, (px.transpose(1, 0, 2), g.transpose(1, 0, 2)))
            return (outs.transpose(1, 0, 2), final_state)
        key = jax.random.key(seed)
        k1, k2, k3, k4, k5 = jax.random.split(key, 5)
        B, T, C = (8, 512, D_MODEL)
        bound = 1.0 / np.sqrt(C)
        return {'x': jax.random.normal(k1, (B, T, C), dtype=jnp.float32), 'W_state': jax.random.uniform(k2, (C, C), dtype=jnp.float32, minval=-bound, maxval=bound), 'b_state': jax.random.uniform(k3, (C,), dtype=jnp.float32, minval=-bound, maxval=bound), 'W_gate': jax.random.uniform(k4, (C, C), dtype=jnp.float32, minval=-bound, maxval=bound), 'b_gate': jax.random.uniform(k5, (C,), dtype=jnp.float32, minval=-bound, maxval=bound)}
    _L0_attn_in = _L0_attn_setup()

    def _L0_ffn_setup():
        import jax, jax.numpy as jnp
        import numpy as np
        S, B, H = (256, 1, 128)
        N_HEADS = 16
        HEAD_DIM = H // N_HEADS
        E, K, F = (8, 2, 256)
        EPS = 1e-05

        def layernorm(x, w, b):
            mu = jnp.mean(x, axis=-1, keepdims=True)
            var = jnp.mean(jnp.square(x - mu), axis=-1, keepdims=True)
            return (x - mu) * jax.lax.rsqrt(var + EPS) * w + b
        key = jax.random.key(seed)
        ks = jax.random.split(key, 8)
        std = 0.02
        return {'x': jax.random.normal(ks[0], (S, B, H), dtype=jnp.float32), 'ln1_w': jnp.ones((H,), jnp.float32), 'ln1_b': jnp.zeros((H,), jnp.float32), 'in_proj_w': jax.random.normal(ks[1], (3 * H, H), jnp.float32) * std, 'in_proj_b': jnp.zeros((3 * H,), jnp.float32), 'out_proj_w': jax.random.normal(ks[2], (H, H), jnp.float32) * std, 'out_proj_b': jnp.zeros((H,), jnp.float32), 'ln2_w': jnp.ones((H,), jnp.float32), 'ln2_b': jnp.zeros((H,), jnp.float32), 'router_w': jax.random.normal(ks[3], (E, H), jnp.float32) * std, 'w1': jax.random.normal(ks[4], (E, H, F), jnp.float32) * std, 'w2': jax.random.normal(ks[5], (E, F, H), jnp.float32) * std}
    _L0_ffn_in = _L0_ffn_setup()

    def _L1_attn_setup():
        import jax, jax.numpy as jnp
        import numpy as np
        NUM_HEADS = 16
        HEAD_DIM = 64
        D_MODEL = 128
        B, L = (8, 512)

        def _relative_position_encoding(seq_len, dim):
            positions = jnp.arange(seq_len, dtype=jnp.float32)[:, None]
            div_term = jnp.exp(jnp.arange(0, dim, 2, dtype=jnp.float32) * -(np.log(10000.0) / dim))
            ang = positions * div_term
            pe = jnp.zeros((seq_len, dim), dtype=jnp.float32)
            pe = pe.at[:, 0::2].set(jnp.sin(ang))
            pe = pe.at[:, 1::2].set(jnp.cos(ang))
            return pe
        key = jax.random.key(seed)
        k1, k2, k3 = jax.random.split(key, 3)
        x = jax.random.normal(k1, (B, L, D_MODEL), dtype=jnp.float32)
        w_qkv = jax.random.normal(k2, (D_MODEL, 3 * NUM_HEADS * HEAD_DIM), dtype=jnp.float32) * (1.0 / np.sqrt(D_MODEL))
        b_qkv = jnp.zeros((3 * NUM_HEADS * HEAD_DIM,), dtype=jnp.float32)
        w_out = jax.random.normal(k3, (NUM_HEADS * HEAD_DIM, D_MODEL), dtype=jnp.float32) * (1.0 / np.sqrt(NUM_HEADS * HEAD_DIM))
        b_out = jnp.zeros((D_MODEL,), dtype=jnp.float32)
        return {'x': x, 'w_qkv': w_qkv, 'b_qkv': b_qkv, 'w_out': w_out, 'b_out': b_out}
    _L1_attn_in = _L1_attn_setup()

    def _L1_ffn_setup():
        import jax, jax.numpy as jnp
        import numpy as np
        B, S, H = (8, 512, 128)
        NAV = 128
        E = 8
        F = 2 * H
        key = jax.random.key(seed)
        ks = jax.random.split(key, 12)

        def w(k, shape, fan_in):
            return jax.random.normal(k, shape, dtype=jnp.float32) / np.sqrt(fan_in)
        return {'hidden_states': jax.random.normal(ks[0], (B, S, H), dtype=jnp.float32), 'Wp1': w(ks[1], (H, NAV), H), 'bp1': jnp.zeros((NAV,), jnp.float32), 'Wp2': w(ks[2], (NAV, E), NAV), 'bp2': jnp.zeros((E,), jnp.float32), 'W1': w(ks[3], (E, H, F), H), 'b1': jnp.zeros((E, F), jnp.float32), 'W2': w(ks[4], (E, F, H), F), 'b2': jnp.zeros((E, H), jnp.float32), 'Wo': w(ks[5], (H, H), H), 'bo': jnp.zeros((H,), jnp.float32)}
    _L1_ffn_in = _L1_ffn_setup()
    _d = {'L0_attn_x': _L0_attn_in['x'], 'L0_attn_W_state': _L0_attn_in['W_state'], 'L0_attn_b_state': _L0_attn_in['b_state'], 'L0_attn_W_gate': _L0_attn_in['W_gate'], 'L0_attn_b_gate': _L0_attn_in['b_gate'], 'L0_ffn_ln1_w': _L0_ffn_in['ln1_w'], 'L0_ffn_ln1_b': _L0_ffn_in['ln1_b'], 'L0_ffn_in_proj_w': _L0_ffn_in['in_proj_w'], 'L0_ffn_in_proj_b': _L0_ffn_in['in_proj_b'], 'L0_ffn_out_proj_w': _L0_ffn_in['out_proj_w'], 'L0_ffn_out_proj_b': _L0_ffn_in['out_proj_b'], 'L0_ffn_ln2_w': _L0_ffn_in['ln2_w'], 'L0_ffn_ln2_b': _L0_ffn_in['ln2_b'], 'L0_ffn_router_w': _L0_ffn_in['router_w'], 'L0_ffn_w1': _L0_ffn_in['w1'], 'L0_ffn_w2': _L0_ffn_in['w2'], 'L1_attn_w_qkv': _L1_attn_in['w_qkv'], 'L1_attn_b_qkv': _L1_attn_in['b_qkv'], 'L1_attn_w_out': _L1_attn_in['w_out'], 'L1_attn_b_out': _L1_attn_in['b_out'], 'L1_ffn_Wp1': _L1_ffn_in['Wp1'], 'L1_ffn_bp1': _L1_ffn_in['bp1'], 'L1_ffn_Wp2': _L1_ffn_in['Wp2'], 'L1_ffn_bp2': _L1_ffn_in['bp2'], 'L1_ffn_W1': _L1_ffn_in['W1'], 'L1_ffn_b1': _L1_ffn_in['b1'], 'L1_ffn_W2': _L1_ffn_in['W2'], 'L1_ffn_b2': _L1_ffn_in['b2'], 'L1_ffn_Wo': _L1_ffn_in['Wo'], 'L1_ffn_bo': _L1_ffn_in['bo']}
    _x0 = _d['L0_attn_x']
    _d['L0_attn_x'] = jax.random.normal(jax.random.fold_in(jax.random.key(seed), 1), (4, 512, 128), dtype=_x0.dtype)
    del _x0
    return _d

def reference(L0_attn_x, L0_attn_W_state, L0_attn_b_state, L0_attn_W_gate, L0_attn_b_gate, L0_ffn_ln1_w, L0_ffn_ln1_b, L0_ffn_in_proj_w, L0_ffn_in_proj_b, L0_ffn_out_proj_w, L0_ffn_out_proj_b, L0_ffn_ln2_w, L0_ffn_ln2_b, L0_ffn_router_w, L0_ffn_w1, L0_ffn_w2, L1_attn_w_qkv, L1_attn_b_qkv, L1_attn_w_out, L1_attn_b_out, L1_ffn_Wp1, L1_ffn_bp1, L1_ffn_Wp2, L1_ffn_bp2, L1_ffn_W1, L1_ffn_b1, L1_ffn_W2, L1_ffn_b2, L1_ffn_Wo, L1_ffn_bo):

    def _L0_attn_ref(x, W_state, b_state, W_gate, b_gate):
        import jax, jax.numpy as jnp
        import numpy as np
        D_MODEL = 128

        def _reference_tuple_inner(x, W_state, b_state, W_gate, b_gate):
            B, T, C = x.shape
            px = jnp.einsum('btc,dc->btd', x, W_state) + b_state
            g = jax.nn.sigmoid(jnp.einsum('btc,dc->btd', x, W_gate) + b_gate)

            def step(state, inp):
                p_t, g_t = inp
                state = jnp.tanh(p_t + state)
                return (state, g_t * state)
            s0 = jnp.zeros((B, C), dtype=x.dtype)
            final_state, outs = jax.lax.scan(step, s0, (px.transpose(1, 0, 2), g.transpose(1, 0, 2)))
            return (outs.transpose(1, 0, 2), final_state)
        return _reference_tuple_inner(x, W_state, b_state, W_gate, b_gate)[0]

    def _L0_ffn_ref(x, ln1_w, ln1_b, in_proj_w, in_proj_b, out_proj_w, out_proj_b, ln2_w, ln2_b, router_w, w1, w2):
        import jax, jax.numpy as jnp
        import numpy as np
        S, B, H = (256, 1, 128)
        N_HEADS = 16
        HEAD_DIM = H // N_HEADS
        E, K, F = (8, 2, 256)
        EPS = 1e-05

        def layernorm(x, w, b):
            mu = jnp.mean(x, axis=-1, keepdims=True)
            var = jnp.mean(jnp.square(x - mu), axis=-1, keepdims=True)
            return (x - mu) * jax.lax.rsqrt(var + EPS) * w + b
        s, b, h = x.shape
        hn = layernorm(x, ln1_w, ln1_b)
        qkv = hn @ in_proj_w.T + in_proj_b
        q, k, v = jnp.split(qkv, 3, axis=-1)
        q = q.reshape(s, b, N_HEADS, HEAD_DIM)
        k = k.reshape(s, b, N_HEADS, HEAD_DIM)
        v = v.reshape(s, b, N_HEADS, HEAD_DIM)
        scores = jnp.einsum('sbnd,tbnd->bnst', q, k) / np.sqrt(HEAD_DIM)
        causal = jnp.tril(jnp.ones((s, s), bool))
        scores = jnp.where(causal[None, None], scores, -jnp.inf)
        probs = jax.nn.softmax(scores, axis=-1)
        attn = jnp.einsum('bnst,tbnd->sbnd', probs, v).reshape(s, b, h)
        attn = attn @ out_proj_w.T + out_proj_b
        x1 = x + attn
        hn2 = layernorm(x1, ln2_w, ln2_b).reshape(s * b, h)
        logits = hn2 @ router_w.T
        rp = jax.nn.softmax(logits, axis=-1)
        topw, topi = jax.lax.top_k(rp, K)
        gates = jnp.sum(jax.nn.one_hot(topi, E, dtype=hn2.dtype) * topw[..., None], axis=1)
        hmid = jax.nn.gelu(jnp.einsum('th,ehf->tef', hn2, w1), approximate=False)
        y = jnp.einsum('tef,efh->th', hmid * gates[:, :, None], w2)
        return x1 + y.reshape(s, b, h)

    def _L1_attn_ref(x, w_qkv, b_qkv, w_out, b_out):
        import jax, jax.numpy as jnp
        import numpy as np
        NUM_HEADS = 16
        HEAD_DIM = 64
        D_MODEL = 128
        B, L = (8, 512)

        def _relative_position_encoding(seq_len, dim):
            positions = jnp.arange(seq_len, dtype=jnp.float32)[:, None]
            div_term = jnp.exp(jnp.arange(0, dim, 2, dtype=jnp.float32) * -(np.log(10000.0) / dim))
            ang = positions * div_term
            pe = jnp.zeros((seq_len, dim), dtype=jnp.float32)
            pe = pe.at[:, 0::2].set(jnp.sin(ang))
            pe = pe.at[:, 1::2].set(jnp.cos(ang))
            return pe
        Bq, Lq, _ = x.shape
        qkv = x @ w_qkv + b_qkv
        qkv = qkv.reshape(Bq, Lq, NUM_HEADS, 3 * HEAD_DIM)
        q, k, v = jnp.split(qkv, 3, axis=-1)
        pos_enc = _relative_position_encoding(Lq, HEAD_DIM)
        k = k + pos_enc[None, :, None, :]
        scale = jnp.sqrt(jnp.float32(HEAD_DIM))
        attn = jnp.einsum('blhd,bl gd->blhg'.replace(' ', ''), q, k) / scale
        attn = jax.nn.softmax(attn, axis=-1)
        out = jnp.einsum('blhg,blgd->blhd', attn, v)
        out = out.reshape(Bq, Lq, NUM_HEADS * HEAD_DIM)
        return out @ w_out + b_out

    def _L1_ffn_ref(hidden_states, Wp1, bp1, Wp2, bp2, W1, b1, W2, b2, Wo, bo):
        import jax, jax.numpy as jnp
        import numpy as np
        B, S, H = (8, 512, 128)
        NAV = 128
        E = 8
        F = 2 * H
        last = hidden_states[:, -1, :]
        logits = jax.nn.gelu(last @ Wp1 + bp1, approximate=False) @ Wp2 + bp2
        action_probs = jax.nn.softmax(logits, axis=-1)
        sel = jnp.argmax(action_probs, axis=-1)
        w1 = W1[sel]
        w2 = W2[sel]
        h = jax.nn.gelu(jnp.einsum('bsh,bhf->bsf', hidden_states, w1) + b1[sel][:, None, :], approximate=False)
        reasoned = jnp.einsum('bsf,bfh->bsh', h, w2) + b2[sel][:, None, :]
        out = reasoned @ Wo + bo
        return hidden_states + 0.3 * out
    x = L0_attn_x
    xn = _layernorm(x, axis=-1)
    s = _L0_attn_ref(xn, L0_attn_W_state, L0_attn_b_state, L0_attn_W_gate, L0_attn_b_gate)
    g = _silu(_L0_ffn_ref(xn, L0_ffn_ln1_w, L0_ffn_ln1_b, L0_ffn_in_proj_w, L0_ffn_in_proj_b, L0_ffn_out_proj_w, L0_ffn_out_proj_b, L0_ffn_ln2_w, L0_ffn_ln2_b, L0_ffn_router_w, L0_ffn_w1, L0_ffn_w2))
    x = x + s * g
    xn = _layernorm(x, axis=-1)
    s = _L1_attn_ref(xn, L1_attn_w_qkv, L1_attn_b_qkv, L1_attn_w_out, L1_attn_b_out)
    g = _silu(_L1_ffn_ref(xn, L1_ffn_Wp1, L1_ffn_bp1, L1_ffn_Wp2, L1_ffn_bp2, L1_ffn_W1, L1_ffn_b1, L1_ffn_W2, L1_ffn_b2, L1_ffn_Wo, L1_ffn_bo))
    x = x + s * g
    return x

_drawn_inputs = setup_inputs


def setup_inputs(seed=0):
    import zlib

    import numpy as np

    out = dict(_drawn_inputs(seed))
    spreads = {'L0_ffn_ln1_w': (1.0, 0.6),
     'L0_ffn_ln1_b': (0.0, 0.8),
     'L0_ffn_in_proj_b': (0.0, 0.8),
     'L0_ffn_out_proj_b': (0.0, 0.389),
     'L0_ffn_ln2_w': (1.0, 0.6),
     'L0_ffn_ln2_b': (0.0, 0.8),
     'L1_attn_b_qkv': (0.0, 0.371),
     'L1_attn_b_out': (0.0, 0.1),
     'L1_ffn_bp1': (0.0, 0.1),
     'L1_ffn_bp2': (0.0, 0.1),
     'L1_ffn_b1': (0.0, 2.0),
     'L1_ffn_b2': (0.0, 0.8),
     'L1_ffn_bo': (0.0, 2.0)}
    factors = {'L0_attn_b_gate': 8.0,
     'L0_ffn_in_proj_w': 6.91,
     'L0_ffn_out_proj_w': 5.765,
     'L0_ffn_router_w': 8.0,
     'L0_ffn_w1': 8.0,
     'L0_ffn_w2': 8.0}
    for name, (base, spread) in spreads.items():
        noise = np.random.default_rng([zlib.crc32(name.encode()), seed]).standard_normal(out[name].shape)
        drawn = base * np.exp(spread * noise) if base else spread * noise
        out[name] = jnp.asarray(drawn.astype(out[name].dtype))
    for name, factor in factors.items():
        out[name] = (out[name] * factor).astype(out[name].dtype)
    return out
```

```python
from contextlib import ExitStack

import numpy as np

import concourse.bass as bass
from concourse import mybir

ALU = mybir.AluOpType
ACT = mybir.ActivationFunctionType
F32 = mybir.dt.float32
I32 = mybir.dt.int32
X = mybir.AxisListType.X

P = 128
B, T, D = 4, 512, 128
CH = T // P
BD = B * D
H0, HD0 = 16, 8
E = 8
F = 256
FT = F // P
H1, HD1 = 16, 64
PAIRS = H1 // 2
UNIT = 256
UNITS = B * T // UNIT
TB = P // H1
KB = UNIT // TB
MB = KB // 4
PROJ = 12
PR_USES = PROJ + 2
EPS = 1e-5
NEG = -3.0e38
MASKED = -1.0e30

ATT_EXP_STEP = 88
ROUTER_EXP_STEP = 198
GATE_TANH_STEP = 160
MOE_STEP = 200
MOE_PERIOD = 9
MOE_LAG = 12

MISC_BANKS = 4
MISC = ([("xnT", 0, 0), ("px", 0, 0)]
        + [(kind, c, 0) for c in range(1, CH) for kind in ("xnT", "px")]
        + [("hnT", c, 0) for c in range(CH)]
        + [("qkv", c, b) for c in range(CH) for b in range(B)]
        + [(kind, c, 0) for kind in ("attT", "gate", "proj", "h2T", "router") for c in range(CH)])
MISC_AT = {use: n for n, use in enumerate(MISC)}


def build(nc, ins, out):
    with ExitStack() as ctx:
        def sb(name, *shape, dt=F32):
            return ctx.enter_context(nc.sbuf_tensor(name, list(shape), dt))

        def sem(name):
            return ctx.enter_context(nc.semaphore(name))

        bank = [ctx.enter_context(nc.psum_tensor(f"bank{i}", [P, 512], F32)) for i in range(8)]

        ident = sb("ident", P, P)
        w_state = sb("w_state", P, D)
        w_gate = sb("w_gate", P, D)
        w_in = sb("w_in", P, 3 * D)
        w_op = sb("w_op", P, D)
        w_router = sb("w_router", P, E)
        w1 = sb("w1", P, E * F)
        w2 = sb("w2", P, E, FT, D)
        cols0 = sb("cols0", P, 5)
        rows0 = sb("rows0", P, 5 * D)
        w_qkv = sb("w_qkv", P, 3, H1 * HD1)
        bqk = sb("bqk", P, 2, PAIRS)
        bq8 = sb("bq8", P, PAIRS)
        bv_row = sb("bv_row", P, H1 * HD1)
        w_out = sb("w_out", P, PAIRS, D)
        own_token = sb("own_token", P, TB)
        w_p1 = sb("w_p1", P, P)
        w_p2 = sb("w_p2", P, E)
        b_p1 = sb("b_p1", P, 1)
        b_p2 = sb("b_p2", 1, E)
        w_o = sb("w_o", P, D)
        rows1 = sb("rows1", P, 2 * D)
        pos = sb("pos", P, UNITS + 1, P)
        falling = sb("falling", P, E)
        exps = sb("exps", P, B)

        def over(tensor, shape, first=0):
            flat = tensor[:]
            while len(flat.shape) > 2:
                flat = flat.rearrange("p a b c -> p a (b c)" if len(flat.shape) == 4 else "p a b -> p (a b)")
            names = "abcd"[:len(shape)]
            flat = flat[:, first:first + int(np.prod(shape))]
            return flat.rearrange(f"p ({' '.join(names)}) -> p {' '.join(names)}", **dict(zip(names, shape)))

        x_tok = sb("x_tok", P, CH, B, D)
        xn_tok = sb("xn_tok", P, CH, B, D)
        xnT = sb("xnT", P, CH, B, P)
        px = sb("px", P, CH, B, P)
        state = sb("state", P, CH, B, P)
        zero_state = sb("zero_state", P, B)
        stats = sb("stats", P, 4, CH, B, 6)
        mv = sb("mv", P, 4, CH, B, 2)
        var = sb("var", P, 4, CH, B)
        rstd = sb("rstd", P, 4, CH, B)
        z_tok = sb("z_tok", P, CH, B, D)
        hnT = sb("hnT", P, CH, B, P)
        heads_words = sb("heads_words", P, CH * B * 3 * D + CH * 10 * D)
        qkv = heads_words[:, 0:CH * B * 3 * D].rearrange("p (c b n) -> p c b n", c=CH, b=B)
        prod = heads_words[:, CH * B * 3 * D:].rearrange("p (c s n) -> p c s n", c=CH, s=10)
        sc = sb("sc", P, CH, B, B, H0)
        mx0 = sb("mx0", P, CH, B, H0)
        rs0 = sb("rs0", P, CH, B, H0)
        sums_words = sb("sums_words", P, 2 * CH * BD)
        att = sums_words[:, 0:CH * BD].rearrange("p (c b d) -> p c b d", c=CH, b=B)
        attT = over(heads_words, (CH, B, P))
        tz = attT
        tg = over(heads_words, (CH, B, D), CH * BD)
        mix = tg
        hg = over(heads_words, (4, BD), 2 * CH * BD)
        xnb = sums_words[:, CH * BD:].rearrange("p (c b d) -> p c b d", c=CH, b=B)
        x1 = sb("x1", P, CH, B, D)
        h2T = hnT
        lg = sb("lg", P, CH * B, E)
        lg2 = sb("lg2", P, CH * B, E)
        oh1 = sb("oh1", P, CH * B, E)
        oh2 = sb("oh2", P, CH * B, E)
        ex = sb("ex", P, CH * B, E)
        gates = sb("gates", P, CH * B, E)
        r16 = sb("r16", P, 8, CH * B)

        xn2_tok = over(xnT, (CH, B, D))
        xn2T = sb("xn2T", P, UNITS + 1, UNIT)
        a1 = sb("a1", P, B)
        rt = sb("rt", 1, 6, B, E)
        sel = sb("sel", 1, B, dt=I32)
        ew = sb("ew", P, B, 2 * F + 3)
        hg1 = over(sums_words, (B, FT, T))
        rT = over(z_tok, (B, T))
        xnb2 = over(px, (CH, B, D))
        z1 = over(w1, (CH, B, D))
        tz1 = over(state, (CH, B, D))
        s_all = over(hnT, (CH, B, D))
        y_all = over(s_all, (CH, B, D))

        d_x = [sem(f"x_loaded{c}") for c in range(CH)]
        d_early = sem("early_weights_loaded")
        d_moe = sem("moe_weights_loaded")
        d_late = sem("late_weights_loaded")
        d_exp = sem("chosen_experts_loaded")
        d_out = sem("output_stored")
        ident_zero = sem("ident_zeroed")
        consts = sem("constants_ready")
        vec = sem("vector_step")
        pool = sem("pool_step")
        var_ready = sem("variance_ready")
        normed = sem("tokens_normed")
        misc_ready = sem("misc_psum_ready")
        misc_free = sem("misc_psum_free")
        chain_sum = sem("chain_sum")
        chain_state = sem("chain_state")
        qk_prod = sem("qk_products_ready")
        sc_ready = sem("scores_centred")
        pe_ready = sem("attention_exp_ready")
        prob_ready = sem("attention_probs_ready")
        pv_prod = sem("pv_products_ready")
        att_ready = sem("attention_ready")
        xnb_ready = sem("xn_plus_bias_ready")
        lg_ready = sem("logits_centred")
        ex_ready = sem("router_exp_ready")
        tg_ready = sem("gate_tanh_ready")
        hm_ready = sem("expert_hidden_ready")
        hg_ready = sem("expert_gelu_ready")
        y_ready = sem("expert_out_ready")
        y_free = sem("expert_out_read")
        z_ready = sem("block_sum_ready")
        tz_ready = sem("block_tanh_ready")
        sT_ready = sem("state_turned")
        sT_free = sem("state_turned_read")
        xn2T_ready = sem("xn2_turned")
        xn2T_done = sem("xn2T_written")
        bc_done = sem("scaled_biases_ready")
        p1_ready = sem("policy_hidden_ready")
        a1_ready = sem("policy_gelu_ready")
        p2_ready = sem("policy_logits_ready")
        sel_ready = sem("expert_chosen")
        f_ready = sem("ffn1_hidden_ready")
        f_gelu = sem("ffn1_gelu_ready")
        r_ready = sem("ffn1_reasoned_ready")
        r_done = sem("ffn1_reasoned_read")
        o_ready = sem("ffn1_out_ready")
        z1_ready = sem("ffn1_sum_ready")
        tz1_ready = sem("ffn1_tanh_ready")
        mix1_ready = sem("ffn1_gate_ready")
        xnb2_ready = sem("xn2_plus_bias_ready")

        qT = over(heads_words, (UNIT, H1), CH * B * 3 * D)
        kT = over(sums_words, (UNIT, H1))
        xc = sb("xc", P, UNIT)
        posb = sb("posb", P, PAIRS, P)
        vt = over(xn_tok, (2, H1 * HD1))
        vb = over(w2, (KB, HD1))
        sc1 = over(heads_words, (KB, H1), CH * B * 3 * D + UNIT * H1)
        m1 = over(heads_words, (3, KB), CH * B * 3 * D + UNIT * H1 + KB * H1)
        pex = over(w1, (2, 4, P)).rearrange("p r k (t g) -> p r k t g", t=TB)
        ptT = over(w1, (2, 4, P), 8 * P)
        onT = over(z_tok, (UNIT, PAIRS))
        v_dram = nc.dram_tensor("v_by_token", (2, P, H1 * HD1), F32, kind="Internal").ap()
        S, TR, O, PR = bank[0:2], bank[2:4], [bank[4], bank[7]], bank[5:7]
        empty_unit = sem("empty_unit_ready")
        masks_in = sem("masks_loaded")
        xc_ready = sem("unit_staged")
        posb_ready = sem("positions_ready")
        pr_ready = sem("projection_ready")
        pr_free = sem("projection_read")
        v_out = sem("v_stored")
        v_in = sem("v_by_block_loaded")
        vb_free = sem("v_by_block_used")
        score = sem("scores_ready")
        sc_max = sem("block_scores_ready")
        sc_sub = sem("unit_scores_centred")
        sc_exp = sem("unit_exp_ready")
        prob = sem("unit_probs_ready")
        small = sem("softmax_step")
        spread = sem("probs_spread")
        turned = sem("probs_turned")
        tcopy = sem("turned_probs_copied")
        pvd = sem("pv_ready")
        ocopy = sem("pv_copied")
        y_done = sem("chunk_output_ready")

        block = ctx.enter_context(nc.Block())

        def misc_bank(use):
            return bank[1 + MISC_AT[use] % MISC_BANKS]

        @block.sync
        def _(sp):
            xs = ins["x"].rearrange("b (c p) d -> p c b d", p=P)
            for c in range(CH):
                sp.dma_start(x_tok[:, c], xs[:, c]).then_inc(d_x[c], 16)
                if c == 0:
                    early = [(w_state[:], "w_state"), (cols0[:], "cols0"), (w_in[:], "w_in"),
                             (rows0[:], "rows0"), (w_op[:], "w_op"), (w_router[:], "w_router"),
                             (w_gate[:], "w_gate")]
                    for dst, name in early:
                        sp.dma_start(dst, ins[name]).then_inc(d_early, 16)
            sp.dma_start(w1[:], ins["w1"]).then_inc(d_moe, 16)
            sp.dma_start(w2[:], ins["w2"]).then_inc(d_moe, 16)
            late = [(w_out[:], "w_out"), (bqk[:], "bqk"), (rows1[:], "rows1"), (w_p1[:], "w_p1"),
                    (w_p2[:], "w_p2"), (b_p1[:], "b_p1"), (b_p2[:], "b_p2"), (w_o[:], "w_o"),
                    (w_qkv[:], "w_qkv"), (pos[:], "pos"), (bv_row[:], "bv_row"), (own_token[:], "own_token")]
            for dst, name in late:
                sp.dma_start(dst, ins[name]).then_inc(d_late, 16)
            sp.wait_ge(hg_ready, FT * CH * E)
            wide = [HD1, UNIT // TB, TB * H1]
            for dst, name in ((qT, "mask_q"), (kT, "mask_k")):
                sp.dma_start(dst[HD1:P].rearrange("p (k t) h -> p k (t h)", t=TB),
                             ins[name].unsqueeze(1).broadcast_to(wide)).then_inc(masks_in, 16)
            sp.wait_ge(xn2T_done, CH)
            sp.dma_start(xc[:], xn2T[:, 0, :]).then_inc(xc_ready, 16)
            sp.wait_ge(sel_ready, 1)
            for b in range(B):
                e = sp.value_load(sel[0:1, b:b + 1], min_val=0, max_val=E - 1)
                sp.dma_start(ew[:, b, :], ins["experts"][bass.ds(e, 1), :, :].rearrange("e p n -> (e p) n")
                             ).then_inc(d_exp, 16)

            def v_store():
                sp.dma_start(v_dram.rearrange("b p n -> p b n"), vt[:]).then_inc(v_out, 16)

            def v_load():
                sp.dma_start(vb[:], v_dram.rearrange("b (k t) (g d) -> (t g) (b k) d", t=TB, d=HD1)
                             ).then_inc(v_in, 16)

            sp.wait_ge(pr_free, 12)
            v_store()
            sp.wait_ge(v_out, 16)
            v_load()
            sp.wait_ge(empty_unit, 1)
            with sp.Fori(0, UNITS) as u:
                sp.wait_ge(pr_ready, u * PR_USES + 12)
                sp.dma_start(xc[:], xn2T[:, bass.ds(u + 1, 1), :].rearrange("p a t -> p (a t)")
                             ).then_inc(xc_ready, 16)
                sp.wait_ge(pr_free, u * PR_USES + 24)
                sp.wait_ge(v_in, u * 16 + 16)
                v_store()
                sp.wait_ge(v_out, u * 16 + 32)
                sp.wait_ge(pvd, u * MB + MB + 1)
                sp.sem_inc(vb_free, 1)
                v_load()
            sp.wait_ge(v_in, 16 * (UNITS + 1))
            ys = out.rearrange("b (c p) d -> p c b d", p=P)
            for c in range(CH):
                sp.wait_ge(y_done, c + 1)
                sp.dma_start(ys[:, c], y_all[:, c]).then_inc(d_out, 16)
            sp.wait_ge(d_out, 16 * CH)

        N_EARLY, N_MOE, N_LATE = 7 * 16, 2 * 16, 12 * 16

        @block.gpsimd
        def _(gp):
            nc.gpsimd.memset(ident[:], 0.0).then_inc(ident_zero, 1)
            nc.gpsimd.memset(exps[:], -0.5).then_inc(consts, 1)
            gp.wait_ge(ident_zero, 1)
            nc.gpsimd.affine_select(out=ident[:], in_=ident[:], compare_op=ALU.not_equal, fill=1.0, base=0,
                                    pattern=[[-1, P]], channel_multiplier=1).then_inc(consts, 1)
            nc.gpsimd.memset(zero_state[:], 0.0).then_inc(consts, 1)
            for e in range(E):
                nc.gpsimd.memset(falling[:, e:e + 1], float(E - e)).then_inc(consts, 1)
            gp.wait_ge(consts, 3)

            steps = [0]

            def norm(ln, c, src, dst):
                gp.wait_ge(var_ready, ln * CH + c + 1)
                nc.gpsimd.tensor_tensor(rstd[:, ln, c, :], var[:, ln, c, :], exps[:], ALU.pow).then_inc(pool, 1)
                steps[0] += 1
                gp.wait_ge(pool, steps[0])
                for b in range(B):
                    nc.gpsimd.tensor_scalar(dst[:, c, b, :], src[:, c, b, :], mv[:, ln, c, b, 0:1],
                                            rstd[:, ln, c, b:b + 1], ALU.subtract, ALU.mult).then_inc(normed, 1)

            for c in range(CH):
                norm(0, c, x_tok, xn_tok)
                if c == 0:
                    nc.gpsimd.memset(sc[:], MASKED).then_inc(consts, 1)
            for c in range(CH):
                if c == 0:
                    gp.wait_ge(normed, B * CH)
                norm(1, c, xn_tok, z_tok)
            for c in range(CH):
                gp.wait_ge(misc_free, MISC_AT[("qkv", c, B - 1)] + 1)
                n = 0
                for s in range(B):
                    q = qkv[:, c, s:s + 1, 0:D].broadcast_to([P, s + 1, D])
                    ins_ = nc.gpsimd.tensor_tensor(prod[:, c, n:n + s + 1, :], q, qkv[:, c, 0:s + 1, D:2 * D], ALU.mult)
                    n += s + 1
                ins_.then_inc(qk_prod, 1)
            for c in range(CH):
                gp.wait_ge(normed, 2 * B * CH)
                nc.gpsimd.tensor_tensor(
                    xnb[:, c], xn_tok[:, c], rows0[:, 3 * D:4 * D].unsqueeze(1).broadcast_to([P, B, D]),
                    ALU.add).then_inc(xnb_ready, 1)
            for c in range(CH):
                gp.wait_ge(prob_ready, c + 1)
                n = 0
                for s in range(B):
                    for u in range(s + 1):
                        prb = sc[:, c, s, u, :].unsqueeze(2).broadcast_to([P, H0, HD0])
                        dst = att[:, c, 0, :] if s == 0 else prod[:, c, n, :]
                        ins_ = nc.gpsimd.tensor_tensor(
                            dst.rearrange("p (h d) -> p h d", h=H0), prb,
                            qkv[:, c, u, 2 * D:3 * D].rearrange("p (h d) -> p h d", h=H0), ALU.mult)
                        n += 1
                ins_.then_inc(pv_prod, 1)
            for c in range(CH):
                norm(2, c, x1, z_tok)
            nc.gpsimd.memset(xn2T[:, UNITS, :], 0.0).then_inc(empty_unit, 1)
            for c in range(CH):
                norm(3, c, x_tok, xn2_tok)
                gp.wait_ge(normed, (3 * CH + c + 1) * B)
                if c == 0:
                    gp.wait_ge(bc_done, 1)
                nc.gpsimd.tensor_tensor(
                    xnb2[:, c], xn2_tok[:, c], rows1[:, D:2 * D].unsqueeze(1).broadcast_to([P, B, D]),
                    ALU.add).then_inc(xnb2_ready, 1)

            def positions_of(chunk):
                nc.gpsimd.tensor_tensor(posb[:], chunk.broadcast_to([P, PAIRS, P]),
                                        bqk[:, 1, :].unsqueeze(2).broadcast_to([P, PAIRS, P]),
                                        ALU.add).then_inc(posb_ready, 1)

            gp.wait_ge(d_late, N_LATE)
            positions_of(pos[:, 0:1, :])
            gp.sem_inc(spread, 1)
            with gp.Fori(0, UNITS) as u:
                gp.wait_ge(pr_free, u * PR_USES + 8)
                positions_of(pos[:, bass.ds(u + 1, 1), :])
                gp.wait_ge(prob, u + 1)
                for m in range(MB):
                    gp.wait_ge(turned, u * MB + max(m, 1))
                    nc.gpsimd.tensor_tensor(
                        pex[:, m % 2], sc1[:, 4 * m:4 * m + 4, :].unsqueeze(2).broadcast_to([P, 4, TB, H1]),
                        own_token[:].unsqueeze(1).unsqueeze(3).broadcast_to([P, 4, TB, H1]), ALU.mult).then_inc(spread, 1)

        @block.tensor
        def _(pe):
            def fill(use):
                n = MISC_AT[use]
                if n >= MISC_BANKS:
                    pe.wait_ge(misc_free, n - MISC_BANKS + 1)
                return misc_bank(use)

            def turn(dst, src):
                for b in range(B):
                    mm = pe.transpose(dst[:, b * P:(b + 1) * P], src[:, b, :], ident[:])
                return mm

            def turn_xn(c):
                pe.wait_ge(normed, B * (c + 1))
                turn(fill(("xnT", c, 0)), xn_tok[:, c]).then_inc(misc_ready, 1)

            def proj_px(c):
                dst = fill(("px", c, 0))
                pe.wait_ge(misc_free, MISC_AT[("xnT", c, 0)] + 1)
                pe.matmul(dst[:], w_state[:], xnT[:, c].rearrange("p b t -> p (b t)"),
                          start=True, stop=True).then_inc(misc_ready, 1)

            pe.wait_ge(consts, 11)
            pe.wait_ge(d_early, N_EARLY)
            for c in range(CH):
                turn_xn(c)
                proj_px(c)
            for c in range(CH):
                pe.wait_ge(normed, B * (CH + c + 1))
                turn(fill(("hnT", c, 0)), z_tok[:, c]).then_inc(misc_ready, 1)
            for c in range(CH):
                pe.wait_ge(misc_free, MISC_AT[("hnT", c, 0)] + 1)
                for b in range(B):
                    pe.matmul(fill(("qkv", c, b))[:, 0:3 * D], hnT[:, c, b, :], w_in[:],
                              start=True, stop=True).then_inc(misc_ready, 1)
            for c in range(CH):
                pe.wait_ge(att_ready, c + 1)
                turn(fill(("attT", c, 0)), att[:, c]).then_inc(misc_ready, 1)

            def per_token(use, lhs, rhs, n):
                dst = fill(use)
                for b in range(B):
                    mm = pe.matmul(dst[:, b * n:(b + 1) * n], lhs[:, b, :], rhs, start=(b == 0), stop=(b == B - 1),
                                   skip_group_check=True)
                mm.then_inc(misc_ready, 1)

            for c in range(CH):
                per_token(("gate", c, 0), xnT[:, c], w_gate[:], D)
            for c in range(CH):
                pe.wait_ge(misc_free, MISC_AT[("attT", c, 0)] + 1)
                per_token(("proj", c, 0), attT[:, c], w_op[:], D)
            for c in range(CH):
                pe.wait_ge(normed, B * (2 * CH + c + 1))
                turn(fill(("h2T", c, 0)), z_tok[:, c]).then_inc(misc_ready, 1)
            for c in range(CH):
                pe.wait_ge(misc_free, MISC_AT[("h2T", c, 0)] + 1)
                per_token(("router", c, 0), h2T[:, c], w_router[:], E)

            def hidden(i):
                c, e = divmod(i, E)
                for f in range(FT):
                    n = FT * i + f
                    if n < 4:
                        pe.wait_ge(misc_free, len(MISC))
                    else:
                        pe.wait_ge(hg_ready, n - 3)
                    pe.matmul(bank[1 + n % 4][:], w1[:, (e * F + f * P):(e * F + (f + 1) * P)],
                              h2T[:, c].rearrange("p b t -> p (b t)"), start=True, stop=True).then_inc(hm_ready, 1)

            def mix_out(i):
                e = i % E
                pe.wait_ge(hg_ready, FT * (i + 1))
                if i >= 2:
                    pe.wait_ge(y_free, i - 1)
                for f in range(FT):
                    for b in range(B):
                        mm = pe.matmul(bank[5 + i % 2][:, b * D:(b + 1) * D],
                                       hg[:, (FT * i + f) % 4, b * P:(b + 1) * P], w2[:, e, f, :],
                                       start=(f == 0 and b == 0), stop=(f == FT - 1), skip_group_check=True)
                mm.then_inc(y_ready, 1)

            def turn_state(c):
                pe.wait_ge(chain_state, (c + 1) * P)
                if c:
                    pe.wait_ge(xn2T_done, c)
                turn(bank[7], state[:, c]).then_inc(sT_ready, 1)

            def turn_xn2(c):
                pe.wait_ge(normed, B * (3 * CH + c + 1))
                pe.wait_ge(sT_free, c + 1)
                turn(bank[7], xn2_tok[:, c]).then_inc(xn2T_ready, 1)

            pe.wait_ge(d_moe, N_MOE)
            hidden(0)
            for i in range(CH * E):
                if i + 1 < CH * E:
                    hidden(i + 1)
                mix_out(i)
                if i >= E and i % E == 1:
                    turn_state(i // E - 1)
                if i >= E and i % E == 5:
                    turn_xn2(i // E - 1)
            turn_state(CH - 1)
            turn_xn2(CH - 1)

            pe.wait_ge(xn2T_done, CH)
            pe.wait_ge(y_free, CH * E)
            pe.wait_ge(d_late, N_LATE)
            xn2T_cb = xn2T[:, 0:UNITS, :].rearrange("p u t -> p (u t)").rearrange("p (c b t) -> p c b t", c=CH, b=B)
            pe.matmul(bank[5][:, 0:B], w_p1[:], xn2T_cb[:, CH - 1, :, P - 1], start=True, stop=True).then_inc(p1_ready, 1)
            pe.wait_ge(a1_ready, 1)
            for b in range(B):
                mm = pe.matmul(bank[6][0:1, b * E:(b + 1) * E], a1[:, b:b + 1], w_p2[:],
                               start=(b == 0), stop=(b == B - 1), skip_group_check=True)
            mm.then_inc(p2_ready, 1)
            def project(count, before):
                for n in range(12):
                    if n >= 2 or before:
                        pe.wait_ge(pr_free, count(n - 1))
                    dst = PR[n % 2]
                    if n < 8:
                        part, quad = divmod(n, 4)
                        for j in range(2):
                            first = (2 * quad + j) * P
                            mm = pe.matmul(dst[:, j * UNIT:(j + 1) * UNIT], w_qkv[:, part, first:first + P], xc[:],
                                           start=(j == 0), stop=(j == 1), skip_group_check=True)
                    else:
                        b, half = divmod(n - 8, 2)
                        mm = pe.matmul(dst[:], xc[:, b * P:(b + 1) * P], w_qkv[:, 2, half * 512:(half + 1) * 512],
                                       start=True, stop=True)
                    mm.then_inc(pr_ready, 1)

            pe.wait_ge(xc_ready, 16)
            pe.wait_ge(sel_ready, 1)
            project(lambda n: n, 0)
            pe.wait_ge(masks_in, 32)
            pe.sem_inc(turned, 1)
            pe.sem_inc(pvd, 1)
            with pe.Fori(0, UNITS) as u:
                base = u * PR_USES
                pe.wait_ge(pr_free, base + 8)
                for m in range(MB):
                    pe.wait_ge(sc_max, u * MB + max(m, 1))
                    for i in range(4):
                        cols = slice((4 * m + i) * TB, (4 * m + i + 1) * TB)
                        mm = pe.matmul(S[m % 2][:, i * P:(i + 1) * P], qT[:, cols, :].rearrange("p t h -> p (t h)"),
                                       kT[:, cols, :].rearrange("p t h -> p (t h)"),
                                       start=(i == 0), stop=(i == 3), skip_group_check=True)
                    mm.then_inc(score, 1)
                pe.wait_ge(xc_ready, u * 16 + 32)
                project(lambda n: base + PROJ + n, 1)

                def turn_probs(m):
                    pe.wait_ge(spread, u * MB + m + 2)
                    pe.wait_ge(tcopy, u * MB + max(m, 1))
                    for i in range(4):
                        mm = pe.transpose(TR[m % 2][:, i * P:(i + 1) * P],
                                          pex[:, m % 2, i].rearrange("p t g -> p (t g)"), ident[:])
                    mm.then_inc(turned, 1)

                turn_probs(0)
                for m in range(MB):
                    if m + 1 < MB:
                        turn_probs(m + 1)
                    if m == 0:
                        pe.wait_ge(v_in, u * 16 + 16)
                    pe.wait_ge(tcopy, u * MB + m + 2)
                    if m % 2 == 0:
                        pe.wait_ge(ocopy, u * (MB // 2) + max(m // 2, 1))
                    for i in range(4):
                        k = 4 * m + i
                        for h in range(2):
                            mm = pe.matmul(O[m // 2 % 2][h * HD1:(h + 1) * HD1, (k % 8) * 64:(k % 8 + 1) * 64],
                                           vb[:, k, :], ptT[:, m % 2, i, h:P:2], start=(k % 8 == 0), stop=(k % 8 == 7),
                                           skip_group_check=True)
                    mm.then_inc(pvd, 1)
                    if m in (5, MB - 1):
                        b = m // 6
                        pe.wait_ge(ocopy, u * (MB // 2) + 2 * b + 3)
                        pe.wait_ge(pr_free, base + 2 * PROJ - 1 + b)
                        for p in range(PAIRS):
                            mm = pe.matmul(PR[b][:, 0:D], onT[:, b * P:(b + 1) * P, p], w_out[:, p, :],
                                           start=(p == 0), stop=(p == PAIRS - 1))
                        mm.then_inc(pr_ready, 1)

            for b in range(B):
                pe.wait_ge(d_exp, 16 * B)
                if b == 0:
                    pe.wait_ge(pr_free, UNITS * PR_USES + PROJ)
                    pe.wait_ge(ocopy, UNITS * MB // 2 + 1)
                for f in range(FT):
                    n = b * FT + f
                    if n >= 4:
                        pe.wait_ge(f_gelu, n - 3)
                    pe.matmul(bank[1 + n % 4][:], ew[:, b, f * P:(f + 1) * P], xn2T_cb[:, :, b, :],
                              start=True, stop=True).then_inc(f_ready, 1)
            for b in range(B):
                pe.wait_ge(f_gelu, FT * (b + 1))
                if b >= 2:
                    pe.wait_ge(r_done, b - 1)
                for f in range(FT):
                    mm = pe.matmul(bank[5 + b % 2][:], ew[:, b, F + f * D:F + (f + 1) * D], hg1[:, b, f, :],
                                   start=(f == 0), stop=(f == FT - 1))
                mm.then_inc(r_ready, 1)
            for b in range(B):
                pe.wait_ge(r_done, b + 1)
                for t in range(CH):
                    mm = pe.matmul(bank[1 + b][:, t * D:(t + 1) * D], rT[:, b, t * P:(t + 1) * P], w_o[:],
                                   start=(t == 0), stop=(t == CH - 1), skip_group_check=True)
                mm.then_inc(o_ready, 1)


        @block.scalar
        def _(act):
            def side(t):
                for c in range(CH):
                    if t == ATT_EXP_STEP + 6 * c:
                        act.wait_ge(sc_ready, c + 1)
                        nc.scalar.activation(sc[:, c].rearrange("p a b h -> p (a b h)"),
                                             sc[:, c].rearrange("p a b h -> p (a b h)"), ACT.Exp,
                                             scale=float(HD0) ** -0.5).then_inc(pe_ready, 1)
                    if t == GATE_TANH_STEP + c:
                        act.wait_ge(misc_free, MISC_AT[("gate", c, 0)] + 1)
                        nc.scalar.activation(tg[:, c], tg[:, c], ACT.Tanh, scale=0.5).then_inc(tg_ready, 1)
                    if t == MOE_STEP + MOE_PERIOD * E * (c + 1) + MOE_LAG:
                        act.wait_ge(z_ready, c + 1)
                        nc.scalar.activation(tz[:, c], x1[:, c], ACT.Tanh, scale=0.5).then_inc(tz_ready, 1)
                if t == ROUTER_EXP_STEP:
                    act.wait_ge(lg_ready, 1)
                    nc.scalar.activation(ex[:], ex[:], ACT.Exp).then_inc(ex_ready, 1)
                i, r = divmod(t - MOE_STEP, MOE_PERIOD)
                if 0 <= i < CH * E and r in (0, 4):
                    n = FT * i + r // 4
                    act.wait_ge(hm_ready, n + 1)
                    if n >= 4:
                        act.wait_ge(y_ready, n // 2 - 1)
                    nc.scalar.activation(hg[:, n % 4, :], bank[1 + n % 4][:], ACT.Gelu).then_inc(hg_ready, 1)

            for t in range(T):
                act.wait_ge(chain_sum, t + 1)
                nc.scalar.activation(state[:, t // P, :, t % P], bank[0][:, 0:B], ACT.Tanh).then_inc(chain_state, 1)
                side(t)
            for t in range(T, MOE_STEP + MOE_PERIOD * E * CH + MOE_LAG + 1):
                side(t)

            act.wait_ge(p1_ready, 1)
            nc.scalar.activation(a1[:], bank[5][:, 0:B], ACT.Gelu, bias=b_p1[:]).then_inc(a1_ready, 1)
            def q_copy(quad, src):
                for j in range(2):
                    for h in range(2):
                        pair = 2 * quad + j
                        rows = slice(h * HD1, (h + 1) * HD1)
                        q = nc.scalar.activation(qT[0:HD1, :, 2 * pair + h], src[rows, j * UNIT:(j + 1) * UNIT],
                                                 ACT.Identity, bias=bq8[rows, pair:pair + 1], scale=float(HD1) ** -0.5)
                q.then_inc(pr_free, 1)

            def o_copy(u, n):
                act.wait_ge(pvd, u * MB + 2 * n + 3)
                if n == 0:
                    act.wait_ge(pr_ready, u * PR_USES + PROJ)
                nc.scalar.copy(onT[:, n * 64:(n + 1) * 64, :].rearrange("p t h -> p (t h)"), O[n % 2][:]).then_inc(ocopy, 1)

            act.wait_ge(bc_done, 2)
            act.sem_inc(tcopy, 1)
            act.sem_inc(ocopy, 1)
            for quad in range(4):
                act.wait_ge(pr_ready, quad + 1)
                q_copy(quad, PR[quad % 2])
            with act.Fori(0, UNITS) as u:
                base = u * PR_USES + PROJ
                act.wait_ge(sc_sub, u + 1)
                nc.scalar.activation(sc1[:], sc1[:], ACT.Exp).then_inc(sc_exp, 1)
                for quad in range(4):
                    act.wait_ge(pr_ready, base + quad + 1)
                    act.wait_ge(pr_free, base + quad)
                    q_copy(quad, PR[quad % 2])
                for m in range(MB):
                    act.wait_ge(turned, u * MB + m + 2)
                    act.wait_ge(pvd, u * MB + max(m, 1))
                    nc.scalar.copy(ptT[:, m % 2].rearrange("p k c -> p (k c)"), TR[m % 2][:]).then_inc(tcopy, 1)
                    if m >= 2 and m % 2 == 0:
                        o_copy(u, m // 2 - 1)
                o_copy(u, MB // 2 - 1)

            act.wait_ge(d_exp, 16 * B)
            for b in range(B):
                for f in range(FT):
                    n = b * FT + f
                    act.wait_ge(f_ready, n + 1)
                    nc.scalar.activation(hg1[:, b, f, :], bank[1 + n % 4][:], ACT.Gelu,
                                         bias=ew[:, b, 2 * F + f:2 * F + f + 1]).then_inc(f_gelu, 1)
            act.wait_ge(z1_ready, B)
            for c in range(CH):
                nc.scalar.activation(tz1[:, c], z1[:, c], ACT.Tanh, scale=0.5).then_inc(tz1_ready, 1)

        @block.vector
        def _(dve):
            count = [0]

            def own(ins_):
                count[0] += 1
                ins_.then_inc(vec, 1)
                return count[0]

            def stats_of(ln, c, src, b):
                own(nc.vector.bn_stats(stats[:, ln, c, b, :], src[:, c, b, :]))

            def aggr_of(ln, c, b, done):
                dve.wait_ge(vec, done)
                return own(nc.vector.bn_aggr(mv[:, ln, c, b, :], stats[:, ln, c, b, :]))

            def variance(ln, c, done):
                dve.wait_ge(vec, done)
                nc.vector.tensor_scalar(var[:, ln, c, :], mv[:, ln, c, :, 1], EPS, None, ALU.add).then_inc(var_ready, 1)

            def read(use):
                dve.wait_ge(misc_ready, MISC_AT[use] + 1)
                return misc_bank(use)

            def flat(t):
                return t.rearrange("p b t -> p (b t)")

            def ln_stats(ln, c, src):
                for b in range(B):
                    stats_of(ln, c, src, b)
                    yield
                base = count[0] - B
                for b in range(B):
                    last = aggr_of(ln, c, b, base + b + 1)
                    if b % 2:
                        yield
                variance(ln, c, last)
                yield

            def evac_xnT(c):
                nc.vector.tensor_copy(flat(xnT[:, c]), read(("xnT", c, 0))[:]).then_inc(misc_free, 1)

            def evac_px(c):
                nc.vector.tensor_scalar(flat(px[:, c]), read(("px", c, 0))[:], cols0[:, 0:1], None,
                                        ALU.add).then_inc(misc_free, 1)

            dve.wait_ge(d_x[0], 16)
            for _ in ln_stats(0, 0, x_tok):
                pass
            dve.wait_ge(d_early, N_EARLY)
            evac_xnT(0)
            evac_px(0)

            slot = [0]

            def until(t):
                while slot[0] < t:
                    yield

            def prep(c):
                dve.wait_ge(tz_ready, c + 1)
                dve.wait_ge(tg_ready, c + 1)
                m = own(nc.vector.scalar_tensor_tensor(out=flat(x1[:, c]), in0=flat(tz[:, c]), scalar=1.0, in1=flat(x1[:, c]),
                                                       op0=ALU.add, op1=ALU.mult))
                yield
                dve.wait_ge(vec, m)
                m = own(nc.vector.scalar_tensor_tensor(out=flat(mix[:, c]), in0=flat(tg[:, c]), scalar=1.0, in1=flat(x1[:, c]),
                                                       op0=ALU.add, op1=ALU.mult))
                yield
                dve.wait_ge(vec, m)
                dve.wait_ge(sT_ready, c + 1)
                m = nc.vector.scalar_tensor_tensor(out=flat(mix[:, c]), in0=bank[7][:], scalar=0.25, in1=flat(mix[:, c]),
                                                   op0=ALU.mult, op1=ALU.mult)
                m.then_inc(sT_free, 1)
                yield
                dve.wait_ge(sT_free, c + 1)
                own(nc.vector.tensor_tensor(flat(x_tok[:, c]), flat(x_tok[:, c]), flat(mix[:, c]), ALU.add))
                yield
                dve.wait_ge(vec, count[0])
                yield from ln_stats(3, c, x_tok)

            def evac_xn2T(c):
                dve.wait_ge(xn2T_ready, c + 1)
                nc.vector.tensor_copy(xn2T[:, 2 * c:2 * c + 2, :].rearrange("p u t -> p (u t)"), bank[7][:]
                                      ).then_inc(xn2T_done, 1)

            def side():
                for c in range(1, CH):
                    dve.wait_ge(d_x[c], 16)
                    yield from ln_stats(0, c, x_tok)
                for c in range(1, CH):
                    evac_xnT(c)
                    yield
                    yield
                    yield
                    evac_px(c)
                    yield
                for c in range(CH):
                    if c == 0:
                        dve.wait_ge(normed, B * CH)
                    yield from ln_stats(1, c, xn_tok)
                for c in range(CH):
                    nc.vector.tensor_scalar(flat(hnT[:, c]), read(("hnT", c, 0))[:], cols0[:, 1:2], cols0[:, 2:3],
                                            ALU.mult, ALU.add).then_inc(misc_free, 1)
                    yield
                for c in range(CH):
                    for b in range(B):
                        nc.vector.tensor_tensor(qkv[:, c, b, :], read(("qkv", c, b))[:, 0:3 * D], rows0[:, 0:3 * D],
                                                ALU.add).then_inc(misc_free, 1)
                        yield
                dve.wait_ge(consts, 12)
                for c in range(CH):
                    dve.wait_ge(qk_prod, c + 1)
                    n = 0
                    for s in range(B):
                        last = own(nc.vector.tensor_reduce(
                            sc[:, c, s, 0:s + 1, :].rearrange("p u h -> p (u h)"),
                            prod[:, c, n:n + s + 1, :].rearrange("p u (h d) -> p (u h) d", h=H0), X, ALU.add))
                        n += s + 1
                        yield
                    dve.wait_ge(vec, last)
                    last = own(nc.vector.tensor_reduce(mx0[:, c], sc[:, c].rearrange("p s u h -> p s h u"), X, ALU.max))
                    yield
                    dve.wait_ge(vec, last)
                    nc.vector.tensor_tensor(sc[:, c], sc[:, c], mx0[:, c].unsqueeze(2).broadcast_to([P, B, B, H0]),
                                            ALU.subtract).then_inc(sc_ready, 1)
                    assert slot[0] <= ATT_EXP_STEP + 6 * c, slot
                    yield
                for c in range(CH):
                    yield from until(ATT_EXP_STEP + 6 * c + 1)
                    dve.wait_ge(pe_ready, c + 1)
                    last = own(nc.vector.tensor_reduce(rs0[:, c], sc[:, c].rearrange("p s u h -> p s h u"), X, ALU.add))
                    yield
                for c in range(CH):
                    dve.wait_ge(vec, last - CH + 1 + c)
                    own(nc.vector.reciprocal(rs0[:, c], rs0[:, c]))
                    yield
                last += CH
                for c in range(CH):
                    dve.wait_ge(vec, last - CH + 1 + c)
                    nc.vector.tensor_tensor(sc[:, c], sc[:, c], rs0[:, c].unsqueeze(2).broadcast_to([P, B, B, H0]),
                                            ALU.mult).then_inc(prob_ready, 1)
                    yield
                for _ in range(6):
                    yield
                for c in range(CH):
                    dve.wait_ge(pv_prod, c + 1)
                    n = 1
                    for s in range(1, B):
                        ins_ = nc.vector.tensor_reduce(att[:, c, s, :], prod[:, c, n:n + s + 1, :].rearrange("p u e -> p e u"),
                                                       X, ALU.add)
                        n += s + 1
                        if s < B - 1:
                            yield
                    ins_.then_inc(att_ready, 1)
                    yield
                for c in range(CH):
                    nc.vector.tensor_copy(flat(attT[:, c]), read(("attT", c, 0))[:]).then_inc(misc_free, 1)
                    yield
                for c in range(CH):
                    nc.vector.tensor_tensor(tg[:, c], read(("gate", c, 0))[:].rearrange("p (b d) -> p b d", b=B),
                                            rows0[:, 4 * D:5 * D].unsqueeze(1).broadcast_to([P, B, D]), ALU.add).then_inc(misc_free, 1)
                    yield
                for c in range(CH):
                    dve.wait_ge(xnb_ready, c + 1)
                    nc.vector.tensor_tensor(flat(x1[:, c]), read(("proj", c, 0))[:], flat(xnb[:, c]), ALU.add).then_inc(misc_free, 1)
                    yield
                for c in range(CH):
                    dve.wait_ge(misc_free, MISC_AT[("proj", c, 0)] + 1)
                    yield from ln_stats(2, c, x1)
                for c in range(CH):
                    nc.vector.tensor_scalar(flat(h2T[:, c]), read(("h2T", c, 0))[:], cols0[:, 3:4], cols0[:, 4:5],
                                            ALU.mult, ALU.add).then_inc(misc_free, 1)
                    yield
                for c in range(CH):
                    ins_ = nc.vector.tensor_copy(lg[:, c * B:(c + 1) * B, :],
                                                 read(("router", c, 0))[:, 0:B * E].rearrange("p (b e) -> p b e", b=B))
                    ins_.then_inc(misc_free, 1)
                    yield
                dve.wait_ge(misc_free, MISC_AT[("router", CH - 1, 0)] + 1)

                def wide(v):
                    return v.unsqueeze(2).broadcast_to([P, CH * B, E])

                fall = falling[:].unsqueeze(1).broadcast_to([P, CH * B, E])
                m = own(nc.vector.tensor_reduce(r16[:, 0], lg[:], X, ALU.max))
                yield
                dve.wait_ge(vec, m)
                nc.vector.tensor_tensor(ex[:], lg[:], wide(r16[:, 0]), ALU.subtract).then_inc(lg_ready, 1)
                assert slot[0] <= ROUTER_EXP_STEP, slot

                yield

                def first_max(src, top, n, hot):
                    m = own(nc.vector.tensor_tensor(hot[:], src[:], wide(top), ALU.is_equal))
                    dve.wait_ge(vec, m)
                    m = own(nc.vector.tensor_tensor(hot[:], hot[:], fall, ALU.mult))
                    yield
                    dve.wait_ge(vec, m)
                    m = own(nc.vector.tensor_reduce(r16[:, n], hot[:], X, ALU.max))
                    dve.wait_ge(vec, m)
                    own(nc.vector.tensor_tensor(hot[:], hot[:], wide(r16[:, n]), ALU.is_equal))
                    yield

                yield from first_max(lg, r16[:, 0], 1, oh1)
                dve.wait_ge(vec, count[0])
                m = own(nc.vector.scalar_tensor_tensor(out=lg2[:], in0=oh1[:], scalar=NEG, in1=lg[:], op0=ALU.mult, op1=ALU.add))
                yield
                dve.wait_ge(vec, m)
                m = own(nc.vector.tensor_reduce(r16[:, 2], lg2[:], X, ALU.max))
                dve.wait_ge(vec, m)
                yield from first_max(lg2, r16[:, 2], 3, oh2)
                dve.wait_ge(vec, count[0])
                own(nc.vector.tensor_tensor(oh1[:], oh1[:], oh2[:], ALU.add))
                yield
                yield from until(ROUTER_EXP_STEP + 1)
                dve.wait_ge(ex_ready, 1)
                m = own(nc.vector.tensor_reduce(r16[:, 4], ex[:], X, ALU.add))
                yield
                dve.wait_ge(vec, m)
                m = own(nc.vector.reciprocal(r16[:, 5], r16[:, 4]))
                own(nc.vector.tensor_tensor(ex[:], ex[:], oh1[:], ALU.mult))
                yield
                dve.wait_ge(vec, m + 1)
                own(nc.vector.tensor_tensor(gates[:], ex[:], wide(r16[:, 5]), ALU.mult))
                yield

                def constants():
                    dve.wait_ge(d_late, N_LATE)
                    nc.vector.tensor_scalar(rows1[:, D:2 * D], rows1[:, D:2 * D], 0.3, None, ALU.mult).then_inc(bc_done, 1)
                    yield
                    nc.vector.tensor_scalar(bq8[:], bqk[:, 0, :], float(HD1) ** -0.5, None, ALU.mult).then_inc(bc_done, 1)
                    yield

                spare = constants()
                dve.wait_ge(vec, count[0])
                last = [None] * B
                for i in range(CH * E):
                    c, e = divmod(i, E)
                    yield from until(MOE_STEP + MOE_PERIOD * i + MOE_LAG)
                    dve.wait_ge(y_ready, i + 1)
                    for b in range(B):
                        if e:
                            dve.wait_ge(vec, last[b])
                        ins_ = nc.vector.scalar_tensor_tensor(
                            out=x1[:, c, b, :], in0=bank[5 + i % 2][:, b * D:(b + 1) * D],
                            scalar=gates[:, c * B + b, e:e + 1], in1=x1[:, c, b, :], op0=ALU.mult, op1=ALU.add)
                        last[b] = own(ins_)
                        if b < B - 1:
                            yield
                    dve.wait_ge(vec, last[B - 1])
                    dve.sem_inc(y_free, 1)
                    if e == E - 1:
                        dve.sem_inc(z_ready, 1)
                    yield
                    if c and e == 1:
                        spare = prep(c - 1)
                    for _ in range(4):
                        next(spare, None)
                        yield
                    if c and e == 6:
                        for _ in spare:
                            yield
                        evac_xn2T(c - 1)

            work = side()
            for t in range(T):
                if t == 0:
                    dve.wait_ge(consts, 3)
                    prev = zero_state[:]
                    dve.wait_ge(misc_free, 2)
                else:
                    dve.wait_ge(chain_state, t)
                    prev = state[:, (t - 1) // P, :, (t - 1) % P]
                if t and t % P == 0:
                    dve.wait_ge(misc_free, MISC_AT[("px", t // P, 0)] + 1)
                nc.vector.tensor_tensor(bank[0][:, 0:B], px[:, t // P, :, t % P], prev, ALU.add).then_inc(chain_sum, 1)
                slot[0] = t
                next(work, None)
            slot[0] = 10 ** 6
            for _ in work:
                pass
            for _ in prep(CH - 1):
                pass
            evac_xn2T(CH - 1)

            dve.wait_ge(p2_ready, 1)
            lgs, eq = rt[:, 0], rt[:, 1]
            m = own(nc.vector.tensor_tensor(lgs, bank[6][0:1, 0:B * E].rearrange("p (b e) -> p b e", b=B),
                                            b_p2[:].unsqueeze(1).broadcast_to([1, B, E]), ALU.add))
            dve.wait_ge(vec, m)
            m = own(nc.vector.tensor_reduce(rt[:, 2, :, 0], lgs, X, ALU.max))
            dve.wait_ge(vec, m)
            m = own(nc.vector.tensor_tensor(eq, lgs, rt[:, 2, :, 0:1].broadcast_to([1, B, E]), ALU.is_equal))
            dve.wait_ge(vec, m)
            m = own(nc.vector.tensor_tensor(eq, eq, falling[0:1, :].unsqueeze(1).broadcast_to([1, B, E]), ALU.mult))
            dve.wait_ge(vec, m)
            m = own(nc.vector.tensor_reduce(rt[:, 3, :, 0], eq, X, ALU.max))
            dve.wait_ge(vec, m)
            nc.vector.tensor_scalar(sel[:], rt[:, 3, :, 0], -1.0, float(E), ALU.mult, ALU.add).then_inc(sel_ready, 1)

            def k_copy(quad, src):
                for h in range(2):
                    rows = slice(h * HD1, (h + 1) * HD1)
                    pairs = slice(2 * quad, 2 * quad + 2)
                    for b in range(2):
                        k = nc.vector.tensor_tensor(
                            kT[0:HD1, b * P:(b + 1) * P, 4 * quad + h:4 * quad + h + 3:2].rearrange("p t j -> p j t"),
                            src[rows, :].rearrange("p (j b t) -> p j b t", j=2, b=2)[:, :, b, :],
                            posb[rows, pairs, :], ALU.add)
                k.then_inc(pr_free, 1)

            def v_copy(n, src):
                b, half = divmod(n, 2)
                cols = slice(half * 512, (half + 1) * 512)
                nc.vector.tensor_tensor(vt[:, b, cols], src[:], bv_row[:, cols], ALU.add).then_inc(pr_free, 1)

            dve.sem_inc(sc_max, 1)
            dve.wait_ge(posb_ready, 1)
            for n in range(4, 12):
                dve.wait_ge(pr_ready, n + 1)
                dve.wait_ge(pr_free, n)
                k_copy(n - 4, PR[n % 2]) if n < 8 else v_copy(n - 8, PR[n % 2])

            def per_block(t):
                return t.unsqueeze(2).broadcast_to([P, KB, H1])

            with dve.Fori(0, UNITS) as u:
                base = u * PR_USES + PROJ
                for m in range(MB):
                    dve.wait_ge(score, u * MB + m + 1)
                    if m == 0:
                        dve.wait_ge(spread, u * MB + 1)
                    nc.vector.tensor_reduce(sc1[:, 4 * m:4 * m + 4, :],
                                            S[m % 2][:].rearrange("p (k t g) -> p k g t", k=4, t=TB), X, ALU.max
                                            ).then_inc(sc_max, 1)
                dve.wait_ge(sc_max, u * MB + MB + 1)
                nc.vector.tensor_reduce(m1[:, 0], sc1[:], X, ALU.max).then_inc(small, 1)
                dve.wait_ge(small, u * 3 + 1)
                nc.vector.tensor_tensor(sc1[:], sc1[:], per_block(m1[:, 0]), ALU.subtract).then_inc(sc_sub, 1)
                dve.wait_ge(sc_exp, u + 1)
                nc.vector.tensor_reduce(m1[:, 1], sc1[:], X, ALU.add).then_inc(small, 1)
                dve.wait_ge(small, u * 3 + 2)
                nc.vector.reciprocal(m1[:, 2], m1[:, 1]).then_inc(small, 1)
                dve.wait_ge(small, u * 3 + 3)
                nc.vector.tensor_tensor(sc1[:], sc1[:], per_block(m1[:, 2]), ALU.mult).then_inc(prob, 1)
                dve.wait_ge(posb_ready, u + 2)
                for n in range(4, 12):
                    dve.wait_ge(pr_ready, base + n + 1)
                    dve.wait_ge(pr_free, base + n)
                    if n == 8:
                        dve.wait_ge(v_out, u * 16 + 16)
                    k_copy(n - 4, PR[n % 2]) if n < 8 else v_copy(n - 8, PR[n % 2])
                for b in range(2):
                    dve.wait_ge(pr_ready, base + 12 + b + 1)
                    s_tile = s_all[:].rearrange("p c b d -> p (c b) d")[:, bass.ds(2 * u + b, 1), :]
                    nc.vector.tensor_tensor(s_tile.rearrange("p a d -> p (a d)"), PR[b][:, 0:D], rows1[:, 0:D],
                                            ALU.add).then_inc(pr_free, 1)

            dve.wait_ge(d_exp, 16 * B)
            for b in range(B):
                dve.wait_ge(r_ready, b + 1)
                nc.vector.tensor_scalar(rT[:, b, :], bank[5 + b % 2][:], ew[:, b, 2 * F + 2:2 * F + 3], None,
                                        ALU.add).then_inc(r_done, 1)
            dve.wait_ge(xnb2_ready, CH)
            for b in range(B):
                dve.wait_ge(o_ready, b + 1)
                nc.vector.scalar_tensor_tensor(out=z1[:, :, b, :], in0=bank[1 + b][:].rearrange("p (c d) -> p c d", c=CH),
                                               scalar=0.3, in1=xnb2[:, :, b, :], op0=ALU.mult, op1=ALU.add).then_inc(z1_ready, 1)
            for c in range(CH):
                dve.wait_ge(tz1_ready, c + 1)
                m = own(nc.vector.scalar_tensor_tensor(out=flat(z1[:, c]), in0=flat(tz1[:, c]), scalar=1.0, in1=flat(z1[:, c]),
                                                       op0=ALU.add, op1=ALU.mult))
                dve.wait_ge(vec, m)
                m = own(nc.vector.scalar_tensor_tensor(out=flat(z1[:, c]), in0=flat(z1[:, c]), scalar=0.5, in1=flat(s_all[:, c]),
                                                       op0=ALU.mult, op1=ALU.mult))
                dve.wait_ge(vec, m)
                nc.vector.tensor_tensor(flat(y_all[:, c]), flat(z1[:, c]), flat(x_tok[:, c]), ALU.add).then_inc(y_done, 1)


def positions():
    p = np.arange(T, dtype=np.float32)[:, None]
    div = np.exp(np.arange(0, HD1, 2, dtype=np.float32) * np.float32(-(np.log(10000.0) / HD1))).astype(np.float32)
    ang = (p * div).astype(np.float32)
    pe = np.zeros((T, HD1), np.float32)
    pe[:, 0::2] = np.sin(ang)
    pe[:, 1::2] = np.cos(ang)
    both = np.concatenate([pe.T, pe.T], 0).reshape(P, CH, P)
    return np.concatenate([both.repeat(2, 1), both[:, :1]], 1)


def block_masks():
    own = np.zeros((HD1, TB, H1), np.float32)
    own[np.arange(TB), np.arange(TB)] = 1.0
    others = np.zeros_like(own)
    others[:TB] = np.where(own[:TB] == 1.0, 0.0, MASKED)
    return own.reshape(HD1, P), others.reshape(HD1, P)


def kernel(**inputs):
    import concourse.bacc as bacc
    from concourse.bass_utils import run_bass_kernel_spmd

    a = {k: np.asarray(v) for k, v in inputs.items()}

    def rows(*vs):
        return np.broadcast_to(np.concatenate(vs)[None, :], (P, sum(v.size for v in vs)))

    wq = a["L1_attn_w_qkv"].reshape(D, H1, 3, HD1).transpose(0, 2, 1, 3).reshape(D, 3, H1 * HD1)
    bq = a["L1_attn_b_qkv"].reshape(PAIRS, 2, 3, HD1)
    mask_q, mask_k = block_masks()
    experts = np.concatenate([
        a["L1_ffn_W1"],
        a["L1_ffn_W2"].reshape(E, FT, P, D).transpose(0, 2, 1, 3).reshape(E, P, FT * D),
        a["L1_ffn_b1"].reshape(E, FT, P).transpose(0, 2, 1),
        a["L1_ffn_b2"][:, :, None]], axis=2)
    data = {
        "x": a["L0_attn_x"],
        "w_state": a["L0_attn_W_state"].T, "w_gate": a["L0_attn_W_gate"].T,
        "w_in": a["L0_ffn_in_proj_w"].T, "w_op": a["L0_ffn_out_proj_w"].T,
        "w_router": a["L0_ffn_router_w"].T,
        "w1": a["L0_ffn_w1"].transpose(1, 0, 2).reshape(D, E * F),
        "w2": a["L0_ffn_w2"].reshape(E, FT, P, D).transpose(2, 0, 1, 3),
        "cols0": np.stack([a["L0_attn_b_state"], a["L0_ffn_ln1_w"], a["L0_ffn_ln1_b"], a["L0_ffn_ln2_w"],
                           a["L0_ffn_ln2_b"]], 1),
        "rows0": rows(a["L0_ffn_in_proj_b"], a["L0_ffn_out_proj_b"], a["L0_attn_b_gate"]),
        "w_qkv": wq, "bqk": bq[:, :, 0:2].transpose(1, 3, 2, 0).reshape(P, 2, PAIRS),
        "bv_row": rows(bq[:, :, 2].reshape(-1)), "own_token": block_masks()[0][:TB].reshape(TB, P).T,
        "mask_q": mask_q, "mask_k": mask_k,
        "w_out": a["L1_attn_w_out"].reshape(PAIRS, P, D).transpose(1, 0, 2),
        "w_p1": a["L1_ffn_Wp1"], "w_p2": a["L1_ffn_Wp2"], "b_p1": a["L1_ffn_bp1"][:, None],
        "b_p2": a["L1_ffn_bp2"][None, :], "w_o": a["L1_ffn_Wo"],
        "rows1": rows(a["L1_attn_b_out"], a["L1_ffn_bo"]),
        "experts": experts, "pos": positions(),
    }
    nc = bacc.Bacc("TRN2", target_bir_lowering=False, num_devices=1)
    arrays, ins = {}, {}
    for name, v in data.items():
        v = np.ascontiguousarray(v)
        arrays[f"in_{name}"] = v
        ins[name] = nc.dram_tensor(f"in_{name}", v.shape, mybir.dt.from_np(v.dtype), kind="ExternalInput").ap()
    out = nc.dram_tensor("out_x", (B, T, D), F32, kind="ExternalOutput").ap()
    build(nc, ins, out)
    r = run_bass_kernel_spmd(nc, [arrays], core_ids=[0])
    return r.results[0]["out_x"]
```

```python
from contextlib import ExitStack

import numpy as np

import concourse.bass as bass
from concourse import mybir

ALU = mybir.AluOpType
ACT = mybir.ActivationFunctionType
F32 = mybir.dt.float32
I32 = mybir.dt.int32
X = mybir.AxisListType.X

P = 128
B, T, D = 4, 512, 128
CH = T // P
BD = B * D
H0, HD0 = 16, 8
E = 8
F = 256
FT = F // P
H1, HD1 = 16, 64
PAIRS = H1 // 2
UNIT = 256
UNITS = B * T // UNIT
TB = P // H1
KB = UNIT // TB
MB = KB // 4
VECTOR_SPREADS = (4, 6)
OB = MB // 2
EPS = 1e-5
NEG = -3.0e38
MASKED = -1.0e30

XNT_STEP = (0, 19, 28, 34)
PX_STEP = (0, 27, 35, 46)
ATT_EXP_STEP = (53, 69, 88, 105)
ATTT_STEP = (98, 120, 143, 168)
H2T_STEP = (134, 151, 174, 194)
ROUTER_EXP_STEP = 204
MOE_STEP = 207
MOE_PERIOD = 9
GATE_TANH_STEP = [MOE_STEP + MOE_PERIOD * c + 1 for c in range(CH)]
MOE_LAG = 20
FREE_US = 0.3

COPY_BANKS = 2
COPIES = ([(kind, c) for c in range(CH) for kind in ("xnT", "px")]
          + [("attT", 0), ("attT", 1), ("h2T", 0), ("attT", 2), ("h2T", 1), ("attT", 3), ("h2T", 2), ("h2T", 3)])
COPY_AT = {use: n for n, use in enumerate(COPIES)}
MISC_BANKS = 4
MISC = ([("bias", 0, 0)] + [("qkv", 0, b) for b in range(B)] + [("qkv", 1, b) for b in range(B)]
        + [("qkv", 2, b) for b in range(B)] + [("qkv", 3, b) for b in range(B)]
        + [("proj", 0, 0), ("proj", 1, 0), ("gate", 0, 0), ("proj", 2, 0), ("router", 0, 0), ("gate", 1, 0),
           ("gate", 2, 0), ("gate", 3, 0), ("proj", 3, 0), ("router", 1, 0), ("router", 2, 0), ("router", 3, 0)])
MISC_AT = {use: n for n, use in enumerate(MISC)}


def build(nc, ins, out):
    with ExitStack() as ctx:
        def sb(name, *shape, dt=F32):
            return ctx.enter_context(nc.sbuf_tensor(name, list(shape), dt))

        def sem(name):
            return ctx.enter_context(nc.semaphore(name))

        bank = [ctx.enter_context(nc.psum_tensor(f"bank{i}", [P, 512], F32)) for i in range(8)]

        ident = sb("ident", P, P)
        w_state = sb("w_state", P, D)
        w_gate = sb("w_gate", P, D)
        w_in = sb("w_in", P, 3 * D)
        w_op = sb("w_op", P, D)
        w_router = sb("w_router", P, E)
        w1 = sb("w1", P, E * F)
        w2 = sb("w2", P, E, FT, D)
        cols0 = sb("cols0", P, 5)
        rows0 = sb("rows0", P, 5 * D)
        w_qkv = sb("w_qkv", P, 3, H1 * HD1)
        bqk = sb("bqk", P, 2, PAIRS)
        bq8 = sb("bq8", P, PAIRS)
        bv_row = sb("bv_row", P, H1 * HD1)
        w_out = sb("w_out", P, PAIRS, D)
        own_token = sb("own_token", P, TB)
        w_p1 = sb("w_p1", P, P)
        w_p2 = sb("w_p2", P, E)
        b_p1 = sb("b_p1", P, 1)
        b_p2 = sb("b_p2", 1, E)
        w_o = sb("w_o", P, D)
        rows1 = sb("rows1", P, 2 * D)
        pos = sb("pos", P, UNITS + 1, P)
        falling = sb("falling", P, E)
        exps = sb("exps", P, B)

        def over(tensor, shape, first=0):
            flat = tensor[:]
            while len(flat.shape) > 2:
                flat = flat.rearrange("p a b c -> p a (b c)" if len(flat.shape) == 4 else "p a b -> p (a b)")
            names = "abcd"[:len(shape)]
            flat = flat[:, first:first + int(np.prod(shape))]
            return flat.rearrange(f"p ({' '.join(names)}) -> p {' '.join(names)}", **dict(zip(names, shape)))

        x_tok = sb("x_tok", P, CH, B, D)
        xn_tok = sb("xn_tok", P, CH, B, D)
        xnT = sb("xnT", P, CH, B, P)
        px = sb("px", P, CH, B, P)
        state = sb("state", P, CH, B, P)
        zero_state = sb("zero_state", P, B)
        stats = sb("stats", P, 3, CH, B, 6)
        mv = sb("mv", P, 3, CH, B, 2)
        var = sb("var", P, 3, CH, B)
        rstd = sb("rstd", P, 3, CH, B)
        again = sb("again", P, CH, B)
        ln1_b = sb("ln1_b", P, P)
        z_tok = sb("z_tok", P, CH, B, D)
        hnT = sb("hnT", P, CH, B, P)
        heads_words = sb("heads_words", P, CH * B * 3 * D + CH * 10 * D)
        qkv = heads_words[:, 0:CH * B * 3 * D].rearrange("p (c b n) -> p c b n", c=CH, b=B)
        prod = heads_words[:, CH * B * 3 * D:].rearrange("p (c s n) -> p c s n", c=CH, s=10)
        sc = sb("sc", P, CH, B, B, H0)
        mx0 = sb("mx0", P, CH, B, H0)
        rs0 = sb("rs0", P, CH, B, H0)
        sums_words = sb("sums_words", P, 2 * CH * BD)
        att = sums_words[:, 0:CH * BD].rearrange("p (c b d) -> p c b d", c=CH, b=B)
        attT = over(heads_words, (CH, B, P))
        tz = attT
        tg = over(heads_words, (CH, B, D), CH * BD)
        mix = tg
        hg = over(heads_words, (4, BD), 2 * CH * BD)
        xnb = sums_words[:, CH * BD:].rearrange("p (c b d) -> p c b d", c=CH, b=B)
        x1 = sb("x1", P, CH, B, D)
        h2T = hnT
        lg = sb("lg", P, CH * B, E)
        lg2 = sb("lg2", P, CH * B, E)
        oh1 = sb("oh1", P, CH * B, E)
        oh2 = sb("oh2", P, CH * B, E)
        ex = sb("ex", P, CH * B, E)
        gates = sb("gates", P, CH * B, E)
        r16 = sb("r16", P, 8, CH * B)

        xn2_tok = over(xnT, (CH, B, D))
        xn2T = sb("xn2T", P, UNITS + 1, UNIT)
        a1 = sb("a1", P, B)
        rt = sb("rt", 1, 6, B, E)
        sel = sb("sel", 1, B, dt=I32)
        ew = sb("ew", P, B, 2 * F + 3)
        hg1 = over(heads_words, (B, FT, T))
        rT = over(heads_words, (B, T), B * FT * T)
        xnb2 = over(px, (CH, B, D))
        z1 = over(x1, (CH, B, D))
        tz1 = over(state, (CH, B, D))
        s_all = over(hnT, (CH, B, D))

        d_x = [sem(f"x_loaded{c}") for c in range(CH)]
        d_early = sem("early_weights_loaded")
        d_moe = sem("moe_weights_loaded")
        d_late = sem("late_weights_loaded")
        d_exp = sem("chosen_experts_loaded")
        d_out = sem("output_stored")
        ident_zero = sem("ident_zeroed")
        consts = sem("constants_ready")
        vec = sem("vector_step")
        pool = sem("pool_step")
        var_ready = sem("variance_ready")
        rstd_ready = sem("deviation_ready")
        again_ready = sem("second_norm_ready")
        ln1_b_ready = sem("ln1_shift_spread")
        w_in_ready = sem("w_in_scaled")
        normed = sem("tokens_normed")
        copy_ready = sem("copy_psum_ready")
        copied = sem("copy_psum_read")
        misc_ready = sem("misc_psum_ready")
        misc_free = sem("misc_psum_free")
        chain_sum = sem("chain_sum")
        chain_state = sem("chain_state")
        qk_prod = sem("qk_products_ready")
        sc_ready = sem("scores_centred")
        pe_ready = sem("attention_exp_ready")
        prob_ready = sem("attention_probs_ready")
        pv_prod = sem("pv_products_ready")
        att_ready = sem("attention_ready")
        xnb_ready = sem("xn_plus_bias_ready")
        lg_ready = sem("logits_centred")
        ex_ready = sem("router_exp_ready")
        tg_ready = sem("gate_tanh_ready")
        hm_ready = sem("expert_hidden_ready")
        hg_ready = sem("expert_gelu_ready")
        y_ready = sem("expert_out_ready")
        y_free = sem("expert_out_read")
        z_ready = sem("block_sum_ready")
        tz_ready = sem("block_tanh_ready")
        sT_ready = sem("state_turned")
        sT_free = sem("state_turned_read")
        xn2T_ready = sem("xn2_turned")
        xn2T_done = sem("xn2T_written")
        halved = sem("w_out_halved")
        bc_done = sem("scaled_biases_ready")
        p1_ready = sem("policy_hidden_ready")
        a1_ready = sem("policy_gelu_ready")
        p2_ready = sem("policy_logits_ready")
        sel_ready = sem("expert_chosen")
        f_ready = sem("ffn1_hidden_ready")
        f_gelu = sem("ffn1_gelu_ready")
        r_ready = sem("ffn1_reasoned_ready")
        r_done = sem("ffn1_reasoned_read")
        o_ready = sem("ffn1_out_ready")
        z1_ready = sem("ffn1_sum_ready")
        tz1_ready = sem("ffn1_tanh_ready")
        mix1_ready = sem("ffn1_gate_ready")
        xnb2_ready = sem("xn2_plus_bias_ready")

        qT = over(heads_words, (UNIT, H1), CH * B * 3 * D)
        kT = over(sums_words, (UNIT, H1))
        xc = sb("xc", P, UNIT)
        posb = sb("posb", P, PAIRS, P)
        vt = over(xn_tok, (2, H1 * HD1))
        vb = over(w2, (KB, HD1))
        sc1 = over(heads_words, (KB, H1), CH * B * 3 * D + UNIT * H1)
        m1 = over(heads_words, (3, KB), CH * B * 3 * D + UNIT * H1 + KB * H1)
        pex = over(w1, (4, 4, P)).rearrange("p r k (t g) -> p r k t g", t=TB)
        ptT = over(heads_words, (2, 4, P))
        onT = over(z_tok, (UNIT, PAIRS))
        v_dram = nc.dram_tensor("v_by_token", (2, P, H1 * HD1), F32, kind="Internal").ap()
        S, TR, O, PR = bank[0:2], bank[2:4], [bank[4], bank[7]], [bank[5], bank[6], bank[4], bank[7]]
        FB = [bank[2], bank[3], bank[4], bank[7]]
        YB = bank[0:4]
        VB = [PR[0], PR[2], PR[1], PR[3]]
        empty_unit = sem("empty_unit_ready")
        masks_in = sem("masks_loaded")
        xc_ready = sem("unit_staged")
        posb_ready = sem("positions_ready")
        q_ready = sem("q_projected")
        q_free = sem("q_copied")
        k_ready = sem("k_projected")
        k_free = sem("k_copied")
        v_ready = sem("v_projected")
        v_free = sem("v_copied")
        v_out = sem("v_stored")
        v_in = sem("v_by_block_loaded")
        vb_free = sem("v_by_block_used")
        v_made = sem("v_of_next_unit_made")
        score = sem("scores_ready")
        sc_max = sem("block_scores_ready")
        sc_sub = sem("unit_scores_centred")
        sc_exp = sem("unit_exp_ready")
        prob = sem("unit_probs_ready")
        small = sem("softmax_step")
        spread_v = sem("vector_spread_probs")
        spread_p = sem("gpsimd_spread_probs")
        turned = sem("probs_turned")
        tcopy = sem("turned_probs_copied")
        pvd = sem("pv_ready")
        even_copied = sem("values_of_even_blocks_copied")
        odd_copied = sem("values_of_odd_blocks_copied")
        s_ready = sem("attention_output_ready")
        s_free = sem("attention_output_read")
        gated = sem("output_step")
        y_done = sem("tile_output_ready")

        def tile_of(t, n):
            return t[:].rearrange("p c b d -> p (c b) d")[:, bass.ds(n, 1), :].rearrange("p a d -> p (a d)")

        def wait_spread(engine, u, m):
            if m in VECTOR_SPREADS:
                engine.wait_ge(spread_v, len(VECTOR_SPREADS) * u + VECTOR_SPREADS.index(m) + 1)
            else:
                others = [n for n in range(MB) if n not in VECTOR_SPREADS]
                engine.wait_ge(spread_p, len(others) * u + others.index(m) + 1)

        def copy_of(n, half, h):
            src = O[n % 2][half * HD1:(half + 1) * HD1, :].rearrange("p (k t q h) -> p k t q h", k=4, t=TB, h=2)
            dst = onT[h * HD1:(h + 1) * HD1, n * 64:(n + 1) * 64, :].rearrange("p (k j t) q -> p k j (t q)", k=4, j=2)
            return dst[:, :, half, :], src[:, :, :, :, h].rearrange("p k t q -> p k (t q)")

        block = ctx.enter_context(nc.Block())

        def misc_bank(use):
            return bank[3 + MISC_AT[use] % MISC_BANKS]

        def copy_bank(use):
            return bank[1 + COPY_AT[use] % COPY_BANKS]

        @block.sync
        def _(sp):
            xs = ins["x"].rearrange("b (c p) d -> p c b d", p=P)
            for c in range(CH):
                sp.dma_start(x_tok[:, c], xs[:, c]).then_inc(d_x[c], 16)
                if c == 0:
                    early = [(w_state[:], "w_state"), (cols0[:], "cols0"), (w_in[:], "w_in"),
                             (rows0[:], "rows0"), (w_op[:], "w_op"), (w_router[:], "w_router"),
                             (w_gate[:], "w_gate")]
                    for dst, name in early:
                        sp.dma_start(dst, ins[name]).then_inc(d_early, 16)
            sp.dma_start(w1[:], ins["w1"]).then_inc(d_moe, 16)
            sp.dma_start(w2[:], ins["w2"]).then_inc(d_moe, 16)
            late = [(w_out[:], "w_out"), (bqk[:], "bqk"), (rows1[:], "rows1"), (w_p1[:], "w_p1"),
                    (w_p2[:], "w_p2"), (b_p1[:], "b_p1"), (b_p2[:], "b_p2"), (w_o[:], "w_o"),
                    (w_qkv[:], "w_qkv"), (pos[:], "pos"), (bv_row[:], "bv_row"), (own_token[:], "own_token")]
            for dst, name in late:
                sp.dma_start(dst, ins[name]).then_inc(d_late, 16)
            sp.wait_ge(hg_ready, FT * CH * E)
            wide = [HD1, UNIT // TB, TB * H1]
            for dst, name in ((qT, "mask_q"), (kT, "mask_k")):
                sp.dma_start(dst[HD1:P].rearrange("p (k t) h -> p k (t h)", t=TB),
                             ins[name].unsqueeze(1).broadcast_to(wide)).then_inc(masks_in, 16)
            sp.wait_ge(empty_unit, 1)
            sp.wait_ge(xn2T_done, 1)
            sp.dma_start(xc[:], xn2T[:, 0, :]).then_inc(xc_ready, 16)

            def v_store():
                sp.dma_start(v_dram.rearrange("b p n -> p b n"), vt[:]).then_inc(v_out, 16)

            def v_load():
                sp.dma_start(vb[:], v_dram.rearrange("b (k t) (g d) -> (t g) (b k) d", t=TB, d=HD1)
                             ).then_inc(v_in, 16)

            def y_store(u):
                sp.dma_start(out[bass.ds(u, 1), :, :, :].rearrange("u b p d -> p (u b) d"),
                             s_all[:].rearrange("p c b d -> p (c b) d")[:, bass.ds(2 * u, 2), :]).then_inc(d_out, 16)

            sp.wait_ge(v_free, 4)
            v_store()
            sp.wait_ge(v_ready, 4)
            sp.wait_ge(xn2T_done, CH)
            sp.dma_start(xc[:], xn2T[:, 1, :]).then_inc(xc_ready, 16)
            sp.wait_ge(sel_ready, 1)
            for b in range(B):
                e = sp.value_load(sel[0:1, b:b + 1], min_val=0, max_val=E - 1)
                sp.dma_start(ew[:, b, :], ins["experts"][bass.ds(e, 1), :, :].rearrange("e p n -> (e p) n")
                             ).then_inc(d_exp, 16)
            sp.wait_ge(v_out, 16)
            v_load()
            with sp.Fori(0, UNITS - 1) as u:
                sp.wait_ge(v_free, 4 * u + 8)
                sp.sem_inc(v_made, 1)
                sp.wait_ge(v_in, u * 16 + 16)
                v_store()
                sp.dma_start(xc[:], xn2T[:, bass.ds(u + 2, 1), :].rearrange("p a t -> p (a t)")
                             ).then_inc(xc_ready, 16)
                sp.wait_ge(v_out, u * 16 + 32)
                sp.wait_ge(pvd, u * MB + MB + 2)
                sp.sem_inc(vb_free, 1)
                v_load()
                sp.wait_ge(y_done, 2 * u + 2)
                y_store(u)
            sp.wait_ge(v_in, 16 * UNITS)
            sp.wait_ge(xc_ready, 16 * (UNITS + 1))
            sp.wait_ge(y_done, 2 * UNITS)
            y_store(UNITS - 1)
            sp.wait_ge(d_out, 16 * UNITS)

        N_EARLY, N_MOE, N_LATE = 7 * 16, 2 * 16, 12 * 16

        @block.gpsimd
        def _(gp):
            nc.gpsimd.memset(ident[:], 0.0).then_inc(ident_zero, 1)
            nc.gpsimd.memset(exps[:], -0.5).then_inc(consts, 1)
            gp.wait_ge(ident_zero, 1)
            nc.gpsimd.affine_select(out=ident[:], in_=ident[:], compare_op=ALU.not_equal, fill=1.0, base=0,
                                    pattern=[[-1, P]], channel_multiplier=1).then_inc(consts, 1)
            nc.gpsimd.memset(zero_state[:], 0.0).then_inc(consts, 1)
            for e in range(E):
                nc.gpsimd.memset(falling[:, e:e + 1], float(E - e)).then_inc(consts, 1)
            gp.wait_ge(consts, 3)

            steps = [0]

            def own(ins_):
                steps[0] += 1
                ins_.then_inc(pool, 1)
                gp.wait_ge(pool, steps[0])

            def deviation(ln, c):
                gp.wait_ge(var_ready, ln * CH + c + 1)
                nc.gpsimd.tensor_tensor(rstd[:, ln, c, :], var[:, ln, c, :], exps[:], ALU.pow).then_inc(rstd_ready, 1)

            def second_norm(c):
                gp.wait_ge(rstd_ready, c + 1)
                own(nc.gpsimd.tensor_tensor(again[:, c, :], mv[:, 0, c, :, 1], rstd[:, 0, c, :], ALU.mult))
                own(nc.gpsimd.tensor_tensor(again[:, c, :], again[:, c, :], rstd[:, 0, c, :], ALU.mult))
                own(nc.gpsimd.tensor_scalar(again[:, c, :], again[:, c, :], EPS, None, ALU.add))
                nc.gpsimd.tensor_tensor(again[:, c, :], again[:, c, :], exps[:], ALU.pow).then_inc(again_ready, 1)

            deviation(0, 0)
            gp.wait_ge(d_early, N_EARLY)
            nc.gpsimd.tensor_copy(ln1_b[:], cols0[:, 2:3].broadcast_to([P, P])).then_inc(ln1_b_ready, 1)
            nc.gpsimd.memset(sc[:], MASKED).then_inc(consts, 1)
            second_norm(0)
            for c in range(1, CH):
                deviation(0, c)
                if c >= 2:
                    second_norm(c - 1)
            second_norm(CH - 1)

            def qk_products(c):
                gp.wait_ge(misc_free, MISC_AT[("qkv", c, B - 1)] + 1)
                n = 0
                for s in range(B):
                    q = qkv[:, c, s:s + 1, 0:D].broadcast_to([P, s + 1, D])
                    ins_ = nc.gpsimd.tensor_tensor(prod[:, c, n:n + s + 1, :], q, qkv[:, c, 0:s + 1, D:2 * D], ALU.mult)
                    n += s + 1
                ins_.then_inc(qk_prod, 1)

            def pv_products(c):
                gp.wait_ge(prob_ready, c + 1)
                n = 0
                for s in range(B):
                    for u in range(s + 1):
                        prb = sc[:, c, s, u, :].unsqueeze(2).broadcast_to([P, H0, HD0])
                        dst = att[:, c, 0, :] if s == 0 else prod[:, c, n, :]
                        ins_ = nc.gpsimd.tensor_tensor(
                            dst.rearrange("p (h d) -> p h d", h=H0), prb,
                            qkv[:, c, u, 2 * D:3 * D].rearrange("p (h d) -> p h d", h=H0), ALU.mult)
                        n += 1
                ins_.then_inc(pv_prod, 1)

            def plus_bias(c):
                gp.wait_ge(normed, c + 1)
                nc.gpsimd.tensor_tensor(
                    xnb[:, c], xn_tok[:, c], rows0[:, 3 * D:4 * D].unsqueeze(1).broadcast_to([P, B, D]),
                    ALU.add).then_inc(xnb_ready, 1)

            plus_bias(0)
            plus_bias(1)
            plus_bias(2)
            qk_products(0)
            plus_bias(3)
            qk_products(1)
            qk_products(2)
            pv_products(0)
            qk_products(3)
            pv_products(1)
            pv_products(2)
            deviation(1, 0)
            pv_products(3)
            deviation(1, 1)
            deviation(1, 2)
            deviation(1, 3)
            gp.wait_ge(d_late, N_LATE)
            nc.gpsimd.tensor_scalar(w_out[:], w_out[:], 0.5, None, ALU.mult).then_inc(halved, 1)
            nc.gpsimd.tensor_scalar(rows1[:, 0:D], rows1[:, 0:D], 0.5, None, ALU.mult).then_inc(halved, 1)
            nc.gpsimd.memset(xn2T[:, UNITS, :], 0.0).then_inc(empty_unit, 1)
            for c in range(CH):
                deviation(2, c)
                gp.wait_ge(normed, 2 * CH + c + 1)
                if c == 0:
                    gp.wait_ge(bc_done, 1)
                nc.gpsimd.tensor_tensor(
                    xnb2[:, c], xn2_tok[:, c], rows1[:, D:2 * D].unsqueeze(1).broadcast_to([P, B, D]),
                    ALU.add).then_inc(xnb2_ready, 1)

            def positions_of(chunk):
                nc.gpsimd.tensor_tensor(posb[:], chunk.broadcast_to([P, PAIRS, P]),
                                        bqk[:, 1, :].unsqueeze(2).broadcast_to([P, PAIRS, P]),
                                        ALU.add).then_inc(posb_ready, 1)

            def spread_pool(u, m):
                gp.wait_ge(turned, u * MB + m + 1)
                nc.gpsimd.tensor_tensor(
                    pex[:, m % 4], sc1[:, 4 * m:4 * m + 4, :].unsqueeze(2).broadcast_to([P, 4, TB, H1]),
                    own_token[:].unsqueeze(1).unsqueeze(3).broadcast_to([P, 4, TB, H1]), ALU.mult).then_inc(spread_p, 1)

            def output(u, b):
                s = tile_of(s_all, 2 * u + b)
                gp.wait_ge(s_free, 2 * u + b + 3)
                nc.gpsimd.tensor_tensor(s, s, tile_of(z1, 2 * u + b), ALU.mult).then_inc(gated, 1)
                gp.wait_ge(gated, 2 * u + b + 1)
                nc.gpsimd.tensor_tensor(s, s, tile_of(x_tok, 2 * u + b), ALU.add).then_inc(y_done, 1)

            gp.wait_ge(d_late, N_LATE)
            positions_of(pos[:, 0:1, :])
            gp.wait_ge(k_free, 4)
            positions_of(pos[:, 1:2, :])
            with gp.Fori(0, UNITS - 1) as u:
                gp.wait_ge(prob, u + 1)
                for m in range(4):
                    spread_pool(u, m)
                gp.wait_ge(k_free, 4 * u + 8)
                positions_of(pos[:, bass.ds(u + 2, 1), :])
                spread_pool(u, 5)
                spread_pool(u, 7)
                output(u, 0)
                output(u, 1)
            gp.wait_ge(prob, UNITS)
            for m in range(MB):
                if m not in VECTOR_SPREADS:
                    spread_pool(UNITS - 1, m)
            for b in range(2):
                output(UNITS - 1, b)

        @block.tensor
        def _(pe):
            def fill(use):
                n = MISC_AT[use]
                if n >= MISC_BANKS:
                    pe.wait_ge(misc_free, n - MISC_BANKS + 1)
                return misc_bank(use)

            def turn(dst, src):
                for b in range(B):
                    mm = pe.transpose(dst[:, b * P:(b + 1) * P], src[:, b, :], ident[:])
                return mm

            def fill_copy(use):
                n = COPY_AT[use]
                if n >= COPY_BANKS:
                    pe.wait_ge(copied, n - COPY_BANKS + 1)
                return copy_bank(use)

            def turn_xn(c):
                pe.wait_ge(normed, c + 1)
                turn(fill_copy(("xnT", c)), xn_tok[:, c]).then_inc(copy_ready, 1)

            def proj_px(c):
                dst = fill_copy(("px", c))
                pe.wait_ge(copied, COPY_AT[("xnT", c)] + 1)
                pe.matmul(dst[:], w_state[:], xnT[:, c].rearrange("p b t -> p (b t)"),
                          start=True, stop=True).then_inc(copy_ready, 1)

            def per_token(use, lhs, rhs, n):
                dst = fill(use)
                for b in range(B):
                    mm = pe.matmul(dst[:, b * n:(b + 1) * n], lhs[:, b, :], rhs, start=(b == 0), stop=(b == B - 1),
                                   skip_group_check=True)
                mm.then_inc(misc_ready, 1)

            def heads(c):
                for b in range(B):
                    pe.matmul(fill(("qkv", c, b))[:, 0:3 * D], xnT[:, c, b, :], w_in[:],
                              start=True, stop=True).then_inc(misc_ready, 1)

            def turn_att(c):
                pe.wait_ge(att_ready, c + 1)
                turn(fill_copy(("attT", c)), att[:, c]).then_inc(copy_ready, 1)

            def gate(c):
                per_token(("gate", c, 0), xnT[:, c], w_gate[:], D)

            def proj(c):
                pe.wait_ge(copied, COPY_AT[("attT", c)] + 1)
                per_token(("proj", c, 0), attT[:, c], w_op[:], D)

            def turn_h2(c):
                pe.wait_ge(normed, CH + c + 1)
                turn(fill_copy(("h2T", c)), z_tok[:, c]).then_inc(copy_ready, 1)

            def router(c):
                pe.wait_ge(copied, COPY_AT[("h2T", c)] + 1)
                per_token(("router", c, 0), h2T[:, c], w_router[:], E)

            pe.wait_ge(consts, 11)
            pe.wait_ge(d_early, N_EARLY)
            for c in range(CH):
                turn_xn(c)
                if c == CH - 1:
                    heads(1)
                proj_px(c)
                if c == 0:
                    pe.wait_ge(ln1_b_ready, 1)
                    pe.matmul(fill(("bias", 0, 0))[:, 0:3 * D], ln1_b[:], w_in[:], start=True,
                              stop=True).then_inc(misc_ready, 1)
                    pe.wait_ge(w_in_ready, 1)
                    heads(0)
            heads(2)
            heads(3)
            turn_att(0)
            proj(0)
            turn_att(1)
            proj(1)
            turn_h2(0)
            gate(0)
            turn_att(2)
            turn_h2(1)
            proj(2)
            router(0)
            gate(1)
            gate(2)
            gate(3)
            turn_att(3)
            turn_h2(2)
            proj(3)
            router(1)
            router(2)
            turn_h2(3)
            router(3)

            def hidden(i):
                c, e = divmod(i, E)
                for f in range(FT):
                    n = FT * i + f
                    if n < 4:
                        pe.wait_ge(misc_free, len(MISC))
                        pe.wait_ge(copied, len(COPIES))
                    else:
                        pe.wait_ge(hg_ready, n - 3)
                    pe.matmul(bank[1 + n % 4][:], w1[:, (e * F + f * P):(e * F + (f + 1) * P)],
                              h2T[:, c].rearrange("p b t -> p (b t)"), start=True, stop=True).then_inc(hm_ready, 1)

            def mix_out(i):
                e = i % E
                pe.wait_ge(hg_ready, FT * (i + 1))
                if i >= 2:
                    pe.wait_ge(y_free, i - 1)
                for f in range(FT):
                    for b in range(B):
                        mm = pe.matmul(bank[5 + i % 2][:, b * D:(b + 1) * D],
                                       hg[:, (FT * i + f) % 4, b * P:(b + 1) * P], w2[:, e, f, :],
                                       start=(f == 0 and b == 0), stop=(f == FT - 1), skip_group_check=True)
                mm.then_inc(y_ready, 1)

            def turn_state(c):
                pe.wait_ge(chain_state, (c + 1) * P)
                if c:
                    pe.wait_ge(xn2T_done, c)
                turn(bank[7], state[:, c]).then_inc(sT_ready, 1)

            def turn_xn2(c):
                pe.wait_ge(normed, 2 * CH + c + 1)
                pe.wait_ge(sT_free, c + 1)
                turn(bank[7], xn2_tok[:, c]).then_inc(xn2T_ready, 1)

            pe.wait_ge(d_moe, N_MOE)
            hidden(0)
            for i in range(CH * E):
                if i + 1 < CH * E:
                    hidden(i + 1)
                mix_out(i)
                if i >= E and i % E == 1:
                    turn_state(i // E - 1)
                if i >= E and i % E == 7:
                    turn_xn2(i // E - 1)
            turn_state(CH - 1)
            turn_xn2(CH - 1)

            pe.wait_ge(xn2T_done, CH)
            pe.wait_ge(y_free, CH * E)
            pe.wait_ge(d_late, N_LATE)
            xn2T_cb = xn2T[:, 0:UNITS, :].rearrange("p u t -> p (u t)").rearrange("p (c b t) -> p c b t", c=CH, b=B)
            pe.matmul(bank[2][:, 0:B], w_p1[:], xn2T_cb[:, CH - 1, :, P - 1], start=True, stop=True).then_inc(p1_ready, 1)

            def project_quads(u, quads, parts=(0, 1), first=False):
                pe.wait_ge(xc_ready, u * 16 + 16)
                for part in parts:
                    ready, free = ((q_ready, q_free), (k_ready, k_free))[part]
                    for quad in quads:
                        if quad >= 2:
                            pe.wait_ge(free, 4 * u + quad - 1)
                        elif quad == 0 and not first:
                            pe.wait_ge(s_free, 2 * (u - 1) + part + 1)
                        for j in range(2):
                            col = (2 * quad + j) * P
                            mm = pe.matmul(PR[part + 2 * (quad % 2)][:, j * UNIT:(j + 1) * UNIT],
                                           w_qkv[:, part, col:col + P], xc[:],
                                           start=(j == 0), stop=(j == 1), skip_group_check=True)
                        mm.then_inc(ready, 1)

            def project_v(u, parts=range(4)):
                for n in parts:
                    b, half = divmod(n, 2)
                    pe.wait_ge((q_free, k_free)[b], 4 * u + 3 + half)
                    pe.matmul(VB[n][:], xc[:, b * P:(b + 1) * P], w_qkv[:, 2, half * 512:(half + 1) * 512],
                              start=True, stop=True).then_inc(v_ready, 1)

            def scores(u, m, first=False):
                if not first or m >= 2:
                    pe.wait_ge(sc_max, u * MB + m - 1)
                for i in range(4):
                    cols = slice((4 * m + i) * TB, (4 * m + i + 1) * TB)
                    mm = pe.matmul(S[m % 2][:, i * P:(i + 1) * P], qT[:, cols, :].rearrange("p t h -> p (t h)"),
                                   kT[:, cols, :].rearrange("p t h -> p (t h)"),
                                   start=(i == 0), stop=(i == 3), skip_group_check=True)
                mm.then_inc(score, 1)

            def turn_probs(u, m):
                wait_spread(pe, u, m)
                pe.wait_ge(tcopy, u * MB + m + 1)
                for i in range(4):
                    mm = pe.transpose(TR[m % 2][:, i * P:(i + 1) * P],
                                      pex[:, m % 4, i].rearrange("p t g -> p (t g)"), ident[:])
                mm.then_inc(turned, 1)

            def values(u, last=False):
                for m in range(MB):
                    if m and m + 1 < MB:
                        turn_probs(u, m + 1)
                    if m == MB - 1:
                        attention_out(u, 0, last)
                    if m == 0:
                        pe.wait_ge(v_in, u * 16 + 16)
                    pe.wait_ge(tcopy, u * MB + m + 3)
                    if m % 2 == 0:
                        pe.wait_ge(even_copied, u * OB + m // 2 + 1)
                        pe.wait_ge(odd_copied, u * OB + m // 2 + 1)
                        if not last and m < 4:
                            pe.wait_ge(v_free, 4 * u + 6 + m)
                    for i in range(4):
                        half, col = i % 2, 2 * (m % 2) + i // 2
                        mm = pe.matmul(O[m // 2 % 2][half * HD1:(half + 1) * HD1, col * P:(col + 1) * P],
                                       vb[:, 4 * m + i, :], ptT[:, m % 2, i], start=(col == 0), stop=(col == 3),
                                       skip_group_check=True)
                    mm.then_inc(pvd, 1)

            def attention_out(u, b, last=False):
                pe.wait_ge(even_copied, u * OB + 2 * b + 4)
                pe.wait_ge(odd_copied, u * OB + 2 * b + 4)
                if last:
                    pe.wait_ge(s_free, 2 * u + b + 1)
                for p in range(PAIRS):
                    mm = pe.matmul(PR[b][:, 0:D], onT[:, b * P:(b + 1) * P, p], w_out[:, p, :],
                                   start=(p == 0), stop=(p == PAIRS - 1))
                mm.then_inc(s_ready, 1)

            project_quads(0, (0, 1), first=True)
            project_quads(0, (2, 3))
            project_v(0)
            pe.wait_ge(a1_ready, 1)
            for b in range(B):
                mm = pe.matmul(bank[3][0:1, b * E:(b + 1) * E], a1[:, b:b + 1], w_p2[:],
                               start=(b == 0), stop=(b == B - 1), skip_group_check=True)
            mm.then_inc(p2_ready, 1)
            pe.wait_ge(masks_in, 32)
            pe.wait_ge(k_free, 4)
            for m in range(MB):
                scores(0, m, first=True)

            pe.wait_ge(sel_ready, 1)
            pe.wait_ge(v_free, 4)
            for b in range(B):
                pe.wait_ge(d_exp, 16 * B)
                for f in range(FT):
                    n = b * FT + f
                    if n >= 4:
                        pe.wait_ge(f_gelu, n - 3)
                    pe.matmul(FB[n % 4][:], ew[:, b, f * P:(f + 1) * P], xn2T_cb[:, :, b, :],
                              start=True, stop=True).then_inc(f_ready, 1)
            for b in range(B):
                pe.wait_ge(f_gelu, FT * (b + 1))
                if b >= 2:
                    pe.wait_ge(r_done, b - 1)
                for f in range(FT):
                    mm = pe.matmul(bank[5 + b % 2][:], ew[:, b, F + f * D:F + (f + 1) * D], hg1[:, b, f, :],
                                   start=(f == 0), stop=(f == FT - 1))
                mm.then_inc(r_ready, 1)
            pe.wait_ge(sc_max, MB)
            for b in range(B):
                pe.wait_ge(r_done, b + 1)
                for t in range(CH):
                    mm = pe.matmul(YB[b][:, t * D:(t + 1) * D], rT[:, b, t * P:(t + 1) * P], w_o[:],
                                   start=(t == 0), stop=(t == CH - 1), skip_group_check=True)
                mm.then_inc(o_ready, 1)

            pe.wait_ge(halved, 2)
            pe.sem_inc(turned, 4)
            pe.sem_inc(pvd, 2)
            pe.sem_inc(s_ready, 2)
            with pe.Fori(0, UNITS - 1) as u:
                project_quads(u + 1, (0, 1))
                project_quads(u + 1, (2, 3))
                project_v(u + 1, range(3))
                turn_probs(u, 0)
                project_v(u + 1, (3,))
                turn_probs(u, 1)
                values(u)
                for m in range(MB):
                    scores(u + 1, m)
                    if m == 1:
                        attention_out(u, 1)
            turn_probs(UNITS - 1, 0)
            turn_probs(UNITS - 1, 1)
            values(UNITS - 1, last=True)
            attention_out(UNITS - 1, 1, last=True)

        @block.scalar
        def _(act):
            def halves(t):
                return t.rearrange("p b t -> p (b t)")

            def copy_half(use, h, dst, bias=None, scale=1.0):
                c = use[1]
                if h == 0:
                    act.wait_ge(copy_ready, COPY_AT[use] + 1)
                cols = slice(h * 256, (h + 1) * 256)
                o, i = halves(dst[:, c])[:, cols], copy_bank(use)[:, cols]
                ins_ = (nc.scalar.copy(o, i) if bias is None else
                        nc.scalar.activation(o, i, ACT.Identity, bias=bias, scale=scale))
                if h:
                    ins_.then_inc(copied, 1)

            def side(t):
                for c in range(CH):
                    for h in range(2):
                        if c and t == XNT_STEP[c] + h:
                            copy_half(("xnT", c), h, xnT)
                        if c and t == PX_STEP[c] + h:
                            copy_half(("px", c), h, px, cols0[:, 0:1])
                        if t == ATTT_STEP[c] + h:
                            copy_half(("attT", c), h, attT)
                        if t == H2T_STEP[c] + h:
                            copy_half(("h2T", c), h, h2T, cols0[:, 4:5], cols0[:, 3:4])
                        if t == GATE_TANH_STEP[c] + 2 * h:
                            act.wait_ge(misc_free, MISC_AT[("gate", c, 0)] + 1)
                            cols = slice(2 * h, 2 * h + 2)
                            o = nc.scalar.activation(tg[:, c, cols], tg[:, c, cols], ACT.Tanh, scale=0.5)
                            if h:
                                o.then_inc(tg_ready, 1)
                        if t == MOE_STEP + MOE_PERIOD * E * (c + 1) + MOE_LAG + 2 * h:
                            act.wait_ge(z_ready, c + 1)
                            cols = slice(2 * h, 2 * h + 2)
                            o = nc.scalar.activation(tz[:, c, cols], x1[:, c, cols], ACT.Tanh, scale=0.5)
                            if h:
                                o.then_inc(tz_ready, 1)
                    if t == ATT_EXP_STEP[c]:
                        act.wait_ge(sc_ready, c + 1)
                        nc.scalar.activation(sc[:, c].rearrange("p a b h -> p (a b h)"),
                                             sc[:, c].rearrange("p a b h -> p (a b h)"), ACT.Exp,
                                             scale=float(HD0) ** -0.5).then_inc(pe_ready, 1)
                if t == ROUTER_EXP_STEP:
                    act.wait_ge(lg_ready, 1)
                    nc.scalar.activation(ex[:], ex[:], ACT.Exp).then_inc(ex_ready, 1)
                i, r = divmod(t - MOE_STEP, MOE_PERIOD)
                if 0 <= i < CH * E and r in (0, 2, 4, 6):
                    n, h = FT * i + r // 4, r // 2 % 2
                    if h == 0:
                        act.wait_ge(hm_ready, n + 1)
                        if n >= 4:
                            act.wait_ge(y_ready, n // 2 - 1)
                    cols = slice(h * 256, (h + 1) * 256)
                    o = nc.scalar.activation(hg[:, n % 4, cols], bank[1 + n % 4][:, cols], ACT.Gelu)
                    if h:
                        o.then_inc(hg_ready, 1)

            act.wait_ge(d_early, N_EARLY)
            for h in range(2):
                copy_half(("xnT", 0), h, xnT)
            for h in range(2):
                copy_half(("px", 0), h, px, cols0[:, 0:1])
            for t in range(T):
                act.wait_ge(chain_sum, t + 1)
                nc.scalar.activation(state[:, t // P, :, t % P], bank[0][:, 0:B], ACT.Tanh).then_inc(chain_state, 1)
                side(t)
            for t in range(T, MOE_STEP + MOE_PERIOD * E * CH + MOE_LAG + 3):
                side(t)

            act.wait_ge(p1_ready, 1)
            nc.scalar.activation(a1[:], bank[2][:, 0:B], ACT.Gelu, bias=b_p1[:]).then_inc(a1_ready, 1)

            def q_copy(u, quads):
                for quad in quads:
                    act.wait_ge(q_ready, 4 * u + quad + 1)
                    for j in range(2):
                        for h in range(2):
                            pair = 2 * quad + j
                            rows = slice(h * HD1, (h + 1) * HD1)
                            q = nc.scalar.activation(qT[0:HD1, :, 2 * pair + h], PR[2 * (quad % 2)][rows, j * UNIT:(j + 1) * UNIT],
                                                     ACT.Identity, bias=bq8[rows, pair:pair + 1],
                                                     scale=float(HD1) ** -0.5)
                    q.then_inc(q_free, 1)

            def even_copy(u, n):
                act.wait_ge(pvd, u * MB + 2 * n + 4)
                if n % 2 == 0:
                    act.wait_ge(s_ready, 2 * u + n // 2 + 1)
                for h in range(2):
                    dst, src = copy_of(n, 0, h)
                    o = nc.scalar.copy(dst, src)
                o.then_inc(even_copied, 1)

            def values(u):
                for m in range(MB):
                    act.wait_ge(turned, u * MB + m + 5)
                    act.wait_ge(pvd, u * MB + m + 1)
                    nc.scalar.copy(ptT[:, m % 2].rearrange("p k c -> p (k c)"), TR[m % 2][:]).then_inc(tcopy, 1)
                    if m >= 2 and m % 2 == 0:
                        even_copy(u, m // 2 - 1)
                even_copy(u, OB - 1)

            act.wait_ge(bc_done, 2)
            q_copy(0, range(4))

            act.wait_ge(d_exp, 16 * B)
            for b in range(B):
                for f in range(FT):
                    n = b * FT + f
                    act.wait_ge(f_ready, n + 1)
                    nc.scalar.activation(hg1[:, b, f, :], FB[n % 4][:], ACT.Gelu,
                                         bias=ew[:, b, 2 * F + f:2 * F + f + 1]).then_inc(f_gelu, 1)
            act.wait_ge(z1_ready, B)
            for c in range(CH):
                nc.scalar.activation(tz1[:, c], z1[:, c], ACT.Tanh, scale=0.5).then_inc(tz1_ready, 1)

            act.sem_inc(tcopy, 2)
            act.sem_inc(even_copied, 2)
            with act.Fori(0, UNITS - 1) as u:
                q_copy(u + 1, (0, 1))
                act.wait_ge(sc_sub, u + 1)
                nc.scalar.activation(sc1[:], sc1[:], ACT.Exp).then_inc(sc_exp, 1)
                q_copy(u + 1, (2, 3))
                values(u)
            act.wait_ge(sc_sub, UNITS)
            nc.scalar.activation(sc1[:], sc1[:], ACT.Exp).then_inc(sc_exp, 1)
            values(UNITS - 1)

        @block.vector
        def _(dve):
            count = [0]

            def own(ins_):
                count[0] += 1
                ins_.then_inc(vec, 1)
                return count[0]

            def stats_of(ln, c, src, b):
                own(nc.vector.bn_stats(stats[:, ln, c, b, :], src[:, c, b, :]))

            def aggr_of(ln, c, b, done):
                dve.wait_ge(vec, done)
                return own(nc.vector.bn_aggr(mv[:, ln, c, b, :], stats[:, ln, c, b, :]))

            def variance(ln, c, done):
                dve.wait_ge(vec, done)
                nc.vector.tensor_scalar(var[:, ln, c, :], mv[:, ln, c, :, 1], EPS, None, ALU.add).then_inc(var_ready, 1)

            def read(use):
                dve.wait_ge(misc_ready, MISC_AT[use] + 1)
                return misc_bank(use)

            def flat(t):
                return t.rearrange("p b t -> p (b t)")

            def ln_stats(ln, c, src):
                for b in range(B):
                    stats_of(ln, c, src, b)
                    yield 0.2
                base = count[0] - B
                for b in range(B):
                    last = aggr_of(ln, c, b, base + b + 1)
                    if b % 2:
                        yield 0.15
                variance(ln, c, last)
                yield 0.07

            def norm(ln, c, src, dst):
                dve.wait_ge(rstd_ready, ln * CH + c + 1)
                for b in range(B):
                    ins_ = nc.vector.tensor_scalar(dst[:, c, b, :], src[:, c, b, :], mv[:, ln, c, b, 0:1],
                                                   rstd[:, ln, c, b:b + 1], ALU.subtract, ALU.mult)
                    if b == B - 1:
                        ins_.then_inc(normed, 1)
                        if ln == 0 and c:
                            assert slot[0] < XNT_STEP[c], (c, slot)
                    yield 0.2

            slot = [-1]

            dve.wait_ge(d_x[0], 16)
            for _ in ln_stats(0, 0, x_tok):
                pass
            for _ in norm(0, 0, x_tok, xn_tok):
                pass
            dve.wait_ge(d_early, N_EARLY)

            def until(t):
                while slot[0] < t:
                    yield None

            def prep(c):
                dve.wait_ge(tz_ready, c + 1)
                dve.wait_ge(tg_ready, c + 1)
                parts = [slice(0, 2), slice(2, 4)]
                for i in parts:
                    m = own(nc.vector.scalar_tensor_tensor(out=flat(x1[:, c, i]), in0=flat(tz[:, c, i]), scalar=1.0,
                                                           in1=flat(x1[:, c, i]), op0=ALU.add, op1=ALU.mult))
                    yield 0.34
                for h, i in enumerate(parts):
                    dve.wait_ge(vec, m - 1 + h)
                    own(nc.vector.scalar_tensor_tensor(out=flat(mix[:, c, i]), in0=flat(tg[:, c, i]), scalar=1.0,
                                                       in1=flat(x1[:, c, i]), op0=ALU.add, op1=ALU.mult))
                    yield 0.34
                dve.wait_ge(sT_ready, c + 1)
                for h, i in enumerate(parts):
                    dve.wait_ge(vec, m + 1 + h)
                    own(nc.vector.scalar_tensor_tensor(out=flat(mix[:, c, i]), in0=bank[7][:, h * 256:(h + 1) * 256],
                                                       scalar=0.25, in1=flat(mix[:, c, i]), op0=ALU.mult, op1=ALU.mult))
                    yield 0.34
                dve.wait_ge(vec, m + 4)
                dve.sem_inc(sT_free, 1)
                for i in parts:
                    own(nc.vector.tensor_tensor(flat(x_tok[:, c, i]), flat(x_tok[:, c, i]), flat(mix[:, c, i]), ALU.add))
                    yield 0.34
                dve.wait_ge(vec, m + 6)
                yield from ln_stats(2, c, x_tok)
                for _ in range(4):
                    yield 0.3
                yield from norm(2, c, x_tok, xn2_tok)

            def pause(steps):
                yield from until(slot[0] + steps)

            def evac_xn2T(c):
                dve.wait_ge(xn2T_ready, c + 1)
                for h in range(2):
                    ins_ = nc.vector.tensor_copy(xn2T[:, 2 * c + h, :], bank[7][:, h * UNIT:(h + 1) * UNIT])
                    if h:
                        ins_.then_inc(xn2T_done, 1)
                    yield 0.34

            def heads(c):
                dve.wait_ge(again_ready, c + 1)
                for b in range(B):
                    nc.vector.scalar_tensor_tensor(out=qkv[:, c, b, :], in0=read(("qkv", c, b))[:, 0:3 * D],
                                                   scalar=again[:, c, b:b + 1], in1=rows0[:, 0:3 * D],
                                                   op0=ALU.mult, op1=ALU.add).then_inc(misc_free, 1)
                    yield 0.47

            def att_scores(c):
                dve.wait_ge(qk_prod, c + 1)
                n = 0
                for s in range(B):
                    last = own(nc.vector.tensor_reduce(
                        sc[:, c, s, 0:s + 1, :].rearrange("p u h -> p (u h)"),
                        prod[:, c, n:n + s + 1, :].rearrange("p u (h d) -> p (u h) d", h=H0), X, ALU.add))
                    n += s + 1
                    yield 0.13 * s + 0.2
                dve.wait_ge(vec, last)
                last = own(nc.vector.tensor_reduce(mx0[:, c], sc[:, c].rearrange("p s u h -> p s h u"), X, ALU.max))
                yield 0.34
                dve.wait_ge(vec, last)
                nc.vector.tensor_tensor(sc[:, c], sc[:, c], mx0[:, c].unsqueeze(2).broadcast_to([P, B, B, H0]),
                                        ALU.subtract).then_inc(sc_ready, 1)
                assert slot[0] <= ATT_EXP_STEP[c], (c, slot)
                yield 0.34

            def att_probs(c):
                yield from until(ATT_EXP_STEP[c] + 1)
                dve.wait_ge(pe_ready, c + 1)
                last = own(nc.vector.tensor_reduce(rs0[:, c], sc[:, c].rearrange("p s u h -> p s h u"), X, ALU.add))
                yield 0.34
                dve.wait_ge(vec, last)
                last = own(nc.vector.reciprocal(rs0[:, c], rs0[:, c]))
                yield 0.47
                dve.wait_ge(vec, last)
                nc.vector.tensor_tensor(sc[:, c], sc[:, c], rs0[:, c].unsqueeze(2).broadcast_to([P, B, B, H0]),
                                        ALU.mult).then_inc(prob_ready, 1)
                yield 0.34

            def att_values(c):
                dve.wait_ge(pv_prod, c + 1)
                n = 1
                for s in range(1, B):
                    ins_ = nc.vector.tensor_reduce(att[:, c, s, :], prod[:, c, n:n + s + 1, :].rearrange("p u e -> p e u"),
                                                   X, ALU.add)
                    n += s + 1
                    if s < B - 1:
                        yield 0.2 + 0.13 * s
                ins_.then_inc(att_ready, 1)
                assert slot[0] < ATTT_STEP[c], (c, slot)
                yield 0.6

            def gate_sum(c):
                for h in range(2):
                    i = slice(2 * h, 2 * h + 2)
                    ins_ = nc.vector.tensor_tensor(
                        tg[:, c, i], read(("gate", c, 0))[:, h * 256:(h + 1) * 256].rearrange("p (b d) -> p b d", b=2),
                        rows0[:, 4 * D:5 * D].unsqueeze(1).broadcast_to([P, 2, D]), ALU.add)
                    if h:
                        ins_.then_inc(misc_free, 1)
                        assert slot[0] < GATE_TANH_STEP[c], (c, slot)
                    yield 0.34

            def attention_sum(c):
                dve.wait_ge(xnb_ready, c + 1)
                for h in range(2):
                    i = slice(2 * h, 2 * h + 2)
                    ins_ = nc.vector.tensor_tensor(flat(x1[:, c, i]), read(("proj", c, 0))[:, h * 256:(h + 1) * 256],
                                                   flat(xnb[:, c, i]), ALU.add)
                    if h:
                        ins_.then_inc(misc_free, 1)
                    yield 0.34
                dve.wait_ge(misc_free, MISC_AT[("proj", c, 0)] + 1)
                yield from ln_stats(1, c, x1)

            def second(c):
                yield from norm(1, c, x1, z_tok)
                assert slot[0] < H2T_STEP[c], (c, slot)

            def logits(c):
                ins_ = nc.vector.tensor_copy(lg[:, c * B:(c + 1) * B, :],
                                             read(("router", c, 0))[:, 0:B * E].rearrange("p (b e) -> p b e", b=B))
                ins_.then_inc(misc_free, 1)
                yield 0.1

            def side():
                dve.wait_ge(misc_ready, 1)
                nc.vector.tensor_scalar(w_in[:], w_in[:], cols0[:, 1:2], None, ALU.mult).then_inc(w_in_ready, 1)
                yield 0.4
                own(nc.vector.tensor_tensor(rows0[:, 0:3 * D], misc_bank(("bias", 0, 0))[:, 0:3 * D], rows0[:, 0:3 * D],
                                            ALU.add))
                yield 0.47
                dve.wait_ge(vec, count[0])
                dve.sem_inc(misc_free, 1)
                for c in range(1, CH):
                    dve.wait_ge(d_x[c], 16)
                    yield from ln_stats(0, c, x_tok)
                    if c >= 2:
                        yield from norm(0, c - 1, x_tok, xn_tok)
                yield from pause(2)
                yield from norm(0, CH - 1, x_tok, xn_tok)
                yield from heads(0)
                yield from heads(1)
                yield from att_scores(0)
                yield from heads(2)
                yield from att_scores(1)
                yield from att_probs(0)
                yield from heads(3)
                yield from att_scores(2)
                yield from att_probs(1)
                yield from att_values(0)
                yield from att_scores(3)
                yield from att_probs(2)
                yield from attention_sum(0)
                yield from att_values(1)
                yield from att_probs(3)
                yield from second(0)
                yield from pause(2)
                yield from attention_sum(1)
                yield from att_values(2)
                yield from second(1)
                yield from gate_sum(0)
                yield from pause(3)
                yield from attention_sum(2)
                yield from logits(0)
                yield from gate_sum(1)
                yield from att_values(3)
                yield from second(2)
                yield from gate_sum(2)
                yield from gate_sum(3)
                yield from pause(3)
                yield from attention_sum(3)
                yield from logits(1)
                yield from pause(3)
                yield from second(3)
                yield from logits(2)
                yield from pause(8)
                yield from logits(3)
                dve.wait_ge(misc_free, MISC_AT[("router", CH - 1, 0)] + 1)

                def wide(v):
                    return v.unsqueeze(2).broadcast_to([P, CH * B, E])

                fall = falling[:].unsqueeze(1).broadcast_to([P, CH * B, E])
                m = own(nc.vector.tensor_reduce(r16[:, 0], lg[:], X, ALU.max))
                yield 0.2
                dve.wait_ge(vec, m)
                nc.vector.tensor_tensor(ex[:], lg[:], wide(r16[:, 0]), ALU.subtract).then_inc(lg_ready, 1)
                assert slot[0] <= ROUTER_EXP_STEP, slot

                yield 0.2

                def first_max(src, top, n, hot):
                    m = own(nc.vector.tensor_tensor(hot[:], src[:], wide(top), ALU.is_equal))
                    dve.wait_ge(vec, m)
                    m = own(nc.vector.tensor_tensor(hot[:], hot[:], fall, ALU.mult))
                    yield 0.2
                    dve.wait_ge(vec, m)
                    m = own(nc.vector.tensor_reduce(r16[:, n], hot[:], X, ALU.max))
                    dve.wait_ge(vec, m)
                    own(nc.vector.tensor_tensor(hot[:], hot[:], wide(r16[:, n]), ALU.is_equal))
                    yield 0.2

                yield from first_max(lg, r16[:, 0], 1, oh1)
                dve.wait_ge(vec, count[0])
                m = own(nc.vector.scalar_tensor_tensor(out=lg2[:], in0=oh1[:], scalar=NEG, in1=lg[:], op0=ALU.mult, op1=ALU.add))
                yield 0.2
                dve.wait_ge(vec, m)
                m = own(nc.vector.tensor_reduce(r16[:, 2], lg2[:], X, ALU.max))
                dve.wait_ge(vec, m)
                yield from first_max(lg2, r16[:, 2], 3, oh2)
                dve.wait_ge(vec, count[0])
                own(nc.vector.tensor_tensor(oh1[:], oh1[:], oh2[:], ALU.add))
                yield 0.2
                yield from until(ROUTER_EXP_STEP + 1)
                dve.wait_ge(ex_ready, 1)
                m = own(nc.vector.tensor_reduce(r16[:, 4], ex[:], X, ALU.add))
                yield 0.2
                dve.wait_ge(vec, m)
                m = own(nc.vector.reciprocal(r16[:, 5], r16[:, 4]))
                own(nc.vector.tensor_tensor(ex[:], ex[:], oh1[:], ALU.mult))
                yield 0.2
                dve.wait_ge(vec, m + 1)
                own(nc.vector.tensor_tensor(gates[:], ex[:], wide(r16[:, 5]), ALU.mult))
                yield 0.2

                def constants():
                    dve.wait_ge(d_late, N_LATE)
                    nc.vector.tensor_scalar(rows1[:, D:2 * D], rows1[:, D:2 * D], 0.3, None, ALU.mult).then_inc(bc_done, 1)
                    yield 0.2
                    nc.vector.tensor_scalar(bq8[:], bqk[:, 0, :], float(HD1) ** -0.5, None, ALU.mult).then_inc(bc_done, 1)
                    yield 0.2

                spare = constants()
                dve.wait_ge(vec, count[0])
                last = [None] * B
                for i in range(CH * E):
                    c, e = divmod(i, E)
                    yield from until(MOE_STEP + MOE_PERIOD * i + MOE_LAG)
                    dve.wait_ge(y_ready, i + 1)
                    for b in range(B):
                        if e:
                            dve.wait_ge(vec, last[b])
                        ins_ = nc.vector.scalar_tensor_tensor(
                            out=x1[:, c, b, :], in0=bank[5 + i % 2][:, b * D:(b + 1) * D],
                            scalar=gates[:, c * B + b, e:e + 1], in1=x1[:, c, b, :], op0=ALU.mult, op1=ALU.add)
                        last[b] = own(ins_)
                        if b < B - 1:
                            yield 0.27
                    dve.wait_ge(vec, last[B - 1])
                    dve.sem_inc(y_free, 1)
                    if e == E - 1:
                        dve.sem_inc(z_ready, 1)
                    yield 0.27
                    if c and e == 1:
                        spare = prep(c - 1)
                    for _ in range(4):
                        yield next(spare, 0.0) or 0.1
                    if c and e == 7:
                        yield from spare
                        yield from evac_xn2T(c - 1)

            work = side()
            budget = 0.0
            for t in range(T):
                if t == 0:
                    dve.wait_ge(consts, 3)
                    prev = zero_state[:]
                    dve.wait_ge(copied, 2)
                else:
                    dve.wait_ge(chain_state, t)
                    prev = state[:, (t - 1) // P, :, (t - 1) % P]
                if t and t % P == 0:
                    dve.wait_ge(copied, COPY_AT[("px", t // P)] + 1)
                nc.vector.tensor_tensor(bank[0][:, 0:B], px[:, t // P, :, t % P], prev, ALU.add).then_inc(chain_sum, 1)
                slot[0] = t
                budget = min(budget + FREE_US, FREE_US)
                while budget > 0.12:
                    spent = next(work, None)
                    if spent is None:
                        break
                    budget -= spent
            slot[0] = 10 ** 6
            for _ in work:
                pass
            for _ in prep(CH - 1):
                pass
            for _ in evac_xn2T(CH - 1):
                pass

            def k_copy(u, quad):
                dve.wait_ge(k_ready, 4 * u + quad + 1)
                if quad == 0:
                    dve.wait_ge(posb_ready, u + 1)
                for h in range(2):
                    rows = slice(h * HD1, (h + 1) * HD1)
                    pairs = slice(2 * quad, 2 * quad + 2)
                    for b in range(2):
                        k = nc.vector.tensor_tensor(
                            kT[0:HD1, b * P:(b + 1) * P, 4 * quad + h:4 * quad + h + 3:2].rearrange("p t j -> p j t"),
                            PR[1 + 2 * (quad % 2)][rows, :].rearrange("p (j b t) -> p j b t", j=2, b=2)[:, :, b, :],
                            posb[rows, pairs, :], ALU.add)
                k.then_inc(k_free, 1)

            def v_copy(u, n):
                b, half = divmod(n, 2)
                cols = slice(half * 512, (half + 1) * 512)
                dve.wait_ge(v_ready, 4 * u + n + 1)
                nc.vector.tensor_tensor(vt[:, b, cols], VB[n][:], bv_row[:, cols], ALU.add).then_inc(v_free, 1)

            def per_block(t):
                return t.unsqueeze(2).broadcast_to([P, KB, H1])

            def block_scores(u, m):
                dve.wait_ge(score, u * MB + m + 1)
                nc.vector.tensor_reduce(sc1[:, 4 * m:4 * m + 4, :],
                                        S[m % 2][:].rearrange("p (k t g) -> p k g t", k=4, t=TB), X, ALU.max
                                        ).then_inc(sc_max, 1)

            def centre(u):
                dve.wait_ge(sc_max, u * MB + MB)
                nc.vector.tensor_reduce(m1[:, 0], sc1[:], X, ALU.max).then_inc(small, 1)
                dve.wait_ge(small, u * 3 + 1)
                nc.vector.tensor_tensor(sc1[:], sc1[:], per_block(m1[:, 0]), ALU.subtract).then_inc(sc_sub, 1)

            def probs(u):
                dve.wait_ge(sc_exp, u + 1)
                nc.vector.tensor_reduce(m1[:, 1], sc1[:], X, ALU.add).then_inc(small, 1)
                dve.wait_ge(small, u * 3 + 2)
                nc.vector.reciprocal(m1[:, 2], m1[:, 1]).then_inc(small, 1)
                dve.wait_ge(small, u * 3 + 3)
                nc.vector.tensor_tensor(sc1[:], sc1[:], per_block(m1[:, 2]), ALU.mult).then_inc(prob, 1)

            def spread_vector(u, m):
                if m == VECTOR_SPREADS[0]:
                    dve.wait_ge(prob, u + 1)
                dve.wait_ge(turned, u * MB + m + 1)
                nc.vector.tensor_tensor(
                    pex[:, m % 4], sc1[:, 4 * m:4 * m + 4, :].unsqueeze(2).broadcast_to([P, 4, TB, H1]),
                    own_token[:].unsqueeze(1).unsqueeze(3).broadcast_to([P, 4, TB, H1]), ALU.mult).then_inc(spread_v, 1)

            def odd_copy(u, n):
                dve.wait_ge(pvd, u * MB + 2 * n + 4)
                if n % 2 == 0:
                    dve.wait_ge(s_ready, 2 * u + n // 2 + 1)
                for h in range(2):
                    dst, src = copy_of(n, 1, h)
                    o = nc.vector.tensor_copy(dst, src)
                o.then_inc(odd_copied, 1)

            def output(u, b):
                dve.wait_ge(s_ready, 2 * u + b + 3)
                nc.vector.tensor_tensor(tile_of(s_all, 2 * u + b), PR[b][:, 0:D], rows1[:, 0:D],
                                        ALU.add).then_inc(s_free, 1)

            for quad in range(4):
                k_copy(0, quad)
            for n in range(4):
                v_copy(0, n)

            dve.wait_ge(p2_ready, 1)
            lgs, eq = rt[:, 0], rt[:, 1]
            m = own(nc.vector.tensor_tensor(lgs, bank[3][0:1, 0:B * E].rearrange("p (b e) -> p b e", b=B),
                                            b_p2[:].unsqueeze(1).broadcast_to([1, B, E]), ALU.add))
            dve.wait_ge(vec, m)
            m = own(nc.vector.tensor_reduce(rt[:, 2, :, 0], lgs, X, ALU.max))
            dve.wait_ge(vec, m)
            m = own(nc.vector.tensor_tensor(eq, lgs, rt[:, 2, :, 0:1].broadcast_to([1, B, E]), ALU.is_equal))
            dve.wait_ge(vec, m)
            m = own(nc.vector.tensor_tensor(eq, eq, falling[0:1, :].unsqueeze(1).broadcast_to([1, B, E]), ALU.mult))
            dve.wait_ge(vec, m)
            m = own(nc.vector.tensor_reduce(rt[:, 3, :, 0], eq, X, ALU.max))
            dve.wait_ge(vec, m)
            nc.vector.tensor_scalar(sel[:], rt[:, 3, :, 0], -1.0, float(E), ALU.mult, ALU.add).then_inc(sel_ready, 1)

            for m in range(MB):
                block_scores(0, m)
            centre(0)

            dve.wait_ge(d_exp, 16 * B)
            for b in range(B):
                dve.wait_ge(r_ready, b + 1)
                nc.vector.tensor_scalar(rT[:, b, :], bank[5 + b % 2][:], ew[:, b, 2 * F + 2:2 * F + 3], None,
                                        ALU.add).then_inc(r_done, 1)
            dve.wait_ge(xnb2_ready, CH)
            for b in range(B):
                dve.wait_ge(o_ready, b + 1)
                nc.vector.scalar_tensor_tensor(out=z1[:, :, b, :], in0=YB[b][:].rearrange("p (c d) -> p c d", c=CH),
                                               scalar=0.3, in1=xnb2[:, :, b, :], op0=ALU.mult, op1=ALU.add).then_inc(z1_ready, 1)
            for c in range(CH):
                dve.wait_ge(tz1_ready, c + 1)
                nc.vector.scalar_tensor_tensor(out=flat(z1[:, c]), in0=flat(tz1[:, c]), scalar=1.0, in1=flat(z1[:, c]),
                                               op0=ALU.add, op1=ALU.mult)

            dve.wait_ge(halved, 2)
            dve.sem_inc(s_free, 2)
            dve.sem_inc(odd_copied, 2)

            def unit(u, last=False):
                if not last:
                    k_copy(u + 1, 0)
                    k_copy(u + 1, 1)
                probs(u)
                if not last:
                    k_copy(u + 1, 2)
                    k_copy(u + 1, 3)
                    for n in range(4):
                        if n == 0:
                            dve.wait_ge(v_out, u * 16 + 16)
                        v_copy(u + 1, n)
                spread_vector(u, 4)
                odd_copy(u, 0)
                spread_vector(u, 6)
                for n in range(1, OB):
                    odd_copy(u, n)
                output(u, 0)
                if last:
                    output(u, 1)
                    return
                for m in range(MB):
                    if m == 0:
                        wait_spread(dve, u, VECTOR_SPREADS[-1])
                        wait_spread(dve, u, MB - 1)
                    block_scores(u + 1, m)
                    if m == 1:
                        output(u, 1)
                centre(u + 1)

            with dve.Fori(0, UNITS - 1) as u:
                unit(u)
            unit(UNITS - 1, last=True)


def positions():
    p = np.arange(T, dtype=np.float32)[:, None]
    div = np.exp(np.arange(0, HD1, 2, dtype=np.float32) * np.float32(-(np.log(10000.0) / HD1))).astype(np.float32)
    ang = (p * div).astype(np.float32)
    pe = np.zeros((T, HD1), np.float32)
    pe[:, 0::2] = np.sin(ang)
    pe[:, 1::2] = np.cos(ang)
    both = np.concatenate([pe.T, pe.T], 0).reshape(P, CH, P)
    return np.concatenate([both.repeat(2, 1), both[:, :1]], 1)


def block_masks():
    own = np.zeros((HD1, TB, H1), np.float32)
    own[np.arange(TB), np.arange(TB)] = 1.0
    others = np.zeros_like(own)
    others[:TB] = np.where(own[:TB] == 1.0, 0.0, MASKED)
    return own.reshape(HD1, P), others.reshape(HD1, P)


def kernel(**inputs):
    import concourse.bacc as bacc
    from concourse.bass_utils import run_bass_kernel_spmd

    a = {k: np.asarray(v) for k, v in inputs.items()}

    def rows(*vs):
        return np.broadcast_to(np.concatenate(vs)[None, :], (P, sum(v.size for v in vs)))

    wq = a["L1_attn_w_qkv"].reshape(D, H1, 3, HD1).transpose(0, 2, 1, 3).reshape(D, 3, H1 * HD1)
    bq = a["L1_attn_b_qkv"].reshape(PAIRS, 2, 3, HD1)
    mask_q, mask_k = block_masks()
    experts = np.concatenate([
        a["L1_ffn_W1"],
        a["L1_ffn_W2"].reshape(E, FT, P, D).transpose(0, 2, 1, 3).reshape(E, P, FT * D),
        a["L1_ffn_b1"].reshape(E, FT, P).transpose(0, 2, 1),
        a["L1_ffn_b2"][:, :, None]], axis=2)
    data = {
        "x": a["L0_attn_x"],
        "w_state": a["L0_attn_W_state"].T, "w_gate": a["L0_attn_W_gate"].T,
        "w_in": a["L0_ffn_in_proj_w"].T, "w_op": a["L0_ffn_out_proj_w"].T,
        "w_router": a["L0_ffn_router_w"].T,
        "w1": a["L0_ffn_w1"].transpose(1, 0, 2).reshape(D, E * F),
        "w2": a["L0_ffn_w2"].reshape(E, FT, P, D).transpose(2, 0, 1, 3),
        "cols0": np.stack([a["L0_attn_b_state"], a["L0_ffn_ln1_w"], a["L0_ffn_ln1_b"], a["L0_ffn_ln2_w"],
                           a["L0_ffn_ln2_b"]], 1),
        "rows0": rows(a["L0_ffn_in_proj_b"], a["L0_ffn_out_proj_b"], a["L0_attn_b_gate"]),
        "w_qkv": wq, "bqk": bq[:, :, 0:2].transpose(1, 3, 2, 0).reshape(P, 2, PAIRS),
        "bv_row": rows(bq[:, :, 2].reshape(-1)), "own_token": block_masks()[0][:TB].reshape(TB, P).T,
        "mask_q": mask_q, "mask_k": mask_k,
        "w_out": a["L1_attn_w_out"].reshape(PAIRS, P, D).transpose(1, 0, 2),
        "w_p1": a["L1_ffn_Wp1"], "w_p2": a["L1_ffn_Wp2"], "b_p1": a["L1_ffn_bp1"][:, None],
        "b_p2": a["L1_ffn_bp2"][None, :], "w_o": a["L1_ffn_Wo"],
        "rows1": rows(a["L1_attn_b_out"], a["L1_ffn_bo"]),
        "experts": experts, "pos": positions(),
    }
    nc = bacc.Bacc("TRN2", target_bir_lowering=False, num_devices=1)
    arrays, ins = {}, {}
    for name, v in data.items():
        v = np.ascontiguousarray(v)
        arrays[f"in_{name}"] = v
        ins[name] = nc.dram_tensor(f"in_{name}", v.shape, mybir.dt.from_np(v.dtype), kind="ExternalInput").ap()
    out = nc.dram_tensor("out_x", (UNITS, 2, P, D), F32, kind="ExternalOutput").ap()
    build(nc, ins, out)
    r = run_bass_kernel_spmd(nc, [arrays], core_ids=[0])
    return r.results[0]["out_x"].reshape(CH, B, P, D).transpose(1, 0, 2, 3).reshape(B, T, D)
```

```python
from contextlib import ExitStack

import numpy as np

import concourse.bass as bass
from concourse import mybir

ALU = mybir.AluOpType
ACT = mybir.ActivationFunctionType
F32 = mybir.dt.float32
F32R = mybir.dt.float32r
I32 = mybir.dt.int32
X = mybir.AxisListType.X

P = 128
B, T, D = 4, 512, 128
CH = T // P
BD = B * D
H0, HD0 = 16, 8
E = 8
F = 256
FT = F // P
H1, HD1 = 16, 64
PAIRS = H1 // 2
UNIT = 256
UNITS = B * T // UNIT
TB = P // H1
KB = UNIT // TB
MB = KB // 4
VECTOR_SPREADS = (4, 6)
OB = MB // 2
EPS = 1e-5
NEG = -3.0e38
MASKED = -1.0e30

XNT_STEP = (0, 19, 28, 37)
PX_STEP = (0, 27, 35, 46)
ATT_EXP_STEP = (53, 69, 88, 105)
ATTT_STEP = (98, 120, 143, 168)
H2T_STEP = (134, 151, 174, 194)
ROUTER_EXP_STEP = 204
MOE_STEP = 207
MOE_PERIOD = 9
GATE_TANH_STEP = [MOE_STEP + MOE_PERIOD * c + 1 for c in range(CH)]
MOE_LAG = 20
FREE_US = 0.3

COPY_BANKS = 2
COPIES = ([(kind, c) for c in range(CH) for kind in ("xnT", "px")]
          + [("attT", 0), ("attT", 1), ("h2T", 0), ("attT", 2), ("h2T", 1), ("attT", 3), ("h2T", 2), ("h2T", 3)])
COPY_AT = {use: n for n, use in enumerate(COPIES)}
MISC_BANKS = 4
MISC = ([("bias", 0, 0)] + [("qkv", 0, b) for b in range(B)] + [("qkv", 1, b) for b in range(B)]
        + [("qkv", 2, b) for b in range(B)] + [("qkv", 3, b) for b in range(B)]
        + [("proj", 0, 0), ("proj", 1, 0), ("gate", 0, 0), ("proj", 2, 0), ("router", 0, 0), ("gate", 1, 0),
           ("gate", 2, 0), ("gate", 3, 0), ("proj", 3, 0), ("router", 1, 0), ("router", 2, 0), ("router", 3, 0)])
MISC_AT = {use: n for n, use in enumerate(MISC)}


def build(nc, ins, out):
    with ExitStack() as ctx:
        def sb(name, *shape, dt=F32):
            return ctx.enter_context(nc.sbuf_tensor(name, list(shape), dt))

        def sem(name):
            return ctx.enter_context(nc.semaphore(name))

        bank = [ctx.enter_context(nc.psum_tensor(f"bank{i}", [P, 512], F32)) for i in range(8)]

        first = ExitStack()

        def first_sb(name, *shape):
            return first.enter_context(nc.sbuf_tensor(name, list(shape), F32))

        w_qkv = first_sb("w_qkv", P, 3, H1 * HD1)
        xnT = first_sb("xnT", P, CH, B, P)
        sc = first_sb("sc", P, CH, B, B, H0)
        w_in = first_sb("w_in", P, 3 * D)
        rows0 = first_sb("rows0", P, 5 * D)
        first.close()
        w_lo = sb("w_lo", P, 3, H1 * HD1, dt=F32R)
        w_hi = sb("w_hi", P, 3, H1 * HD1, dt=F32R)
        xc_hi = sb("xc_hi", P, UNIT, dt=F32R)
        xc_lo = sb("xc_lo", P, UNIT, dt=F32R)
        first_words = 3 * H1 * HD1 + CH * BD + CH * B * B * H0 + 3 * D + 5 * D
        sb("rest_of_first", P, first_words - 2 * 3 * H1 * HD1 - 2 * UNIT)

        ident = sb("ident", P, P)
        w_state = sb("w_state", P, D)
        w_gate = sb("w_gate", P, D)
        w_op = sb("w_op", P, D)
        w_router = sb("w_router", P, E)
        w1 = sb("w1", P, E * F)
        w2 = sb("w2", P, E, FT, D)
        cols0 = sb("cols0", P, 5)
        bqk = sb("bqk", P, 2, PAIRS)
        bq8 = sb("bq8", P, PAIRS)
        bv_row = sb("bv_row", P, H1 * HD1)
        w_out = sb("w_out", P, PAIRS, D)
        own_token = sb("own_token", P, TB)
        w_p1 = sb("w_p1", P, P)
        w_p2 = sb("w_p2", P, E)
        b_p1 = sb("b_p1", P, 1)
        b_p2 = sb("b_p2", 1, E)
        w_o = sb("w_o", P, D)
        rows1 = sb("rows1", P, 2 * D)
        pos = sb("pos", P, UNITS + 1, P)
        falling = sb("falling", P, E)
        exps = sb("exps", P, B)

        def over(tensor, shape, first=0):
            flat = tensor[:]
            while len(flat.shape) > 2:
                free = "abcd"[:len(flat.shape) - 1]
                flat = flat.rearrange(f"p {' '.join(free)} -> p {' '.join(free[:-2])} ({free[-2]} {free[-1]})")
            names = "abcd"[:len(shape)]
            flat = flat[:, first:first + int(np.prod(shape))]
            return flat.rearrange(f"p ({' '.join(names)}) -> p {' '.join(names)}", **dict(zip(names, shape)))

        x_tok = sb("x_tok", P, CH, B, D)
        xn_tok = sb("xn_tok", P, CH, B, D)
        px = sb("px", P, CH, B, P)
        state = sb("state", P, CH, B, P)
        zero_state = sb("zero_state", P, B)
        stats = sb("stats", P, 3, CH, B, 6)
        mv = sb("mv", P, 3, CH, B, 2)
        var = sb("var", P, 3, CH, B)
        rstd = sb("rstd", P, 3, CH, B)
        again = sb("again", P, CH, B)
        ln1_b = sb("ln1_b", P, P)
        z_tok = sb("z_tok", P, CH, B, D)
        hnT = sb("hnT", P, CH, B, P)
        heads_words = sb("heads_words", P, CH * B * 3 * D + CH * 10 * D)
        qkv = heads_words[:, 0:CH * B * 3 * D].rearrange("p (c b n) -> p c b n", c=CH, b=B)
        prod = heads_words[:, CH * B * 3 * D:].rearrange("p (c s n) -> p c s n", c=CH, s=10)
        mx0 = sb("mx0", P, CH, B, H0)
        rs0 = sb("rs0", P, CH, B, H0)
        sums_words = sb("sums_words", P, 2 * CH * BD)
        att = sums_words[:, 0:CH * BD].rearrange("p (c b d) -> p c b d", c=CH, b=B)
        attT = over(heads_words, (CH, B, P))
        tz = attT
        tg = over(heads_words, (CH, B, D), CH * BD)
        mix = tg
        hg = over(heads_words, (4, BD), 2 * CH * BD)
        xnb = sums_words[:, CH * BD:].rearrange("p (c b d) -> p c b d", c=CH, b=B)
        x1 = sb("x1", P, CH, B, D)
        h2T = hnT
        lg = sb("lg", P, CH * B, E)
        lg2 = sb("lg2", P, CH * B, E)
        oh1 = sb("oh1", P, CH * B, E)
        oh2 = sb("oh2", P, CH * B, E)
        ex = sb("ex", P, CH * B, E)
        gates = sb("gates", P, CH * B, E)
        r16 = sb("r16", P, 8, CH * B)

        xn2_tok = over(xnT, (CH, B, D))
        xn2T = sb("xn2T", P, UNITS + 1, UNIT)
        a1 = sb("a1", P, B)
        rt = sb("rt", 1, 6, B, E)
        sel = sb("sel", 1, B, dt=I32)
        ew = sb("ew", P, B, 2 * F + 3)
        hg1 = over(heads_words, (B, FT, T))
        rT = over(heads_words, (B, T), B * FT * T)
        xnb2 = over(px, (CH, B, D))
        z1 = over(x1, (CH, B, D))
        tz1 = over(state, (CH, B, D))
        s_all = over(hnT, (CH, B, D))

        d_x = [sem(f"x_loaded{c}") for c in range(CH)]
        d_early = sem("early_weights_loaded")
        d_moe = sem("moe_weights_loaded")
        d_late = sem("late_weights_loaded")
        d_exp = [sem(f"chosen_expert_loaded{b}") for b in range(B)]
        d_out = sem("output_stored")
        ident_zero = sem("ident_zeroed")
        consts = sem("constants_ready")
        vec = sem("vector_step")
        pool = sem("pool_step")
        var_ready = sem("variance_ready")
        rstd_ready = sem("deviation_ready")
        again_ready = sem("second_norm_ready")
        ln1_b_ready = sem("ln1_shift_spread")
        w_in_ready = sem("w_in_scaled")
        normed = sem("tokens_normed")
        copy_ready = sem("copy_psum_ready")
        copied = sem("copy_psum_read")
        misc_ready = sem("misc_psum_ready")
        misc_free = sem("misc_psum_free")
        chain_sum = sem("chain_sum")
        chain_state = sem("chain_state")
        qk_prod = sem("qk_products_ready")
        sc_ready = sem("scores_centred")
        pe_ready = sem("attention_exp_ready")
        prob_ready = sem("attention_probs_ready")
        pv_prod = sem("pv_products_ready")
        att_ready = sem("attention_ready")
        xnb_ready = sem("xn_plus_bias_ready")
        lg_ready = sem("logits_centred")
        ex_ready = sem("router_exp_ready")
        tg_ready = sem("gate_tanh_ready")
        hm_ready = sem("expert_hidden_ready")
        hg_ready = sem("expert_gelu_ready")
        y_ready = sem("expert_out_ready")
        y_free = sem("expert_out_read")
        z_ready = sem("block_sum_ready")
        tz_ready = sem("block_tanh_ready")
        sT_ready = sem("state_turned")
        sT_free = sem("state_turned_read")
        xn2T_ready = sem("xn2_turned")
        xn2T_done = sem("xn2T_written")
        halved = sem("w_out_halved")
        bc_done = sem("scaled_biases_ready")
        p1_ready = sem("policy_hidden_ready")
        a1_ready = sem("policy_gelu_ready")
        p2_ready = sem("policy_logits_ready")
        sel_ready = sem("expert_chosen")
        f_ready = sem("ffn1_hidden_ready")
        f_gelu = sem("ffn1_gelu_ready")
        r_ready = sem("ffn1_reasoned_ready")
        r_done = sem("ffn1_reasoned_read")
        o_ready = sem("ffn1_out_ready")
        z1_ready = sem("ffn1_sum_ready")
        tz1_ready = sem("ffn1_tanh_ready")
        xnb2_ready = sem("xn2_plus_bias_ready")

        qT = over(heads_words, (UNIT, H1), CH * B * 3 * D)
        kT = over(sums_words, (UNIT, H1))
        xc = sb("xc", P, UNIT)
        posb = sb("posb", P, PAIRS, P)
        vt = over(xn_tok, (2, H1 * HD1))
        vb = over(w2, (KB, HD1))
        sc1 = over(heads_words, (KB, H1), CH * B * 3 * D + UNIT * H1)
        m1 = over(heads_words, (3, KB), CH * B * 3 * D + UNIT * H1 + KB * H1)
        pex = over(w1, (4, 4, P)).rearrange("p r k (t g) -> p r k t g", t=TB)
        ptT = over(heads_words, (2, 4, P))
        onT = over(z_tok, (UNIT, PAIRS))
        v_dram = nc.dram_tensor("v_by_token", (2, P, H1 * HD1), F32, kind="Internal").ap()
        S, TR, O, PR = bank[0:2], bank[2:4], [bank[4], bank[7]], bank[5:7]
        FB = [bank[2], bank[3], bank[4], bank[7]]
        HALVES = [slice(0, KB // 2), slice(KB // 2, KB)]
        YB = [bank[0], bank[1], bank[7], bank[4]]
        Q_BANKS = [bank[5], bank[2], bank[4], bank[5]]
        K_BANKS = [bank[6], bank[3], bank[7], bank[6]]
        V_BANKS = [bank[0], bank[1], bank[6], bank[5]]
        w_split = sem("w_qkv_split")
        halves_ready = sem("unit_split")
        empty_unit = sem("empty_unit_ready")
        masks_in = sem("masks_loaded")
        xc_ready = sem("unit_staged")
        posb_ready = sem("positions_ready")
        q_ready = sem("q_projected")
        q_free = sem("q_copied")
        k_ready = sem("k_projected")
        k_free = sem("k_copied")
        v_ready = sem("v_projected")
        v_free = sem("v_copied")
        v_out = sem("v_stored")
        v_in = sem("v_by_block_loaded")
        vb_free = sem("v_by_block_used")
        v_made = sem("v_of_next_unit_made")
        score = sem("scores_ready")
        sc_max = sem("block_scores_ready")
        sc_sub = sem("unit_scores_centred")
        sc_exp = sem("unit_exp_ready")
        prob = sem("unit_probs_ready")
        small = sem("softmax_step")
        xc_hi_made = sem("unit_high_half_ready")
        spread_v = sem("vector_spread_probs")
        spread_p = sem("gpsimd_spread_probs")
        turned = sem("probs_turned")
        tcopy = sem("turned_probs_copied")
        pvd = sem("pv_ready")
        even_copied = sem("values_of_even_blocks_copied")
        odd_copied = sem("values_of_odd_blocks_copied")
        s_ready = sem("attention_output_ready")
        s_free = sem("attention_output_read")
        gated = sem("output_step")
        y_done = sem("tile_output_ready")

        def tile_of(t, n):
            return t[:].rearrange("p c b d -> p (c b) d")[:, bass.ds(n, 1), :].rearrange("p a d -> p (a d)")

        def wait_spread(engine, u, m):
            if m in VECTOR_SPREADS:
                engine.wait_ge(spread_v, len(VECTOR_SPREADS) * u + VECTOR_SPREADS.index(m) + 1)
            else:
                others = [n for n in range(MB) if n not in VECTOR_SPREADS]
                engine.wait_ge(spread_p, len(others) * u + others.index(m) + 1)

        def copy_of(n, half, h):
            src = O[n % 2][half * HD1:(half + 1) * HD1, :].rearrange("p (k t q h) -> p k t q h", k=4, t=TB, h=2)
            dst = onT[h * HD1:(h + 1) * HD1, n * 64:(n + 1) * 64, :].rearrange("p (k j t) q -> p k j (t q)", k=4, j=2)
            return dst[:, :, half, :], src[:, :, :, :, h].rearrange("p k t q -> p k (t q)")

        block = ctx.enter_context(nc.Block())

        def misc_bank(use):
            return bank[3 + MISC_AT[use] % MISC_BANKS]

        def turn_bank(c):
            return bank[7] if c < CH - 1 else bank[1]

        def copy_bank(use):
            return bank[1 + COPY_AT[use] % COPY_BANKS]

        @block.sync
        def _(sp):
            xs = ins["x"].rearrange("b (c p) d -> p c b d", p=P)
            for c in range(CH):
                sp.dma_start(x_tok[:, c], xs[:, c]).then_inc(d_x[c], 16)
                if c == 0:
                    early = [(w_state[:], "w_state"), (cols0[:], "cols0"), (w_in[:], "w_in"),
                             (rows0[:], "rows0"), (w_op[:], "w_op"), (w_router[:], "w_router"),
                             (w_gate[:], "w_gate")]
                    for dst, name in early:
                        sp.dma_start(dst, ins[name]).then_inc(d_early, 16)
            sp.dma_start(w1[:], ins["w1"]).then_inc(d_moe, 16)
            sp.dma_start(w2[:], ins["w2"]).then_inc(d_moe, 16)
            late = [(w_out[:], "w_out"), (bqk[:], "bqk"), (rows1[:], "rows1"), (w_p1[:], "w_p1"),
                    (w_p2[:], "w_p2"), (b_p1[:], "b_p1"), (b_p2[:], "b_p2"), (w_o[:], "w_o"),
                    (w_qkv[:], "w_qkv"), (pos[:], "pos"), (bv_row[:], "bv_row"), (own_token[:], "own_token")]
            for dst, name in late:
                sp.dma_start(dst, ins[name]).then_inc(d_late, 16)
            sp.wait_ge(hg_ready, FT * CH * E)
            wide = [HD1, UNIT // TB, TB * H1]
            for dst, name in ((qT, "mask_q"), (kT, "mask_k")):
                sp.dma_start(dst[HD1:P].rearrange("p (k t) h -> p k (t h)", t=TB),
                             ins[name].unsqueeze(1).broadcast_to(wide)).then_inc(masks_in, 16)
            sp.wait_ge(empty_unit, 1)
            sp.wait_ge(xn2T_done, 1)
            sp.dma_start(xc[:], xn2T[:, 0, :]).then_inc(xc_ready, 16)

            def v_store():
                sp.dma_start(v_dram.rearrange("b p n -> p b n"), vt[:]).then_inc(v_out, 16)

            def v_load():
                sp.dma_start(vb[:], v_dram.rearrange("b (k t) (g d) -> (t g) (b k) d", t=TB, d=HD1)
                             ).then_inc(v_in, 16)

            def y_store(u):
                sp.dma_start(out[bass.ds(u, 1), :, :, :].rearrange("u b p d -> p (u b) d"),
                             s_all[:].rearrange("p c b d -> p (c b) d")[:, bass.ds(2 * u, 2), :]).then_inc(d_out, 16)

            sp.wait_ge(sel_ready, 1)
            for b in range(B):
                e = sp.value_load(sel[0:1, b:b + 1], min_val=0, max_val=E - 1)
                sp.dma_start(ew[:, b, :], ins["experts"][bass.ds(e, 1), :, :].rearrange("e p n -> (e p) n")
                             ).then_inc(d_exp[b], 16)
            sp.wait_ge(v_ready, 4)
            sp.wait_ge(xn2T_done, CH)
            sp.dma_start(xc[:], xn2T[:, 1, :]).then_inc(xc_ready, 16)
            sp.wait_ge(v_free, 4)
            v_store()
            sp.wait_ge(v_out, 16)
            v_load()
            with sp.Fori(0, UNITS - 1) as u:
                sp.wait_ge(v_free, 4 * u + 8)
                sp.sem_inc(v_made, 1)
                sp.wait_ge(v_in, u * 16 + 16)
                v_store()
                sp.dma_start(xc[:], xn2T[:, bass.ds(u + 2, 1), :].rearrange("p a t -> p (a t)")
                             ).then_inc(xc_ready, 16)
                sp.wait_ge(v_out, u * 16 + 32)
                sp.wait_ge(pvd, u * MB + MB + 2)
                sp.sem_inc(vb_free, 1)
                v_load()
                sp.wait_ge(y_done, 2 * u + 2)
                y_store(u)
            sp.wait_ge(v_in, 16 * UNITS)
            sp.wait_ge(xc_ready, 16 * (UNITS + 1))
            sp.wait_ge(y_done, 2 * UNITS)
            y_store(UNITS - 1)
            sp.wait_ge(d_out, 16 * UNITS)

        N_EARLY, N_MOE, N_LATE = 7 * 16, 2 * 16, 12 * 16

        @block.gpsimd
        def _(gp):
            nc.gpsimd.memset(ident[:], 0.0).then_inc(ident_zero, 1)
            nc.gpsimd.memset(exps[:], -0.5).then_inc(consts, 1)
            gp.wait_ge(ident_zero, 1)
            nc.gpsimd.affine_select(out=ident[:], in_=ident[:], compare_op=ALU.not_equal, fill=1.0, base=0,
                                    pattern=[[-1, P]], channel_multiplier=1).then_inc(consts, 1)
            nc.gpsimd.memset(zero_state[:], 0.0).then_inc(consts, 1)
            for e in range(E):
                nc.gpsimd.memset(falling[:, e:e + 1], float(E - e)).then_inc(consts, 1)
            gp.wait_ge(consts, 3)

            steps = [0]

            def own(ins_):
                steps[0] += 1
                ins_.then_inc(pool, 1)
                gp.wait_ge(pool, steps[0])

            def deviation(ln, c):
                gp.wait_ge(var_ready, ln * CH + c + 1)
                nc.gpsimd.tensor_tensor(rstd[:, ln, c, :], var[:, ln, c, :], exps[:], ALU.pow).then_inc(rstd_ready, 1)

            def second_norm(c):
                gp.wait_ge(rstd_ready, c + 1)
                own(nc.gpsimd.tensor_tensor(again[:, c, :], mv[:, 0, c, :, 1], rstd[:, 0, c, :], ALU.mult))
                own(nc.gpsimd.tensor_tensor(again[:, c, :], again[:, c, :], rstd[:, 0, c, :], ALU.mult))
                own(nc.gpsimd.tensor_scalar(again[:, c, :], again[:, c, :], EPS, None, ALU.add))
                nc.gpsimd.tensor_tensor(again[:, c, :], again[:, c, :], exps[:], ALU.pow).then_inc(again_ready, 1)

            deviation(0, 0)
            gp.wait_ge(d_early, N_EARLY)
            nc.gpsimd.tensor_copy(ln1_b[:], cols0[:, 2:3].broadcast_to([P, P])).then_inc(ln1_b_ready, 1)
            nc.gpsimd.memset(sc[:], MASKED).then_inc(consts, 1)
            second_norm(0)
            for c in range(1, CH):
                deviation(0, c)
                if c >= 2:
                    second_norm(c - 1)
            second_norm(CH - 1)

            def qk_products(c):
                gp.wait_ge(misc_free, MISC_AT[("qkv", c, B - 1)] + 1)
                n = 0
                for s in range(B):
                    q = qkv[:, c, s:s + 1, 0:D].broadcast_to([P, s + 1, D])
                    ins_ = nc.gpsimd.tensor_tensor(prod[:, c, n:n + s + 1, :], q, qkv[:, c, 0:s + 1, D:2 * D], ALU.mult)
                    n += s + 1
                ins_.then_inc(qk_prod, 1)

            def pv_products(c):
                gp.wait_ge(prob_ready, c + 1)
                n = 0
                for s in range(B):
                    for u in range(s + 1):
                        prb = sc[:, c, s, u, :].unsqueeze(2).broadcast_to([P, H0, HD0])
                        dst = att[:, c, 0, :] if s == 0 else prod[:, c, n, :]
                        ins_ = nc.gpsimd.tensor_tensor(
                            dst.rearrange("p (h d) -> p h d", h=H0), prb,
                            qkv[:, c, u, 2 * D:3 * D].rearrange("p (h d) -> p h d", h=H0), ALU.mult)
                        n += 1
                ins_.then_inc(pv_prod, 1)

            def plus_bias(c):
                gp.wait_ge(normed, c + 1)
                nc.gpsimd.tensor_tensor(
                    xnb[:, c], xn_tok[:, c], rows0[:, 3 * D:4 * D].unsqueeze(1).broadcast_to([P, B, D]),
                    ALU.add).then_inc(xnb_ready, 1)

            plus_bias(0)
            plus_bias(1)
            plus_bias(2)
            qk_products(0)
            plus_bias(3)
            qk_products(1)
            qk_products(2)
            pv_products(0)
            qk_products(3)
            pv_products(1)
            pv_products(2)
            deviation(1, 0)
            pv_products(3)
            deviation(1, 1)
            deviation(1, 2)
            deviation(1, 3)
            gp.wait_ge(d_late, N_LATE)
            nc.gpsimd.tensor_scalar(w_out[:], w_out[:], 0.5, None, ALU.mult).then_inc(halved, 1)
            nc.gpsimd.tensor_scalar(rows1[:, 0:D], rows1[:, 0:D], 0.5, None, ALU.mult).then_inc(halved, 1)
            def positions_of(chunk):
                nc.gpsimd.tensor_tensor(posb[:], chunk.broadcast_to([P, PAIRS, P]),
                                        bqk[:, 1, :].unsqueeze(2).broadcast_to([P, PAIRS, P]),
                                        ALU.add).then_inc(posb_ready, 1)

            positions_of(pos[:, 0:1, :])
            nc.gpsimd.memset(xn2T[:, UNITS, :], 0.0).then_inc(empty_unit, 1)
            for c in range(CH):
                deviation(2, c)
                gp.wait_ge(normed, 2 * CH + c + 1)
                if c == 0:
                    gp.wait_ge(bc_done, 1)
                nc.gpsimd.tensor_tensor(
                    xnb2[:, c], xn2_tok[:, c], rows1[:, D:2 * D].unsqueeze(1).broadcast_to([P, B, D]),
                    ALU.add).then_inc(xnb2_ready, 1)

            def spread_pool(u, m):
                gp.wait_ge(turned, u * MB + m + 1)
                nc.gpsimd.tensor_tensor(
                    pex[:, m % 4], sc1[:, 4 * m:4 * m + 4, :].unsqueeze(2).broadcast_to([P, 4, TB, H1]),
                    own_token[:].unsqueeze(1).unsqueeze(3).broadcast_to([P, 4, TB, H1]), ALU.mult).then_inc(spread_p, 1)

            def output(u, b):
                s = tile_of(s_all, 2 * u + b)
                gp.wait_ge(s_free, 2 * u + b + 3)
                nc.gpsimd.tensor_tensor(s, s, tile_of(z1, 2 * u + b), ALU.mult).then_inc(gated, 1)
                gp.wait_ge(gated, 2 * u + b + 1)
                nc.gpsimd.tensor_tensor(s, s, tile_of(x_tok, 2 * u + b), ALU.add).then_inc(y_done, 1)

            gp.wait_ge(k_free, 4)
            positions_of(pos[:, 1:2, :])
            with gp.Fori(0, UNITS - 1) as u:
                gp.wait_ge(prob, 2 * u + 1)
                for m in range(4):
                    spread_pool(u, m)
                gp.wait_ge(prob, 2 * u + 2)
                gp.wait_ge(k_free, 4 * u + 8)
                positions_of(pos[:, bass.ds(u + 2, 1), :])
                spread_pool(u, 5)
                spread_pool(u, 7)
                output(u, 0)
                output(u, 1)
            gp.wait_ge(prob, 2 * UNITS)
            for m in range(MB):
                if m not in VECTOR_SPREADS:
                    spread_pool(UNITS - 1, m)
            for b in range(2):
                output(UNITS - 1, b)

        @block.tensor
        def _(pe):
            def fill(use):
                n = MISC_AT[use]
                if n >= MISC_BANKS:
                    pe.wait_ge(misc_free, n - MISC_BANKS + 1)
                return misc_bank(use)

            def turn(dst, src):
                for b in range(B):
                    mm = pe.transpose(dst[:, b * P:(b + 1) * P], src[:, b, :], ident[:])
                return mm

            def fill_copy(use):
                n = COPY_AT[use]
                if n >= COPY_BANKS:
                    pe.wait_ge(copied, n - COPY_BANKS + 1)
                return copy_bank(use)

            def turn_xn(c):
                pe.wait_ge(normed, c + 1)
                turn(fill_copy(("xnT", c)), xn_tok[:, c]).then_inc(copy_ready, 1)

            def proj_px(c):
                dst = fill_copy(("px", c))
                pe.wait_ge(copied, COPY_AT[("xnT", c)] + 1)
                pe.matmul(dst[:], w_state[:], xnT[:, c].rearrange("p b t -> p (b t)"),
                          start=True, stop=True).then_inc(copy_ready, 1)

            def per_token(use, lhs, rhs, n):
                dst = fill(use)
                for b in range(B):
                    mm = pe.matmul(dst[:, b * n:(b + 1) * n], lhs[:, b, :], rhs, start=(b == 0), stop=(b == B - 1),
                                   skip_group_check=True)
                mm.then_inc(misc_ready, 1)

            def heads(c):
                for b in range(B):
                    pe.matmul(fill(("qkv", c, b))[:, 0:3 * D], xnT[:, c, b, :], w_in[:],
                              start=True, stop=True).then_inc(misc_ready, 1)

            def turn_att(c):
                pe.wait_ge(att_ready, c + 1)
                turn(fill_copy(("attT", c)), att[:, c]).then_inc(copy_ready, 1)

            def gate(c):
                per_token(("gate", c, 0), xnT[:, c], w_gate[:], D)

            def proj(c):
                pe.wait_ge(copied, COPY_AT[("attT", c)] + 1)
                per_token(("proj", c, 0), attT[:, c], w_op[:], D)

            def turn_h2(c):
                pe.wait_ge(normed, CH + c + 1)
                turn(fill_copy(("h2T", c)), z_tok[:, c]).then_inc(copy_ready, 1)

            def router(c):
                pe.wait_ge(copied, COPY_AT[("h2T", c)] + 1)
                per_token(("router", c, 0), h2T[:, c], w_router[:], E)

            pe.wait_ge(consts, 11)
            pe.wait_ge(d_early, N_EARLY)
            for c in range(CH):
                turn_xn(c)
                if c == CH - 1:
                    heads(1)
                proj_px(c)
                if c == 0:
                    pe.wait_ge(ln1_b_ready, 1)
                    pe.matmul(fill(("bias", 0, 0))[:, 0:3 * D], ln1_b[:], w_in[:], start=True,
                              stop=True).then_inc(misc_ready, 1)
                    pe.wait_ge(w_in_ready, 1)
                    heads(0)
            heads(2)
            heads(3)
            turn_att(0)
            proj(0)
            turn_att(1)
            proj(1)
            turn_h2(0)
            gate(0)
            turn_att(2)
            turn_h2(1)
            proj(2)
            router(0)
            gate(1)
            gate(2)
            gate(3)
            turn_att(3)
            turn_h2(2)
            proj(3)
            router(1)
            router(2)
            turn_h2(3)
            router(3)

            def hidden(i):
                c, e = divmod(i, E)
                for f in range(FT):
                    n = FT * i + f
                    if n < 4:
                        pe.wait_ge(misc_free, len(MISC))
                        pe.wait_ge(copied, len(COPIES))
                    else:
                        pe.wait_ge(hg_ready, n - 3)
                    pe.matmul(bank[1 + n % 4][:], w1[:, (e * F + f * P):(e * F + (f + 1) * P)],
                              h2T[:, c].rearrange("p b t -> p (b t)"), start=True, stop=True).then_inc(hm_ready, 1)

            def mix_out(i):
                e = i % E
                pe.wait_ge(hg_ready, FT * (i + 1))
                if i >= 2:
                    pe.wait_ge(y_free, i - 1)
                for f in range(FT):
                    for b in range(B):
                        mm = pe.matmul(bank[5 + i % 2][:, b * D:(b + 1) * D],
                                       hg[:, (FT * i + f) % 4, b * P:(b + 1) * P], w2[:, e, f, :],
                                       start=(f == 0 and b == 0), stop=(f == FT - 1), skip_group_check=True)
                mm.then_inc(y_ready, 1)

            def turn_state(c):
                pe.wait_ge(chain_state, (c + 1) * P)
                if c:
                    pe.wait_ge(xn2T_done, c)
                turn(turn_bank(c), state[:, c]).then_inc(sT_ready, 1)

            def turn_xn2(c):
                pe.wait_ge(normed, 2 * CH + c + 1)
                pe.wait_ge(sT_free, c + 1)
                turn(turn_bank(c), xn2_tok[:, c]).then_inc(xn2T_ready, 1)

            pe.wait_ge(d_moe, N_MOE)
            hidden(0)
            for i in range(CH * E):
                if i + 1 < CH * E:
                    hidden(i + 1)
                mix_out(i)
                if i >= 2 * E and i % E == 2:
                    turn_xn2(i // E - 2)
                if i >= E and i % E == 3:
                    turn_state(i // E - 1)
            turn_xn2(CH - 2)
            def w_parts(part, cols):
                return w_hi[:, part, cols], w_lo[:, part, cols]

            def product(dst, left, right, start, stop):
                pairs = [(left[0], right[0]), (left[0], right[1]), (left[1], right[0])]
                for n, (lhs, rhs) in enumerate(pairs):
                    mm = pe.matmul(dst, lhs, rhs, start=start and n == 0, stop=stop and n == 2, skip_group_check=True)
                return mm

            def project_heads(u, part, quads, whole=False):
                ready = (q_ready, k_ready)[part]
                for quad in quads:
                    if quad == 3:
                        pe.wait_ge((q_free, k_free)[part], 4 * u + 1)
                    elif quad == 2 and not whole:
                        pe.wait_ge(z1_ready, B)
                    elif quad == 0 and not whole:
                        if part == 0:
                            pe.wait_ge(halves_ready, u)
                        pe.wait_ge(s_free, 2 * (u - 1) + part + 1)
                    for j in range(2):
                        col = (2 * quad + j) * P
                        dst = (Q_BANKS, K_BANKS)[part][quad][:, j * UNIT:(j + 1) * UNIT]
                        if whole:
                            mm = pe.matmul(dst, w_qkv[:, part, col:col + P], xc[:],
                                           start=(j == 0), stop=(j == 1), skip_group_check=True)
                        else:
                            mm = product(dst, w_parts(part, slice(col, col + P)), (xc_hi[:], xc_lo[:]), j == 0, j == 1)
                    mm.then_inc(ready, 1)

            def project_v(u, n, whole=False):
                b, half = divmod(n, 2)
                if n == 2:
                    pe.wait_ge(k_free, 4 * u + 4)
                elif n == 3:
                    pe.wait_ge(q_free, 4 * u + 4)
                elif not whole:
                    pe.wait_ge(z1_ready, B)
                    pe.wait_ge(sc_max, u * MB)
                cols, tokens = slice(half * 512, (half + 1) * 512), slice(b * P, (b + 1) * P)
                if whole:
                    mm = pe.matmul(V_BANKS[n][:], xc[:, tokens], w_qkv[:, 2, cols], start=True, stop=True)
                else:
                    mm = product(V_BANKS[n][:], (xc_hi[:, tokens], xc_lo[:, tokens]), w_parts(2, cols), True, True)
                mm.then_inc(v_ready, 1)

            def scores(u, m, first=False):
                if not first or m >= 2:
                    pe.wait_ge(sc_max, u * MB + m - 1)
                for i in range(4):
                    cols = slice((4 * m + i) * TB, (4 * m + i + 1) * TB)
                    mm = pe.matmul(S[m % 2][:, i * P:(i + 1) * P], qT[:, cols, :].rearrange("p t h -> p (t h)"),
                                   kT[:, cols, :].rearrange("p t h -> p (t h)"),
                                   start=(i == 0), stop=(i == 3), skip_group_check=True)
                mm.then_inc(score, 1)

            def turn_probs(u, m, last=False):
                wait_spread(pe, u, m)
                if m == 0 and not last:
                    pe.wait_ge(q_free, 4 * u + 6)
                if m == 1 and not last:
                    pe.wait_ge(k_free, 4 * u + 6)
                pe.wait_ge(tcopy, u * MB + m + 1)
                for i in range(4):
                    mm = pe.transpose(TR[m % 2][:, i * P:(i + 1) * P],
                                      pex[:, m % 4, i].rearrange("p t g -> p (t g)"), ident[:])
                mm.then_inc(turned, 1)

            def values(u, last=False):
                for m in range(MB):
                    if m and m + 1 < MB:
                        turn_probs(u, m + 1)
                    if m == MB - 1:
                        attention_out(u, 0, last)
                    if m == 0:
                        pe.wait_ge(v_in, u * 16 + 16)
                    pe.wait_ge(tcopy, u * MB + m + 3)
                    if m % 2 == 0:
                        pe.wait_ge(even_copied, u * OB + m // 2 + 1)
                        pe.wait_ge(odd_copied, u * OB + m // 2 + 1)
                    if not last and m == 0:
                        pe.wait_ge(q_free, 4 * u + 7)
                    if not last and m == 2:
                        pe.wait_ge(k_free, 4 * u + 7)
                    for i in range(4):
                        half, col = i % 2, 2 * (m % 2) + i // 2
                        mm = pe.matmul(O[m // 2 % 2][half * HD1:(half + 1) * HD1, col * P:(col + 1) * P],
                                       vb[:, 4 * m + i, :], ptT[:, m % 2, i], start=(col == 0), stop=(col == 3),
                                       skip_group_check=True)
                    mm.then_inc(pvd, 1)
                    if not last and m in (1, 3):
                        project_v(u + 1, 2 + m // 2)

            def attention_out(u, b, last=False):
                pe.wait_ge(even_copied, u * OB + 2 * b + 4)
                pe.wait_ge(odd_copied, u * OB + 2 * b + 4)
                if last:
                    pe.wait_ge(s_free, 2 * u + b + 1)
                else:
                    pe.wait_ge(v_free, 4 * u + 8 - b)
                for p in range(PAIRS):
                    mm = pe.matmul(PR[b][:, 0:D], onT[:, b * P:(b + 1) * P, p], w_out[:, p, :],
                                   start=(p == 0), stop=(p == PAIRS - 1))
                mm.then_inc(s_ready, 1)

            pe.wait_ge(d_late, N_LATE)
            pe.wait_ge(y_free, CH * E)
            turn_state(CH - 1)
            pe.wait_ge(xc_ready, 16)
            project_heads(0, 0, (0, 1), whole=True)
            project_heads(0, 1, (0, 1), whole=True)
            turn_xn2(CH - 1)
            project_heads(0, 0, (2,), whole=True)
            project_heads(0, 1, (2,), whole=True)
            project_heads(0, 0, (3,), whole=True)
            project_heads(0, 1, (3,), whole=True)
            pe.wait_ge(xn2T_done, CH)
            pe.wait_ge(q_free, 2)
            xn2T_cb = xn2T[:, 0:UNITS, :].rearrange("p u t -> p (u t)").rearrange("p (c b t) -> p c b t", c=CH, b=B)
            pe.matmul(bank[2][:, 0:B], w_p1[:], xn2T_cb[:, CH - 1, :, P - 1], start=True, stop=True).then_inc(p1_ready, 1)
            project_v(0, 0, whole=True)
            project_v(0, 1, whole=True)
            pe.wait_ge(a1_ready, 1)
            pe.wait_ge(k_free, 2)
            for b in range(B):
                mm = pe.matmul(bank[3][0:1, b * E:(b + 1) * E], a1[:, b:b + 1], w_p2[:],
                               start=(b == 0), stop=(b == B - 1), skip_group_check=True)
            mm.then_inc(p2_ready, 1)
            project_v(0, 2, whole=True)
            project_v(0, 3, whole=True)
            pe.wait_ge(masks_in, 32)
            pe.wait_ge(q_free, 4)
            pe.wait_ge(v_free, 2)
            for m in range(MB):
                scores(0, m, first=True)

            pe.wait_ge(sel_ready, 1)
            for b in range(B):
                pe.wait_ge(d_exp[b], 16)
                for f in range(FT):
                    n = b * FT + f
                    if n >= 4:
                        pe.wait_ge(f_gelu, n - 3)
                    pe.matmul(FB[n % 4][:], ew[:, b, f * P:(f + 1) * P], xn2T_cb[:, :, b, :],
                              start=True, stop=True).then_inc(f_ready, 1)
            for b in range(B):
                pe.wait_ge(f_gelu, FT * (b + 1))
                if b >= 2:
                    pe.wait_ge(r_done, b - 1)
                else:
                    pe.wait_ge(v_free, 4)
                for f in range(FT):
                    mm = pe.matmul(bank[5 + b % 2][:], ew[:, b, F + f * D:F + (f + 1) * D], hg1[:, b, f, :],
                                   start=(f == 0), stop=(f == FT - 1))
                mm.then_inc(r_ready, 1)
            pe.wait_ge(sc_max, MB)
            for b in range(B):
                pe.wait_ge(r_done, b + 1)
                for t in range(CH):
                    mm = pe.matmul(YB[b][:, t * D:(t + 1) * D], rT[:, b, t * P:(t + 1) * P], w_o[:],
                                   start=(t == 0), stop=(t == CH - 1), skip_group_check=True)
                mm.then_inc(o_ready, 1)

            pe.wait_ge(halved, 2)
            pe.wait_ge(w_split, 6)
            pe.sem_inc(turned, 4)
            pe.sem_inc(pvd, 2)
            pe.sem_inc(s_ready, 2)
            with pe.Fori(0, UNITS - 1) as u:
                project_heads(u + 1, 0, (0, 1))
                project_heads(u + 1, 1, (0, 1))
                project_heads(u + 1, 0, (2, 3))
                project_v(u + 1, 0)
                project_v(u + 1, 1)
                project_heads(u + 1, 1, (2,))
                turn_probs(u, 0)
                project_heads(u + 1, 1, (3,))
                turn_probs(u, 1)
                values(u)
                for m in range(MB):
                    scores(u + 1, m)
                    if m == MB // 2 - 1:
                        attention_out(u, 1)
            turn_probs(UNITS - 1, 0, last=True)
            turn_probs(UNITS - 1, 1, last=True)
            values(UNITS - 1, last=True)
            attention_out(UNITS - 1, 1, last=True)

        @block.scalar
        def _(act):
            def columns(t):
                return t.rearrange("p b t -> p (b t)")

            def copy_half(use, h, dst, bias=None, scale=1.0):
                c = use[1]
                if h == 0:
                    act.wait_ge(copy_ready, COPY_AT[use] + 1)
                cols = slice(h * 256, (h + 1) * 256)
                o, i = columns(dst[:, c])[:, cols], copy_bank(use)[:, cols]
                ins_ = (nc.scalar.copy(o, i) if bias is None else
                        nc.scalar.activation(o, i, ACT.Identity, bias=bias, scale=scale))
                if h:
                    ins_.then_inc(copied, 1)

            def side(t):
                for c in range(CH):
                    for h in range(2):
                        if c and t == XNT_STEP[c] + h:
                            copy_half(("xnT", c), h, xnT)
                        if c and t == PX_STEP[c] + h:
                            copy_half(("px", c), h, px, cols0[:, 0:1])
                        if t == ATTT_STEP[c] + h:
                            copy_half(("attT", c), h, attT)
                        if t == H2T_STEP[c] + h:
                            copy_half(("h2T", c), h, h2T, cols0[:, 4:5], cols0[:, 3:4])
                        if t == GATE_TANH_STEP[c] + 2 * h:
                            act.wait_ge(misc_free, MISC_AT[("gate", c, 0)] + 1)
                            cols = slice(2 * h, 2 * h + 2)
                            o = nc.scalar.activation(tg[:, c, cols], tg[:, c, cols], ACT.Tanh, scale=0.5)
                            if h:
                                o.then_inc(tg_ready, 1)
                        if t == MOE_STEP + MOE_PERIOD * E * (c + 1) + MOE_LAG + 2 * h:
                            act.wait_ge(z_ready, c + 1)
                            cols = slice(2 * h, 2 * h + 2)
                            o = nc.scalar.activation(tz[:, c, cols], x1[:, c, cols], ACT.Tanh, scale=0.5)
                            if h:
                                o.then_inc(tz_ready, 1)
                    if t == ATT_EXP_STEP[c]:
                        act.wait_ge(sc_ready, c + 1)
                        nc.scalar.activation(sc[:, c].rearrange("p a b h -> p (a b h)"),
                                             sc[:, c].rearrange("p a b h -> p (a b h)"), ACT.Exp,
                                             scale=float(HD0) ** -0.5).then_inc(pe_ready, 1)
                if t == ROUTER_EXP_STEP:
                    act.wait_ge(lg_ready, 1)
                    nc.scalar.activation(ex[:], ex[:], ACT.Exp).then_inc(ex_ready, 1)
                i, r = divmod(t - MOE_STEP, MOE_PERIOD)
                if 0 <= i < CH * E and r in (0, 2, 4, 6):
                    n, h = FT * i + r // 4, r // 2 % 2
                    if h == 0:
                        act.wait_ge(hm_ready, n + 1)
                        if n >= 4:
                            act.wait_ge(y_ready, n // 2 - 1)
                    cols = slice(h * 256, (h + 1) * 256)
                    o = nc.scalar.activation(hg[:, n % 4, cols], bank[1 + n % 4][:, cols], ACT.Gelu)
                    if h:
                        o.then_inc(hg_ready, 1)

            act.wait_ge(consts, 3)
            nc.scalar.activation(zero_state[:], zero_state[:], ACT.Tanh)
            act.wait_ge(d_early, N_EARLY)
            for h in range(2):
                copy_half(("xnT", 0), h, xnT)
            for h in range(2):
                copy_half(("px", 0), h, px, cols0[:, 0:1])
            for t in range(T):
                act.wait_ge(chain_sum, t + 1)
                nc.scalar.activation(state[:, t // P, :, t % P], bank[0][:, 0:B], ACT.Tanh).then_inc(chain_state, 1)
                side(t)
            for t in range(T, MOE_STEP + MOE_PERIOD * E * CH + MOE_LAG + 3):
                side(t)

            def q_copy(u, quads, pairs=(0, 1)):
                for quad in quads:
                    act.wait_ge(q_ready, 4 * u + quad + 1)
                    for j in pairs:
                        for h in range(2):
                            pair = 2 * quad + j
                            rows = slice(h * HD1, (h + 1) * HD1)
                            q = nc.scalar.activation(qT[0:HD1, :, 2 * pair + h], Q_BANKS[quad][rows, j * UNIT:(j + 1) * UNIT],
                                                     ACT.Identity, bias=bq8[rows, pair:pair + 1],
                                                     scale=float(HD1) ** -0.5)
                    if pairs[-1] == 1:
                        q.then_inc(q_free, 1)

            def exponential(u, h):
                act.wait_ge(sc_sub, 2 * u + h + 1)
                nc.scalar.activation(sc1[:, HALVES[h]], sc1[:, HALVES[h]], ACT.Exp).then_inc(sc_exp, 1)

            def even_copy(u, n):
                act.wait_ge(pvd, u * MB + 2 * n + 4)
                if n % 2 == 0:
                    act.wait_ge(s_ready, 2 * u + n // 2 + 1)
                for h in range(2):
                    dst, src = copy_of(n, 0, h)
                    o = nc.scalar.copy(dst, src)
                o.then_inc(even_copied, 1)

            def values(u, last=False):
                for m in range(MB):
                    if m in (1, 2) and not last:
                        q_copy(u + 1, (3,), (m - 1,))
                    act.wait_ge(turned, u * MB + m + 5)
                    act.wait_ge(pvd, u * MB + m + 1)
                    nc.scalar.copy(ptT[:, m % 2].rearrange("p k c -> p (k c)"), TR[m % 2][:]).then_inc(tcopy, 1)
                    if m >= 2 and m % 2 == 0:
                        even_copy(u, m // 2 - 1)
                even_copy(u, OB - 1)

            act.wait_ge(bc_done, 2)
            q_copy(0, range(4))

            act.wait_ge(p1_ready, 1)
            nc.scalar.activation(a1[:], bank[2][:, 0:B], ACT.Gelu, bias=b_p1[:]).then_inc(a1_ready, 1)

            for b in range(B):
                act.wait_ge(d_exp[b], 16)
                for f in range(FT):
                    n = b * FT + f
                    act.wait_ge(f_ready, n + 1)
                    nc.scalar.activation(hg1[:, b, f, :], FB[n % 4][:], ACT.Gelu,
                                         bias=ew[:, b, 2 * F + f:2 * F + f + 1]).then_inc(f_gelu, 1)
            for b in range(B):
                act.wait_ge(z1_ready, b + 1)
                nc.scalar.activation(tz1[:, :, b], z1[:, :, b], ACT.Tanh, scale=0.5).then_inc(tz1_ready, 1)

            act.sem_inc(tcopy, 2)
            act.sem_inc(even_copied, 2)
            with act.Fori(0, UNITS - 1) as u:
                exponential(u, 0)
                q_copy(u + 1, (0,))
                exponential(u, 1)
                q_copy(u + 1, (1, 2))
                values(u)
            exponential(UNITS - 1, 0)
            exponential(UNITS - 1, 1)
            values(UNITS - 1, last=True)

        @block.vector
        def _(dve):
            count = [0]

            def own(ins_):
                count[0] += 1
                ins_.then_inc(vec, 1)
                return count[0]

            def stats_of(ln, c, src, b):
                own(nc.vector.bn_stats(stats[:, ln, c, b, :], src[:, c, b, :]))

            def aggr_of(ln, c, b, done):
                dve.wait_ge(vec, done)
                return own(nc.vector.bn_aggr(mv[:, ln, c, b, :], stats[:, ln, c, b, :]))

            def variance(ln, c, done):
                dve.wait_ge(vec, done)
                nc.vector.tensor_scalar(var[:, ln, c, :], mv[:, ln, c, :, 1], EPS, None, ALU.add).then_inc(var_ready, 1)

            def read(use):
                dve.wait_ge(misc_ready, MISC_AT[use] + 1)
                return misc_bank(use)

            def flat(t):
                return t.rearrange("p b t -> p (b t)")

            def ln_stats(ln, c, src):
                for b in range(B):
                    stats_of(ln, c, src, b)
                    yield 0.2
                base = count[0] - B
                for b in range(B):
                    last = aggr_of(ln, c, b, base + b + 1)
                    if b % 2:
                        yield 0.15
                variance(ln, c, last)
                yield 0.07

            def norm(ln, c, src, dst):
                dve.wait_ge(rstd_ready, ln * CH + c + 1)
                for b in range(B):
                    ins_ = nc.vector.tensor_scalar(dst[:, c, b, :], src[:, c, b, :], mv[:, ln, c, b, 0:1],
                                                   rstd[:, ln, c, b:b + 1], ALU.subtract, ALU.mult)
                    if b == B - 1:
                        ins_.then_inc(normed, 1)
                        if ln == 0 and c:
                            assert slot[0] < XNT_STEP[c], (c, slot)
                    yield 0.2

            slot = [-1]

            dve.wait_ge(d_x[0], 16)
            for _ in ln_stats(0, 0, x_tok):
                pass
            for _ in norm(0, 0, x_tok, xn_tok):
                pass
            dve.wait_ge(d_early, N_EARLY)

            def until(t):
                while slot[0] < t:
                    yield None

            def prep(c, meanwhile=None):
                dve.wait_ge(tz_ready, c + 1)
                dve.wait_ge(tg_ready, c + 1)
                parts = [slice(0, 2), slice(2, 4)]
                for i in parts:
                    m = own(nc.vector.scalar_tensor_tensor(out=flat(x1[:, c, i]), in0=flat(tz[:, c, i]), scalar=1.0,
                                                           in1=flat(x1[:, c, i]), op0=ALU.add, op1=ALU.mult))
                    yield 0.34
                for h, i in enumerate(parts):
                    dve.wait_ge(vec, m - 1 + h)
                    own(nc.vector.scalar_tensor_tensor(out=flat(mix[:, c, i]), in0=flat(tg[:, c, i]), scalar=1.0,
                                                       in1=flat(x1[:, c, i]), op0=ALU.add, op1=ALU.mult))
                    yield 0.34
                dve.wait_ge(sT_ready, c + 1)
                for h, i in enumerate(parts):
                    dve.wait_ge(vec, m + 1 + h)
                    own(nc.vector.scalar_tensor_tensor(out=flat(mix[:, c, i]), in0=turn_bank(c)[:, h * 256:(h + 1) * 256],
                                                       scalar=0.25, in1=flat(mix[:, c, i]), op0=ALU.mult, op1=ALU.mult))
                    yield 0.34
                dve.wait_ge(vec, m + 4)
                dve.sem_inc(sT_free, 1)
                for i in parts:
                    own(nc.vector.tensor_tensor(flat(x_tok[:, c, i]), flat(x_tok[:, c, i]), flat(mix[:, c, i]), ALU.add))
                    yield 0.34
                dve.wait_ge(vec, m + 6)
                yield from ln_stats(2, c, x_tok)
                if meanwhile:
                    meanwhile()
                for _ in range(4):
                    yield 0.3
                yield from norm(2, c, x_tok, xn2_tok)

            def pause(steps):
                yield from until(slot[0] + steps)

            def evac_xn2T(c):
                dve.wait_ge(xn2T_ready, c + 1)
                for h in range(2):
                    ins_ = nc.vector.tensor_copy(xn2T[:, 2 * c + h, :], turn_bank(c)[:, h * UNIT:(h + 1) * UNIT])
                    if h:
                        ins_.then_inc(xn2T_done, 1)
                    yield 0.34

            def heads(c):
                dve.wait_ge(again_ready, c + 1)
                for b in range(B):
                    nc.vector.scalar_tensor_tensor(out=qkv[:, c, b, :], in0=read(("qkv", c, b))[:, 0:3 * D],
                                                   scalar=again[:, c, b:b + 1], in1=rows0[:, 0:3 * D],
                                                   op0=ALU.mult, op1=ALU.add).then_inc(misc_free, 1)
                    yield 0.47

            def att_scores(c):
                dve.wait_ge(qk_prod, c + 1)
                n = 0
                for s in range(B):
                    last = own(nc.vector.tensor_reduce(
                        sc[:, c, s, 0:s + 1, :].rearrange("p u h -> p (u h)"),
                        prod[:, c, n:n + s + 1, :].rearrange("p u (h d) -> p (u h) d", h=H0), X, ALU.add))
                    n += s + 1
                    yield 0.13 * s + 0.2
                dve.wait_ge(vec, last)
                last = own(nc.vector.tensor_reduce(mx0[:, c], sc[:, c].rearrange("p s u h -> p s h u"), X, ALU.max))
                yield 0.34
                dve.wait_ge(vec, last)
                nc.vector.tensor_tensor(sc[:, c], sc[:, c], mx0[:, c].unsqueeze(2).broadcast_to([P, B, B, H0]),
                                        ALU.subtract).then_inc(sc_ready, 1)
                assert slot[0] <= ATT_EXP_STEP[c], (c, slot)
                yield 0.34

            def att_probs(c):
                yield from until(ATT_EXP_STEP[c] + 1)
                dve.wait_ge(pe_ready, c + 1)
                last = own(nc.vector.tensor_reduce(rs0[:, c], sc[:, c].rearrange("p s u h -> p s h u"), X, ALU.add))
                yield 0.34
                dve.wait_ge(vec, last)
                last = own(nc.vector.reciprocal(rs0[:, c], rs0[:, c]))
                yield 0.47
                dve.wait_ge(vec, last)
                nc.vector.tensor_tensor(sc[:, c], sc[:, c], rs0[:, c].unsqueeze(2).broadcast_to([P, B, B, H0]),
                                        ALU.mult).then_inc(prob_ready, 1)
                yield 0.34

            def att_values(c):
                dve.wait_ge(pv_prod, c + 1)
                n = 1
                for s in range(1, B):
                    ins_ = nc.vector.tensor_reduce(att[:, c, s, :], prod[:, c, n:n + s + 1, :].rearrange("p u e -> p e u"),
                                                   X, ALU.add)
                    n += s + 1
                    if s < B - 1:
                        yield 0.2 + 0.13 * s
                ins_.then_inc(att_ready, 1)
                assert slot[0] < ATTT_STEP[c], (c, slot)
                yield 0.6

            def gate_sum(c):
                for h in range(2):
                    i = slice(2 * h, 2 * h + 2)
                    ins_ = nc.vector.tensor_tensor(
                        tg[:, c, i], read(("gate", c, 0))[:, h * 256:(h + 1) * 256].rearrange("p (b d) -> p b d", b=2),
                        rows0[:, 4 * D:5 * D].unsqueeze(1).broadcast_to([P, 2, D]), ALU.add)
                    if h:
                        ins_.then_inc(misc_free, 1)
                        assert slot[0] < GATE_TANH_STEP[c], (c, slot)
                    yield 0.34

            def attention_sum(c):
                dve.wait_ge(xnb_ready, c + 1)
                for h in range(2):
                    i = slice(2 * h, 2 * h + 2)
                    ins_ = nc.vector.tensor_tensor(flat(x1[:, c, i]), read(("proj", c, 0))[:, h * 256:(h + 1) * 256],
                                                   flat(xnb[:, c, i]), ALU.add)
                    if h:
                        ins_.then_inc(misc_free, 1)
                    yield 0.34
                dve.wait_ge(misc_free, MISC_AT[("proj", c, 0)] + 1)
                yield from ln_stats(1, c, x1)

            def second(c):
                yield from norm(1, c, x1, z_tok)
                assert slot[0] < H2T_STEP[c], (c, slot)

            def logits(c):
                ins_ = nc.vector.tensor_copy(lg[:, c * B:(c + 1) * B, :],
                                             read(("router", c, 0))[:, 0:B * E].rearrange("p (b e) -> p b e", b=B))
                ins_.then_inc(misc_free, 1)
                yield 0.1

            def side():
                dve.wait_ge(misc_ready, 1)
                nc.vector.tensor_scalar(w_in[:], w_in[:], cols0[:, 1:2], None, ALU.mult).then_inc(w_in_ready, 1)
                yield 0.4
                own(nc.vector.tensor_tensor(rows0[:, 0:3 * D], misc_bank(("bias", 0, 0))[:, 0:3 * D], rows0[:, 0:3 * D],
                                            ALU.add))
                yield 0.47
                dve.wait_ge(vec, count[0])
                dve.sem_inc(misc_free, 1)
                for c in range(1, CH):
                    dve.wait_ge(d_x[c], 16)
                    yield from ln_stats(0, c, x_tok)
                    if c >= 2:
                        yield from norm(0, c - 1, x_tok, xn_tok)
                yield from pause(2)
                yield from norm(0, CH - 1, x_tok, xn_tok)
                yield from heads(0)
                yield from heads(1)
                yield from att_scores(0)
                yield from heads(2)
                yield from att_scores(1)
                yield from att_probs(0)
                yield from heads(3)
                yield from att_scores(2)
                yield from att_probs(1)
                yield from att_values(0)
                yield from att_scores(3)
                yield from att_probs(2)
                yield from attention_sum(0)
                yield from att_values(1)
                yield from att_probs(3)
                yield from second(0)
                yield from pause(2)
                yield from attention_sum(1)
                yield from att_values(2)
                yield from second(1)
                yield from gate_sum(0)
                yield from pause(3)
                yield from attention_sum(2)
                yield from logits(0)
                yield from gate_sum(1)
                yield from att_values(3)
                yield from second(2)
                yield from gate_sum(2)
                yield from gate_sum(3)
                yield from pause(3)
                yield from attention_sum(3)
                yield from logits(1)
                yield from pause(3)
                yield from second(3)
                yield from logits(2)
                yield from pause(8)
                yield from logits(3)
                dve.wait_ge(misc_free, MISC_AT[("router", CH - 1, 0)] + 1)

                def wide(v):
                    return v.unsqueeze(2).broadcast_to([P, CH * B, E])

                fall = falling[:].unsqueeze(1).broadcast_to([P, CH * B, E])
                m = own(nc.vector.tensor_reduce(r16[:, 0], lg[:], X, ALU.max))
                yield 0.2
                dve.wait_ge(vec, m)
                nc.vector.tensor_tensor(ex[:], lg[:], wide(r16[:, 0]), ALU.subtract).then_inc(lg_ready, 1)
                assert slot[0] <= ROUTER_EXP_STEP, slot

                yield 0.2

                def first_max(src, top, n, hot):
                    m = own(nc.vector.tensor_tensor(hot[:], src[:], wide(top), ALU.is_equal))
                    dve.wait_ge(vec, m)
                    m = own(nc.vector.tensor_tensor(hot[:], hot[:], fall, ALU.mult))
                    yield 0.2
                    dve.wait_ge(vec, m)
                    m = own(nc.vector.tensor_reduce(r16[:, n], hot[:], X, ALU.max))
                    dve.wait_ge(vec, m)
                    own(nc.vector.tensor_tensor(hot[:], hot[:], wide(r16[:, n]), ALU.is_equal))
                    yield 0.2

                yield from first_max(lg, r16[:, 0], 1, oh1)
                dve.wait_ge(vec, count[0])
                m = own(nc.vector.scalar_tensor_tensor(out=lg2[:], in0=oh1[:], scalar=NEG, in1=lg[:], op0=ALU.mult, op1=ALU.add))
                yield 0.2
                dve.wait_ge(vec, m)
                m = own(nc.vector.tensor_reduce(r16[:, 2], lg2[:], X, ALU.max))
                dve.wait_ge(vec, m)
                yield from first_max(lg2, r16[:, 2], 3, oh2)
                dve.wait_ge(vec, count[0])
                own(nc.vector.tensor_tensor(oh1[:], oh1[:], oh2[:], ALU.add))
                yield 0.2
                yield from until(ROUTER_EXP_STEP + 1)
                dve.wait_ge(ex_ready, 1)
                m = own(nc.vector.tensor_reduce(r16[:, 4], ex[:], X, ALU.add))
                yield 0.2
                dve.wait_ge(vec, m)
                m = own(nc.vector.reciprocal(r16[:, 5], r16[:, 4]))
                own(nc.vector.tensor_tensor(ex[:], ex[:], oh1[:], ALU.mult))
                yield 0.2
                dve.wait_ge(vec, m + 1)
                own(nc.vector.tensor_tensor(gates[:], ex[:], wide(r16[:, 5]), ALU.mult))
                yield 0.2

                def constants():
                    dve.wait_ge(d_late, N_LATE)
                    nc.vector.tensor_scalar(rows1[:, D:2 * D], rows1[:, D:2 * D], 0.3, None, ALU.mult).then_inc(bc_done, 1)
                    yield 0.2
                    nc.vector.tensor_scalar(bq8[:], bqk[:, 0, :], float(HD1) ** -0.5, None, ALU.mult).then_inc(bc_done, 1)
                    yield 0.2

                spare = constants()
                dve.wait_ge(vec, count[0])
                last = [None] * B
                for i in range(CH * E):
                    c, e = divmod(i, E)
                    yield from until(MOE_STEP + MOE_PERIOD * i + MOE_LAG)
                    dve.wait_ge(y_ready, i + 1)
                    for b in range(B):
                        if e:
                            dve.wait_ge(vec, last[b])
                        ins_ = nc.vector.scalar_tensor_tensor(
                            out=x1[:, c, b, :], in0=bank[5 + i % 2][:, b * D:(b + 1) * D],
                            scalar=gates[:, c * B + b, e:e + 1], in1=x1[:, c, b, :], op0=ALU.mult, op1=ALU.add)
                        last[b] = own(ins_)
                        if b < B - 1:
                            yield 0.27
                    dve.wait_ge(vec, last[B - 1])
                    dve.sem_inc(y_free, 1)
                    if e == E - 1:
                        dve.sem_inc(z_ready, 1)
                    yield 0.27
                    if c and e == 2:
                        spare = prep(c - 1)
                    for _ in range(4):
                        yield next(spare, 0.0) or 0.1
                    if c and e == 7:
                        yield from spare
                    if c >= 2 and e == 1:
                        yield from evac_xn2T(c - 2)

            work = side()
            budget = 0.0
            for t in range(T):
                if t == 0:
                    dve.wait_ge(consts, 3)
                    prev = zero_state[:]
                    dve.wait_ge(copied, 2)
                else:
                    dve.wait_ge(chain_state, t)
                    prev = state[:, (t - 1) // P, :, (t - 1) % P]
                if t and t % P == 0:
                    dve.wait_ge(copied, COPY_AT[("px", t // P)] + 1)
                nc.vector.tensor_tensor(bank[0][:, 0:B], px[:, t // P, :, t % P], prev, ALU.add).then_inc(chain_sum, 1)
                slot[0] = t
                budget = min(budget + FREE_US, FREE_US)
                while budget > 0.12:
                    spent = next(work, None)
                    if spent is None:
                        break
                    budget -= spent
            slot[0] = 10 ** 6
            for _ in work:
                pass

            def k_copy(u, quad, heads=(0, 1)):
                dve.wait_ge(k_ready, 4 * u + quad + 1)
                if quad == 0:
                    dve.wait_ge(posb_ready, u + 1)
                for h in heads:
                    rows = slice(h * HD1, (h + 1) * HD1)
                    pairs = slice(2 * quad, 2 * quad + 2)
                    for b in range(2):
                        k = nc.vector.tensor_tensor(
                            kT[0:HD1, b * P:(b + 1) * P, 4 * quad + h:4 * quad + h + 3:2].rearrange("p t j -> p j t"),
                            K_BANKS[quad][rows, :].rearrange("p (j b t) -> p j b t", j=2, b=2)[:, :, b, :],
                            posb[rows, pairs, :], ALU.add)
                if heads[-1] == 1:
                    k.then_inc(k_free, 1)

            def v_copy(u, n):
                b, half = divmod(n, 2)
                cols = slice(half * 512, (half + 1) * 512)
                dve.wait_ge(v_ready, 4 * u + n + 1)
                nc.vector.tensor_tensor(vt[:, b, cols], V_BANKS[n][:], bv_row[:, cols], ALU.add).then_inc(v_free, 1)

            def per_block(t):
                return t.unsqueeze(2).broadcast_to([P, KB // 2, H1])

            def block_scores(u, m):
                dve.wait_ge(score, u * MB + m + 1)
                nc.vector.tensor_reduce(sc1[:, 4 * m:4 * m + 4, :],
                                        S[m % 2][:].rearrange("p (k t g) -> p k g t", k=4, t=TB), X, ALU.max
                                        ).then_inc(sc_max, 1)

            def centre(u, h):
                k = HALVES[h]
                dve.wait_ge(sc_max, u * MB + (h + 1) * MB // 2)
                nc.vector.tensor_reduce(m1[:, 0, k], sc1[:, k], X, ALU.max).then_inc(small, 1)
                dve.wait_ge(small, u * 5 + h + 1)
                nc.vector.tensor_tensor(sc1[:, k], sc1[:, k], per_block(m1[:, 0, k]), ALU.subtract).then_inc(sc_sub, 1)

            def sums(u, h):
                dve.wait_ge(sc_exp, 2 * u + h + 1)
                nc.vector.tensor_reduce(m1[:, 1, HALVES[h]], sc1[:, HALVES[h]], X, ALU.add).then_inc(small, 1)

            def probs(u):
                dve.wait_ge(small, u * 5 + 4)
                nc.vector.reciprocal(m1[:, 2], m1[:, 1]).then_inc(small, 1)
                dve.wait_ge(small, u * 5 + 5)
                for k in HALVES:
                    nc.vector.tensor_tensor(sc1[:, k], sc1[:, k], per_block(m1[:, 2, k]), ALU.mult).then_inc(prob, 1)

            def spread_vector(u, m):
                if m == VECTOR_SPREADS[0]:
                    dve.wait_ge(prob, 2 * u + 2)
                dve.wait_ge(turned, u * MB + m + 1)
                nc.vector.tensor_tensor(
                    pex[:, m % 4], sc1[:, 4 * m:4 * m + 4, :].unsqueeze(2).broadcast_to([P, 4, TB, H1]),
                    own_token[:].unsqueeze(1).unsqueeze(3).broadcast_to([P, 4, TB, H1]), ALU.mult).then_inc(spread_v, 1)

            def odd_copy(u, n):
                dve.wait_ge(pvd, u * MB + 2 * n + 4)
                if n % 2 == 0:
                    dve.wait_ge(s_ready, 2 * u + n // 2 + 1)
                for h in range(2):
                    dst, src = copy_of(n, 1, h)
                    o = nc.vector.tensor_copy(dst, src)
                o.then_inc(odd_copied, 1)

            def output(u, b):
                dve.wait_ge(s_ready, 2 * u + b + 3)
                nc.vector.tensor_tensor(tile_of(s_all, 2 * u + b), PR[b][:, 0:D], rows1[:, 0:D],
                                        ALU.add).then_inc(s_free, 1)

            for _ in evac_xn2T(CH - 2):
                pass
            for _ in prep(CH - 1):
                pass
            k_copy(0, 0)
            k_copy(0, 1)
            for _ in evac_xn2T(CH - 1):
                pass
            k_copy(0, 2)
            k_copy(0, 3)
            v_copy(0, 0)
            v_copy(0, 1)

            dve.wait_ge(p2_ready, 1)
            lgs, eq = rt[:, 0], rt[:, 1]
            m = own(nc.vector.tensor_tensor(lgs, bank[3][0:1, 0:B * E].rearrange("p (b e) -> p b e", b=B),
                                            b_p2[:].unsqueeze(1).broadcast_to([1, B, E]), ALU.add))
            dve.wait_ge(vec, m)
            m = own(nc.vector.tensor_reduce(rt[:, 2, :, 0], lgs, X, ALU.max))
            dve.wait_ge(vec, m)
            m = own(nc.vector.tensor_tensor(eq, lgs, rt[:, 2, :, 0:1].broadcast_to([1, B, E]), ALU.is_equal))
            dve.wait_ge(vec, m)
            m = own(nc.vector.tensor_tensor(eq, eq, falling[0:1, :].unsqueeze(1).broadcast_to([1, B, E]), ALU.mult))
            dve.wait_ge(vec, m)
            m = own(nc.vector.tensor_reduce(rt[:, 3, :, 0], eq, X, ALU.max))
            dve.wait_ge(vec, m)
            nc.vector.tensor_scalar(sel[:], rt[:, 3, :, 0], -1.0, float(E), ALU.mult, ALU.add).then_inc(sel_ready, 1)
            v_copy(0, 2)
            v_copy(0, 3)

            for m in range(MB):
                block_scores(0, m)
            centre(0, 0)
            centre(0, 1)

            def split_unit(n):
                dve.wait_ge(xc_ready, n * 16 + 32)
                nc.vector.tensor_copy(xc_hi[:], xc[:]).then_inc(xc_hi_made, 1)
                dve.wait_ge(xc_hi_made, n + 1)
                nc.vector.tensor_tensor(xc_lo[:], xc[:], xc_hi[:].bitcast(F32), ALU.subtract).then_inc(halves_ready, 1)

            dve.wait_ge(v_ready, 4)
            dve.wait_ge(xnb2_ready, CH)
            for n in range(6):
                part, cols = n // 2, slice(n % 2 * 512, (n % 2 + 1) * 512)
                m = own(nc.vector.tensor_copy(w_hi[:, part, cols], w_qkv[:, part, cols]))
                dve.wait_ge(vec, m)
                nc.vector.tensor_tensor(w_lo[:, part, cols], w_qkv[:, part, cols], w_hi[:, part, cols].bitcast(F32),
                                        ALU.subtract).then_inc(w_split, 1)
            split_unit(0)

            for b in range(B):
                dve.wait_ge(d_exp[b], 16)
                dve.wait_ge(r_ready, b + 1)
                nc.vector.tensor_scalar(rT[:, b, :], bank[5 + b % 2][:], ew[:, b, 2 * F + 2:2 * F + 3], None,
                                        ALU.add).then_inc(r_done, 1)
            dve.sem_inc(s_free, 2)
            dve.wait_ge(xnb2_ready, CH)
            for b in range(B):
                dve.wait_ge(o_ready, b + 1)
                nc.vector.scalar_tensor_tensor(out=z1[:, :, b, :], in0=YB[b][:].rearrange("p (c d) -> p c d", c=CH),
                                               scalar=0.3, in1=xnb2[:, :, b, :], op0=ALU.mult, op1=ALU.add).then_inc(z1_ready, 1)
            for b in range(B):
                dve.wait_ge(tz1_ready, b + 1)
                nc.vector.scalar_tensor_tensor(out=z1[:, :, b], in0=tz1[:, :, b], scalar=1.0, in1=z1[:, :, b],
                                               op0=ALU.add, op1=ALU.mult)

            dve.wait_ge(halved, 2)
            dve.sem_inc(odd_copied, 2)

            def unit(u, last=False):
                sums(u, 0)
                if not last:
                    k_copy(u + 1, 0, (0,))
                sums(u, 1)
                probs(u)
                if not last:
                    k_copy(u + 1, 0, (1,))
                    k_copy(u + 1, 1)
                    k_copy(u + 1, 2)
                    k_copy(u + 1, 3)
                    dve.wait_ge(v_out, u * 16 + 16)
                    v_copy(u + 1, 0)
                    v_copy(u + 1, 1)
                for n in range(OB):
                    if n < len(VECTOR_SPREADS):
                        spread_vector(u, VECTOR_SPREADS[n])
                    odd_copy(u, n)
                    if not last and n < 2:
                        v_copy(u + 1, 2 + n)
                output(u, 0)
                if last:
                    output(u, 1)
                    return
                for m in range(MB):
                    if m == 0:
                        wait_spread(dve, u, VECTOR_SPREADS[-1])
                        wait_spread(dve, u, MB - 1)
                    block_scores(u + 1, m)
                    if m == MB // 2 - 1:
                        split_unit(u + 1)
                        centre(u + 1, 0)
                        output(u, 1)
                centre(u + 1, 1)

            with dve.Fori(0, UNITS - 1) as u:
                unit(u)
            unit(UNITS - 1, last=True)


def positions():
    p = np.arange(T, dtype=np.float32)[:, None]
    div = np.exp(np.arange(0, HD1, 2, dtype=np.float32) * np.float32(-(np.log(10000.0) / HD1))).astype(np.float32)
    ang = (p * div).astype(np.float32)
    pe = np.zeros((T, HD1), np.float32)
    pe[:, 0::2] = np.sin(ang)
    pe[:, 1::2] = np.cos(ang)
    both = np.concatenate([pe.T, pe.T], 0).reshape(P, CH, P)
    return np.concatenate([both.repeat(2, 1), both[:, :1]], 1)


def block_masks():
    own = np.zeros((HD1, TB, H1), np.float32)
    own[np.arange(TB), np.arange(TB)] = 1.0
    others = np.zeros_like(own)
    others[:TB] = np.where(own[:TB] == 1.0, 0.0, MASKED)
    return own.reshape(HD1, P), others.reshape(HD1, P)


def kernel(**inputs):
    import concourse.bacc as bacc
    from concourse.bass_utils import run_bass_kernel_spmd

    a = {k: np.asarray(v) for k, v in inputs.items()}

    def rows(*vs):
        return np.broadcast_to(np.concatenate(vs)[None, :], (P, sum(v.size for v in vs)))

    wq = a["L1_attn_w_qkv"].reshape(D, H1, 3, HD1).transpose(0, 2, 1, 3).reshape(D, 3, H1 * HD1)
    bq = a["L1_attn_b_qkv"].reshape(PAIRS, 2, 3, HD1)
    mask_q, mask_k = block_masks()
    experts = np.concatenate([
        a["L1_ffn_W1"],
        a["L1_ffn_W2"].reshape(E, FT, P, D).transpose(0, 2, 1, 3).reshape(E, P, FT * D),
        a["L1_ffn_b1"].reshape(E, FT, P).transpose(0, 2, 1),
        a["L1_ffn_b2"][:, :, None]], axis=2)
    data = {
        "x": a["L0_attn_x"],
        "w_state": a["L0_attn_W_state"].T, "w_gate": a["L0_attn_W_gate"].T,
        "w_in": a["L0_ffn_in_proj_w"].T, "w_op": a["L0_ffn_out_proj_w"].T,
        "w_router": a["L0_ffn_router_w"].T,
        "w1": a["L0_ffn_w1"].transpose(1, 0, 2).reshape(D, E * F),
        "w2": a["L0_ffn_w2"].reshape(E, FT, P, D).transpose(2, 0, 1, 3),
        "cols0": np.stack([a["L0_attn_b_state"], a["L0_ffn_ln1_w"], a["L0_ffn_ln1_b"], a["L0_ffn_ln2_w"],
                           a["L0_ffn_ln2_b"]], 1),
        "rows0": rows(a["L0_ffn_in_proj_b"], a["L0_ffn_out_proj_b"], a["L0_attn_b_gate"]),
        "w_qkv": wq, "bqk": bq[:, :, 0:2].transpose(1, 3, 2, 0).reshape(P, 2, PAIRS),
        "bv_row": rows(bq[:, :, 2].reshape(-1)), "own_token": block_masks()[0][:TB].reshape(TB, P).T,
        "mask_q": mask_q, "mask_k": mask_k,
        "w_out": a["L1_attn_w_out"].reshape(PAIRS, P, D).transpose(1, 0, 2),
        "w_p1": a["L1_ffn_Wp1"], "w_p2": a["L1_ffn_Wp2"], "b_p1": a["L1_ffn_bp1"][:, None],
        "b_p2": a["L1_ffn_bp2"][None, :], "w_o": a["L1_ffn_Wo"],
        "rows1": rows(a["L1_attn_b_out"], a["L1_ffn_bo"]),
        "experts": experts, "pos": positions(),
    }
    nc = bacc.Bacc("TRN2", target_bir_lowering=False, num_devices=1)
    arrays, ins = {}, {}
    for name, v in data.items():
        v = np.ascontiguousarray(v)
        arrays[f"in_{name}"] = v
        ins[name] = nc.dram_tensor(f"in_{name}", v.shape, mybir.dt.from_np(v.dtype), kind="ExternalInput").ap()
    out = nc.dram_tensor("out_x", (UNITS, 2, P, D), F32, kind="ExternalOutput").ap()
    build(nc, ins, out)
    r = run_bass_kernel_spmd(nc, [arrays], core_ids=[0])
    return r.results[0]["out_x"].reshape(CH, B, P, D).transpose(1, 0, 2, 3).reshape(B, T, D)
```
